# Optimizing a Trainium2 kernel written in Bass

```python
import numpy as np
import jax
import jax.numpy as jnp

def _softmax(x, axis=-1):
    return jax.nn.softmax(x, axis=axis)

def _gelu(x):
    return jax.nn.gelu(x, approximate=True)

def _silu(x):
    return jax.nn.silu(x)

def _sigmoid(x):
    return jax.nn.sigmoid(x)

def _layernorm(x, axis=-1, eps=1e-05):
    m = jnp.mean(x, axis=axis, keepdims=True)
    v = jnp.var(x, axis=axis, keepdims=True)
    return (x - m) / jnp.sqrt(v + eps)

def _scatter_add(tgt, idx, src, axis=0):
    return tgt.at[idx].add(src)

def _segment_sum(src, seg, n):
    return jax.ops.segment_sum(src, seg, n)
kernel_name = 'mk_xattn_ffn_d2_seqx_r8_49ddf3'

def setup_inputs(seed: int=0):
    np.random.seed(seed)
    _w = jnp.asarray

    def _rec_inputs():
        import jax
        import jax.numpy as jnp
        _rk = jax.random.key(seed)
        x = 7.22e-05 + 1 * jax.random.normal(jax.random.fold_in(_rk, 1), (4, 256, 256), jnp.float32)
        _lenS = 256 - jax.random.randint(jax.random.fold_in(_rk, 7), (4,), 0, max(1, 256 // 4) + 1, jnp.int32)
        _lenS2 = 1601 - jax.random.randint(jax.random.fold_in(_rk, 8), (4,), 0, max(1, 1601 // 4) + 1, jnp.int32)
        _ctx_2048P = jax.random.normal(jax.random.fold_in(_rk, 11), (4, 16, 256), jnp.float32)
        _ctx_2048c = jax.random.dirichlet(jax.random.fold_in(_rk, 511), 0.3 * jnp.ones((16,), jnp.float32), (4, 1601))
        _ctx_2048t = jnp.einsum('bsk,bkd->bsd', _ctx_2048c, _ctx_2048P)
        _ctx_2048t = _ctx_2048t * jax.lax.rsqrt(jnp.mean(jnp.square(_ctx_2048t)) + 1e-12) * 0.953939
        ctx_2048 = -0.000514642 + 1.00011 * (_ctx_2048t + 0.3 * jax.random.normal(jax.random.fold_in(_rk, 611), (4, 1601, 256), jnp.float32))
        return (x, ctx_2048)
    x, ctx_2048 = _rec_inputs()

    def _L0_xattn_setup():
        import jax, jax.numpy as jnp
        import numpy as np
        HIDDEN = 256
        NUM_HEADS = 16
        NUM_KV_HEADS = 4
        HEAD_DIM = 128
        ROPE_THETA = 10000.0
        EPS = 1e-06

        def rms_norm(x, w, eps=EPS):
            var = jnp.mean(jnp.square(x), axis=-1, keepdims=True)
            return x * jax.lax.rsqrt(var + eps) * w

        def rope_cache(L, head_dim, theta, dtype):
            inv_freq = 1.0 / theta ** (jnp.arange(0, head_dim, 2, dtype=jnp.float32) / head_dim)
            t = jnp.arange(L, dtype=jnp.float32)
            freqs = jnp.outer(t, inv_freq)
            emb = jnp.concatenate([freqs, freqs], -1)
            cos = jnp.cos(emb).astype(dtype)[None, :, None, :]
            sin = jnp.sin(emb).astype(dtype)[None, :, None, :]
            return (cos, sin)

        def rotate_half(x):
            x1, x2 = jnp.split(x, 2, axis=-1)
            return jnp.concatenate([-x2, x1], axis=-1)
        key = jax.random.key(seed)
        ks = jax.random.split(key, 10)
        B, L, T = (2, 256, 64)
        q_out = NUM_HEADS * HEAD_DIM
        kv_out = NUM_KV_HEADS * HEAD_DIM
        s = lambda fan_in: 1.0 / np.sqrt(fan_in)
        return {'x': jax.random.normal(ks[0], (B, L, HIDDEN), jnp.float32), 'h_ctx_kv': jax.random.normal(ks[1], (B, T, HIDDEN), jnp.float32), 'wq': jax.random.normal(ks[2], (HIDDEN, q_out), jnp.float32) * s(HIDDEN), 'wk': jax.random.normal(ks[3], (HIDDEN, kv_out), jnp.float32) * s(HIDDEN), 'wv': jax.random.normal(ks[4], (HIDDEN, kv_out), jnp.float32) * s(HIDDEN), 'wo': jax.random.normal(ks[5], (q_out, HIDDEN), jnp.float32) * s(q_out), 'wk_ctx': jax.random.normal(ks[6], (HIDDEN, kv_out), jnp.float32) * s(HIDDEN), 'wv_ctx': jax.random.normal(ks[7], (HIDDEN, kv_out), jnp.float32) * s(HIDDEN), 'q_norm_w': jnp.ones((HEAD_DIM,), jnp.float32), 'k_norm_w': jnp.ones((HEAD_DIM,), jnp.float32)}
    _L0_xattn_all = _L0_xattn_setup()
    _L0_xattn_in = {k: v for k, v in _L0_xattn_all.items() if k in ('wq', 'wk', 'wv', 'wo', 'wk_ctx', 'wv_ctx', 'q_norm_w', 'k_norm_w')}
    del _L0_xattn_all

    def _L0_ffn_setup():
        import jax, jax.numpy as jnp
        import numpy as np
        EPS = 1e-05

        def fwht(x):
            orig_shape = x.shape
            n = orig_shape[-1]
            x = x.reshape(-1, n)
            h = 1
            while h < n:
                x = x.reshape(-1, n // (2 * h), 2, h)
                a, b = (x[:, :, 0, :], x[:, :, 1, :])
                x = jnp.stack([a + b, a - b], axis=2).reshape(-1, n)
                h *= 2
            return (x * (1.0 / np.sqrt(n))).reshape(orig_shape)

        def act_quant(x):
            scale = 127.0 / jnp.clip(jnp.max(jnp.abs(x), axis=-1, keepdims=True), EPS)
            q = jnp.clip(jnp.round(x * scale), -128.0, 127.0) / scale
            return x + jax.lax.stop_gradient(q - x)

        def weight_quant(w):
            scale = jnp.clip(jnp.mean(jnp.abs(w)), EPS)
            q = jnp.clip(jnp.round(w / scale), -1.0, 1.0) * scale
            return w + jax.lax.stop_gradient(q - w)

        def h_bitlinear(x, w):
            xq = act_quant(fwht(x))
            wq = weight_quant(w)
            return jnp.einsum('bsh,oh->bso', xq, wq)
        key = jax.random.key(seed)
        k1, k2, k3, k4 = jax.random.split(key, 4)
        H, I = (256, 1024)
        B, S = (2, 256)
        hidden_states = jax.random.normal(k1, (B, S, H), dtype=jnp.float32)
        w_gate = jax.random.normal(k2, (I, H), dtype=jnp.float32) * 0.02
        w_up = jax.random.normal(k3, (I, H), dtype=jnp.float32) * 0.02
        w_down = jax.random.normal(k4, (H, I), dtype=jnp.float32) * 0.02
        return {'hidden_states': hidden_states, 'w_gate': w_gate, 'w_up': w_up, 'w_down': w_down}
    _L0_ffn_all = _L0_ffn_setup()
    _L0_ffn_in = {k: v for k, v in _L0_ffn_all.items() if k in ('w_gate', 'w_up', 'w_down')}
    del _L0_ffn_all

    def _L1_xattn_setup():
        import jax, jax.numpy as jnp
        import numpy as np
        EPS = 1e-06
        NUM_HEADS = 16

        def _feature_map(x):
            return jnp.where(x > 0, x + 1.0, jnp.exp(x))
        key = jax.random.key(seed)
        ks = jax.random.split(key, 7)
        B, L, S, D = (4, 512, 512, 256)
        sc = 1.0 / np.sqrt(D)
        return {'query': jax.random.normal(ks[0], (B, L, D), jnp.float32), 'kv': jax.random.normal(ks[1], (B, S, D), jnp.float32), 'Wq': jax.random.normal(ks[2], (D, D), jnp.float32) * sc, 'Wg': jax.random.normal(ks[3], (D, D), jnp.float32) * sc, 'bg': jnp.ones((D,), jnp.float32), 'Wkv': jax.random.normal(ks[4], (2 * D, D), jnp.float32) * sc, 'Wo': jax.random.normal(ks[5], (D, D), jnp.float32) * sc}
    _L1_xattn_all = _L1_xattn_setup()
    _L1_xattn_in = {k: v for k, v in _L1_xattn_all.items() if k in ('Wq', 'Wg', 'bg', 'Wkv', 'Wo')}
    del _L1_xattn_all

    def _L1_ffn_setup():
        import jax, jax.numpy as jnp
        import numpy as np
        NUM_EXPERTS = 8
        TOP_K = 2
        MODEL_DIM = 256
        INTER_DIM = 128
        GATE_SCALE = 1.0
        UP_SCALE = 0.0
        key = jax.random.key(seed)
        k1, k2, k3, k4 = jax.random.split(key, 4)
        hidden_states = jax.random.normal(k1, (2, 256, MODEL_DIM), jnp.float32)
        router_gate = jax.random.normal(k2, (NUM_EXPERTS, MODEL_DIM), jnp.float32) * 0.02
        expert_gate_up = jax.random.normal(k3, (NUM_EXPERTS, MODEL_DIM, 2 * INTER_DIM), jnp.float32) * 0.02
        expert_down = jax.random.normal(k4, (NUM_EXPERTS, INTER_DIM, MODEL_DIM), jnp.float32) * 0.02
        return {'hidden_states': hidden_states, 'router_gate': router_gate, 'expert_gate_up': expert_gate_up, 'expert_down': expert_down}
    _L1_ffn_all = _L1_ffn_setup()
    _L1_ffn_in = {k: v for k, v in _L1_ffn_all.items() if k in ('router_gate', 'expert_gate_up', 'expert_down')}
    del _L1_ffn_all
    return {'x': x, 'ctx_2048': ctx_2048, 'L0_xattn_wq': _L0_xattn_in['wq'], 'L0_xattn_wk': _L0_xattn_in['wk'], 'L0_xattn_wv': _L0_xattn_in['wv'], 'L0_xattn_wo': _L0_xattn_in['wo'], 'L0_xattn_wk_ctx': _L0_xattn_in['wk_ctx'], 'L0_xattn_wv_ctx': _L0_xattn_in['wv_ctx'], 'L0_xattn_q_norm_w': _L0_xattn_in['q_norm_w'], 'L0_xattn_k_norm_w': _L0_xattn_in['k_norm_w'], 'L0_ffn_w_gate': _L0_ffn_in['w_gate'], 'L0_ffn_w_up': _L0_ffn_in['w_up'], 'L0_ffn_w_down': _L0_ffn_in['w_down'], 'L1_xattn_Wq': _L1_xattn_in['Wq'], 'L1_xattn_Wg': _L1_xattn_in['Wg'], 'L1_xattn_bg': _L1_xattn_in['bg'], 'L1_xattn_Wkv': _L1_xattn_in['Wkv'], 'L1_xattn_Wo': _L1_xattn_in['Wo'], 'L1_ffn_router_gate': _L1_ffn_in['router_gate'], 'L1_ffn_expert_gate_up': _L1_ffn_in['expert_gate_up'], 'L1_ffn_expert_down': _L1_ffn_in['expert_down']}

def reference(x, ctx_2048, L0_xattn_wq, L0_xattn_wk, L0_xattn_wv, L0_xattn_wo, L0_xattn_wk_ctx, L0_xattn_wv_ctx, L0_xattn_q_norm_w, L0_xattn_k_norm_w, L0_ffn_w_gate, L0_ffn_w_up, L0_ffn_w_down, L1_xattn_Wq, L1_xattn_Wg, L1_xattn_bg, L1_xattn_Wkv, L1_xattn_Wo, L1_ffn_router_gate, L1_ffn_expert_gate_up, L1_ffn_expert_down):
    import jax
    import jax.numpy as jnp

    def _L0_xattn_ref(x, h_ctx_kv, wq, wk, wv, wo, wk_ctx, wv_ctx, q_norm_w, k_norm_w):
        import jax, jax.numpy as jnp
        import numpy as np
        HIDDEN = 256
        NUM_HEADS = 16
        NUM_KV_HEADS = 4
        HEAD_DIM = 128
        ROPE_THETA = 10000.0
        EPS = 1e-06

        def rms_norm(x, w, eps=EPS):
            var = jnp.mean(jnp.square(x), axis=-1, keepdims=True)
            return x * jax.lax.rsqrt(var + eps) * w

        def rope_cache(L, head_dim, theta, dtype):
            inv_freq = 1.0 / theta ** (jnp.arange(0, head_dim, 2, dtype=jnp.float32) / head_dim)
            t = jnp.arange(L, dtype=jnp.float32)
            freqs = jnp.outer(t, inv_freq)
            emb = jnp.concatenate([freqs, freqs], -1)
            cos = jnp.cos(emb).astype(dtype)[None, :, None, :]
            sin = jnp.sin(emb).astype(dtype)[None, :, None, :]
            return (cos, sin)

        def rotate_half(x):
            x1, x2 = jnp.split(x, 2, axis=-1)
            return jnp.concatenate([-x2, x1], axis=-1)
        B, L, _ = x.shape
        T = h_ctx_kv.shape[1]
        rep = NUM_HEADS // NUM_KV_HEADS
        q = (x @ wq).reshape(B, L, NUM_HEADS, HEAD_DIM)
        k = (x @ wk).reshape(B, L, NUM_KV_HEADS, HEAD_DIM)
        v = (x @ wv).reshape(B, L, NUM_KV_HEADS, HEAD_DIM)
        q = rms_norm(q, q_norm_w)
        k = rms_norm(k, k_norm_w)
        k_ctx = (h_ctx_kv @ wk_ctx).reshape(B, T, NUM_KV_HEADS, HEAD_DIM)
        v_ctx = (h_ctx_kv @ wv_ctx).reshape(B, T, NUM_KV_HEADS, HEAD_DIM)
        k_ctx = rms_norm(k_ctx, k_norm_w)
        cos, sin = rope_cache(L, HEAD_DIM, ROPE_THETA, x.dtype)
        q = q * cos + rotate_half(q) * sin
        k = k * cos + rotate_half(k) * sin
        k_full = jnp.concatenate([k_ctx, k], axis=1)
        v_full = jnp.concatenate([v_ctx, v], axis=1)
        k_full = jnp.repeat(k_full, rep, axis=2)
        v_full = jnpp_repeat = jnp.repeat(v_full, rep, axis=2)
        i = jnp.arange(L)[:, None]
        j = jnp.arange(L)[None, :]
        causal = jnp.where(j > i, -jnp.inf, 0.0).astype(x.dtype)
        mask = jnp.concatenate([jnp.zeros((L, T), x.dtype), causal], axis=1)
        scale = 1.0 / np.sqrt(HEAD_DIM)
        scores = jnp.einsum('blhd,bmhd->bhlm', q, k_full) * scale + mask
        probs = jax.nn.softmax(scores, axis=-1)
        out = jnp.einsum('bhlm,bmhd->blhd', probs, v_full)
        out = out.reshape(B, L, NUM_HEADS * HEAD_DIM)
        return out @ wo

    def _L0_ffn_ref(hidden_states, w_gate, w_up, w_down):
        import jax, jax.numpy as jnp
        import numpy as np
        EPS = 1e-05

        def fwht(x):
            orig_shape = x.shape
            n = orig_shape[-1]
            x = x.reshape(-1, n)
            h = 1
            while h < n:
                x = x.reshape(-1, n // (2 * h), 2, h)
                a, b = (x[:, :, 0, :], x[:, :, 1, :])
                x = jnp.stack([a + b, a - b], axis=2).reshape(-1, n)
                h *= 2
            return (x * (1.0 / np.sqrt(n))).reshape(orig_shape)

        def act_quant(x):
            scale = 127.0 / jnp.clip(jnp.max(jnp.abs(x), axis=-1, keepdims=True), EPS)
            q = jnp.clip(jnp.round(x * scale), -128.0, 127.0) / scale
            return x + jax.lax.stop_gradient(q - x)

        def weight_quant(w):
            scale = jnp.clip(jnp.mean(jnp.abs(w)), EPS)
            q = jnp.clip(jnp.round(w / scale), -1.0, 1.0) * scale
            return w + jax.lax.stop_gradient(q - w)

        def h_bitlinear(x, w):
            xq = act_quant(fwht(x))
            wq = weight_quant(w)
            return jnp.einsum('bsh,oh->bso', xq, wq)
        gate = h_bitlinear(hidden_states, w_gate)
        up = h_bitlinear(hidden_states, w_up)
        return h_bitlinear(jax.nn.silu(gate) * up, w_down)

    def _L1_xattn_ref(query, kv, Wq, Wg, bg, Wkv, Wo):
        import jax, jax.numpy as jnp
        import numpy as np
        EPS = 1e-06
        NUM_HEADS = 16

        def _feature_map(x):
            return jnp.where(x > 0, x + 1.0, jnp.exp(x))
        B, L, D = query.shape
        S = kv.shape[1]
        H = NUM_HEADS
        hd = D // H
        q = query @ Wq.T
        gate = jax.nn.sigmoid(query @ Wg.T + bg)
        kvp = kv @ Wkv.T
        k, v = jnp.split(kvp, 2, axis=-1)
        q = _feature_map(q.reshape(B, L, H, hd).transpose(0, 2, 1, 3))
        k = _feature_map(k.reshape(B, S, H, hd).transpose(0, 2, 1, 3))
        v = v.reshape(B, S, H, hd).transpose(0, 2, 1, 3)
        kv_summary = jnp.einsum('bhsd,bhse->bhde', k, v)
        k_sum = k.sum(axis=-2)
        z = 1.0 / (jnp.einsum('bhld,bhd->bhl', q, k_sum)[..., None] + EPS)
        attn = jnp.einsum('bhld,bhde->bhle', q, kv_summary) * z
        attn = attn.transpose(0, 2, 1, 3).reshape(B, L, D)
        out = attn * gate @ Wo.T
        return out

    def _L1_ffn_ref(hidden_states, router_gate, expert_gate_up, expert_down):
        import jax, jax.numpy as jnp
        import numpy as np
        NUM_EXPERTS = 8
        TOP_K = 2
        MODEL_DIM = 256
        INTER_DIM = 128
        GATE_SCALE = 1.0
        UP_SCALE = 0.0
        orig_shape = hidden_states.shape
        hs = hidden_states.reshape(-1, orig_shape[-1])
        T = hs.shape[0]
        logits = hs @ router_gate.T
        probs = jax.nn.softmax(logits.astype(jnp.float32), axis=-1)
        topk_scores, topk_idx = jax.lax.top_k(probs, TOP_K)
        topk_scores = topk_scores / jnp.sum(topk_scores, axis=-1, keepdims=True)
        scores_f = topk_scores.T.reshape(-1).astype(hs.dtype)
        ids_f = topk_idx.T.reshape(-1)
        order = jnp.argsort(ids_f)
        sorted_ids = ids_f[order]
        scores_sorted = scores_f[order]
        token_slots = order % T
        x = hs[token_slots]
        inter = jnp.zeros((x.shape[0], 2 * INTER_DIM), x.dtype)
        for e in range(NUM_EXPERTS):
            m = (sorted_ids == e)[:, None]
            inter = inter + jnp.where(m, x, 0) @ expert_gate_up[e]
        gate = inter[..., 0::2]
        up = inter[..., 1::2]
        h = (up + UP_SCALE) * jax.nn.silu(gate * GATE_SCALE)
        out_rows = jnp.zeros((x.shape[0], MODEL_DIM), x.dtype)
        for e in range(NUM_EXPERTS):
            m = (sorted_ids == e)[:, None]
            out_rows = out_rows + jnp.where(m, h, 0) @ expert_down[e]
        out = jnp.zeros_like(hs).at[token_slots].add(out_rows * scores_sorted[:, None])
        return out.reshape(orig_shape)
    x = x + _L0_xattn_ref(_layernorm(x, axis=-1), ctx_2048, L0_xattn_wq, L0_xattn_wk, L0_xattn_wv, L0_xattn_wo, L0_xattn_wk_ctx, L0_xattn_wv_ctx, L0_xattn_q_norm_w, L0_xattn_k_norm_w)
    x = x + _L0_ffn_ref(_layernorm(x, axis=-1), L0_ffn_w_gate, L0_ffn_w_up, L0_ffn_w_down)
    x = x + _L1_xattn_ref(_layernorm(x, axis=-1), ctx_2048, L1_xattn_Wq, L1_xattn_Wg, L1_xattn_bg, L1_xattn_Wkv, L1_xattn_Wo)
    x = x + _L1_ffn_ref(_layernorm(x, axis=-1), L1_ffn_router_gate, L1_ffn_expert_gate_up, L1_ffn_expert_down)
    return x

_drawn_inputs = setup_inputs


def setup_inputs(seed=0):
    import zlib

    import numpy as np

    out = dict(_drawn_inputs(seed))
    spreads = {'L0_xattn_q_norm_w': (1.0, 0.2),
     'L0_xattn_k_norm_w': (1.0, 0.2),
     'L1_xattn_bg': (1.0, 0.6)}
    factors = {'L0_xattn_wk': 4.122,
     'L0_xattn_wv': 3.817,
     'L0_ffn_w_gate': 6.924,
     'L0_ffn_w_up': 6.932,
     'L0_ffn_w_down': 6.927,
     'L1_xattn_Wq': 4.729,
     'L1_ffn_router_gate': 8.0,
     'L1_ffn_expert_gate_up': 7.83,
     'L1_ffn_expert_down': 7.815}
    for name, (base, spread) in spreads.items():
        noise = np.random.default_rng([zlib.crc32(name.encode()), seed]).standard_normal(out[name].shape)
        drawn = base * np.exp(spread * noise) if base else spread * noise
        out[name] = jnp.asarray(drawn.astype(out[name].dtype))
    for name, factor in factors.items():
        out[name] = (out[name] * factor).astype(out[name].dtype)
    return out
```

```python
from contextlib import ExitStack

import numpy as np

import concourse.bass as bass
from concourse import mybir

ALU = mybir.AluOpType
ACT = mybir.ActivationFunctionType
F32 = mybir.dt.float32
F16 = mybir.dt.float16
BF16 = mybir.dt.bfloat16
AX_X = mybir.AxisListType.X
ds = bass.ds

P = 128
B, L, D = 4, 256, 256
SC = 1601
HEADS, KVH, DH = 16, 4, 128
REP = HEADS // KVH
NG = B * KVH
DC = D // P
LT = L // P
TILES = B * LT
CT = -(-SC // P)
CREM = SC - (CT - 1) * P
KT_N = CT + LT
KEYS = KT_N * P
BANK = 512
CHUNKS = -(-KEYS // BANK)
LAST = (CHUNKS - 1) * BANK
UNITS = REP * LT
FF = 1024
NE, FI = 8, 128
WS = 64.0
PSCALE_LN = 10 * float(np.log(2.0))
SCALE = 1.0 / float(np.sqrt(DH))
LANES = 16
LANE_N = FF * D // LANES // NG
TAIL_LINKS = 31
MAGIC = 1.5 * 2.0 ** 23
EPS_LN, EPS_RMS, EPS_Q, EPS_Z = 1e-5, 1e-6, 1e-5, 1e-6
PIECES = ["q0", "self", "q1", "rem"] + [("ctx", i) for i in range((CT - 1) // 2)]
NP = len(PIECES)
PIECES_AT = [[0, 1], [2], [3, 4], [5], [6], [7], [8], [9]]
ROPE_AT = {3: ["k"], 4: ["q00"], 5: ["q01"], 6: ["q10"], 7: ["q11"]}
ROPES = ["k", "q00", "q01", "q10", "q11"]
KQ_STEPS = 7


def width(lt):
    return (CT + lt + 1) * P - LAST


def cols(lt, c):
    return BANK if c < CHUNKS - 1 else width(lt)


def build(nc, x, ctxT, wq, wk, wv, wo, wk_ctx, wv_ctx, q_norm, k_norm, w_gateT, w_upT, w_downT,
          WqT, WgT, bg, WkvT, WoT, routerT, w_lanes, e_gate, e_up, e_down,
          c_ident, c_mask, c_cos, c_sin, c_h256, c_h1024, c_blk, c_lower, out):
    main = ExitStack()
    with ExitStack() as ctx:
        def sb(name, shape, dt, at=ctx):
            return at.enter_context(nc.sbuf_tensor(name, shape, dt))

        def sem(name):
            return ctx.enter_context(nc.semaphore(name))

        PS = ctx.enter_context(nc.psum_tensor("PS", [P, 8, BANK], F32))
        SB, TB, OB, XB = 0, 4, 6, 7
        xs = sb("xs", [P, TILES * D], F32)
        R1 = sb("R1", [P, B, DC, 136], F32)
        ident = sb("ident", [P, P], F32)
        ident16 = sb("ident16", [P, P], F16)
        ones = sb("ones", [P, P], F32)
        mhalf = sb("mhalf", [P, TILES], F32)
        eps_ln = sb("eps_ln", [P, TILES], F32)
        eps_rms = sb("eps_rms", [P, TILES], F32)
        per_dh = sb("per_dh", [P, TILES], F32)
        lanes = sb("lanes", [3 * LANES, 1 + LANE_N], F32)
        lsum = sb("lsum", [1, 3 * LANES + 3], F32)
        idle = sb("idle", [P, 2], F32)
        stat = sb("stat", [P, TILES, 6], F32)
        mv = sb("mv", [P, TILES, 2], F32)
        rstd = sb("rstd", [P, TILES], F32)

        def sm(name, shape, dt):
            return sb(name, shape, dt, main)

        identb = sm("identb", [P, P], BF16)
        mask = sm("mask", [P, LT, width(1)], BF16)
        blk = sm("blk", [P, 136], F32)
        wcol = sm("wcol", [P, 1], F32)
        tab = sm("tab", [P, 4, LT, DH], F32)
        ctx_h = sm("ctx_h", [P, B, DC, SC], F16)
        ctx_l = sm("ctx_l", [P, B, DC, SC], F16)
        wc_h = sm("wc_h", [P, DC, KVH, 256], F16)
        wc_l = sm("wc_l", [P, DC, KVH, 256], F16)
        w1_h = sm("w1_h", [P, DC, 512], F16)
        w1_l = sm("w1_l", [P, DC, 512], F16)
        wsf_h = sm("wsf_h", [P, DC, KVH, 768], F16)
        wsf_l = sm("wsf_l", [P, DC, KVH, 768], F16)
        wo_h = sm("wo_h", [P, HEADS, D], F16)
        wo_l = sm("wo_l", [P, HEADS, D], F16)
        xT_h = sm("xT_h", [P, DC, TILES * P], F16)
        xT_l = sm("xT_l", [P, DC, TILES * P], F16)

        setup = ExitStack()
        stage = [sb(f"stage{i}", [P, DC * SC], F32, setup) for i in range(2)]
        xn = sb("xn", [P, TILES * D], F32, setup)
        mask32 = sb("mask32", [P, LT, width(1)], F32, setup)
        nwb = sb("nwb", [P, 2, DH], F32, setup)
        cos = sb("cos", [P, LT, DH], F32, setup)
        sin = sb("sin", [P, LT, DH], F32, setup)
        kv_s = sb("kv_s", [P, 2, 512], F32, setup)
        ex_s = sb("ex_s", [P, 2, 256], F32, setup)
        kf_s = sb("kf_s", [P, 2, 256], F32, setup)
        vf_s = sb("vf_s", [P, 2, DC, 129], F32, setup)
        setup.close()

        kvr = sm("kvr", [P, KT_N, 256], F32)
        qr = sm("qr", [P, UNITS, DH], F32)
        sq = sm("sq", [P, REP, DH], F32)
        ss = sm("ss", [P, REP], F32)
        rs = sm("rs", [P, REP], F32)
        rot = sm("rot", [P, 2, 2, DH], F32)
        kT_h = sm("kT_h", [P, KEYS], F16)
        kT_l = sm("kT_l", [P, KEYS], F16)
        qT_h = sm("qT_h", [P, UNITS, P], F16)
        qT_l = sm("qT_l", [P, UNITS, P], F16)
        v_h = sm("v_h", [P, KT_N, DH + 1], F16)
        v_l = sm("v_l", [P, KT_N, DH], F16)
        pr = sm("pr", [P, KEYS], F32)
        pT_h = sm("pT_h", [P, CHUNKS, BANK], F16)
        pT_l = sm("pT_l", [P, CHUNKS, BANK], F16)
        mx = sm("mx", [P, CHUNKS], F32)
        mr = sm("mr", [P, 1], F32)
        nb = sm("nb", [P, 2], F32)
        rden = sm("rden", [P, 1], F32)
        o_s = sm("o_s", [P, LT, REP, DH], F32)
        oT_h = sm("oT_h", [P, LT, BANK], F16)
        oT_l = sm("oT_l", [P, LT, BANK], F16)
        main.close()

        H1 = sb("H1", [P, FF // P, FF], F16)
        H0 = sb("H0", [P, DC, D], F16)
        lower = sb("lower", [P, 4 * NE, NE], F32)
        wraw = sb("wraw", [P, 4096], F32)
        wraw2 = sb("wraw2", [P, 4096], F32)
        tern = sb("tern", [P, 2048], F32)
        wg3 = sb("wg3", [P, DC, FF], F16)
        wu3 = sb("wu3", [P, DC, FF], F16)
        wd3 = sb("wd3", [P, FF // P, D], F16)
        wqg_h = sb("wqg_h", [P, 2, DC, D], F16)
        wqg_l = sb("wqg_l", [P, 2, DC, D], F16)
        wo1_h = sb("wo1_h", [P, DC, D], F16)
        wo1_l = sb("wo1_l", [P, DC, D], F16)
        rt_h = sb("rt_h", [P, DC, NE], F16)
        rt_l = sb("rt_l", [P, DC, NE], F16)
        eg_h = sb("eg_h", [P, 2, DC, NE * FI], F16)
        eg_l = sb("eg_l", [P, 2, DC, NE * FI], F16)
        ed_h = sb("ed_h", [P, NE, D], F16)
        ed_l = sb("ed_l", [P, NE, D], F16)
        bgs = sb("bgs", [1, D], F32)
        wmean = sb("wmean", [P, 4], F32)
        thr = sb("thr", [P, 8], F32)
        xn4 = sb("xn4", [P, 4, D], F32)
        xnT_h = sb("xnT_h", [P, DC, BANK], F16)
        xnT_l = sb("xnT_l", [P, DC, BANK], F16)
        am = sb("am", [P, 4, 4], F32)
        dq = sb("dq", [P, 4, 4], F32)
        qf = sb("qf", [P, 2, FF], F32)
        qi = sb("qi", [P, 4, FF], F16)
        qiT = sb("qiT", [P, 4, FF], F16)
        sil = sb("sil", [P, 2, FF], F32)
        hh = sb("hh", [P, 4, FF], F32)
        hT_h = sb("hT_h", [P, 4, FF], F16)
        hT_l = sb("hT_l", [P, 4, FF], F16)
        sg = sb("sg", [P, 4, D], F32)
        z = sb("z", [P, 4, 16], F32)
        lg = sb("lg", [P, 4, NE], F32)
        pb = sb("pb", [P, 4, NE], F32)
        gt = sb("gt", [P, 4, NE * NE], F32)
        eq = sb("eq", [P, 4, NE * NE], F32)
        rk = sb("rk", [P, 4, NE], F32)
        r4 = sb("r4", [P, 4, 4], F32)

        in_const, in_x, in_out = sem("in_const"), sem("in_x"), sem("out_stored")
        in_w = [sem(f"in_w{i}") for i in range(2)]
        set_hi, set_lo = sem("set_hi"), sem("set_lo")
        made_const = sem("made_const")
        ln_stat, ln_agg, ln_var, ln_rstd, ln_out, ln_tr, ln_hi, ln_lo = (
            sem(f"ln0_{n}") for n in ("stat", "agg", "var", "rstd", "out", "tr", "hi", "lo"))
        tab_made = sem("tab_made")
        l1_mm, l1_copy, l1_min, l1_exp, l1_k, l1_sum, l1_R = (
            sem(f"l1_{n}") for n in ("mm", "copy", "min", "exp", "k", "sum", "R"))
        pc_mm, pc_copy, pc_sq, pc_ss, pc_norm = (
            sem(f"pc_{n}") for n in ("mm", "copy", "sq", "ss", "norm"))
        pool_step, rope_done = sem("pool_step"), sem("rope_done")
        kq_tr, kq_hi, kq_lo, vs_hi, vs_lo = (sem(n) for n in ("kq_tr", "kq_hi", "kq_lo", "vs_hi", "vs_lo"))
        qk_done, mx_part, mx_all, nb_done, exp_done = (
            sem(n) for n in ("qk_done", "mx_part", "mx_all", "nb_done", "exp_done"))
        pt_tr, pt_hi, pt_lo, pv_done, rd_done, o_done = (
            sem(n) for n in ("pt_tr", "pt_hi", "pt_lo", "pv_done", "rd_done", "o_done"))
        ot_tr, ot_hi, ot_lo, oj_mm, x1_done = (sem(n) for n in ("ot_tr", "ot_hi", "ot_lo", "oj_mm", "x1_done"))
        dve_step, act_step = sem("dve_step"), sem("act_step")
        lane_in, lane_sum, lane_tr, lane_tot, lane_b = (
            sem(n) for n in ("lane_in", "lane_sum", "lane_tr", "lane_tot", "lane_b"))
        tw_in = [sem(f"tw_in{i}") for i in range(2)]
        tw_const, tw_hi, tw_lo, tw_made = (sem(f"tw_{n}") for n in ("const", "hi", "lo", "made"))
        tl = {n: [sem(f"t{n}{i}") for i in range(4)]
              for n in ("agg", "rstd", "norm", "tr", "hi", "lo")}
        fw_mm, fw_q, qt_tr, qt_ev = ([sem(f"{n}{i}") for i in range(2)]
                                     for n in ("fw_mm", "fw_q", "qt_tr", "qt_ev"))
        gu_mm, gu_silu, gu_h, ht_tr, ht_hi, ht_lo, dn_mm, dn_x = (
            [sem(f"{n}{i}") for i in range(2)]
            for n in ("gu_mm", "gu_silu", "gu_h", "ht_tr", "ht_hi", "ht_lo", "dn_mm", "dn_x"))
        lq_mm, lg_mm, lq_copy, lq_min, lq_exp, lq_f, lg_sig, la_mm, la_out, lo_mm, lo_x = (
            sem(n) for n in ("lq_mm", "lg_mm", "lq_copy", "lq_min", "lq_exp", "lq_f", "lg_sig",
                             "la_mm", "la_out", "lo_mm", "lo_x"))
        rt_mm, rt_sub, rt_exp, rt_w = (sem(n) for n in ("rt_mm", "rt_sub", "rt_exp", "rt_w"))

        rows = lambda t: t.rearrange("(c p) n -> p c n", p=P)
        loads = []

        def st(i, n, off=0):
            return stage[i % 2][:, off:off + n]

        i = 0
        loads.append(([(st(i, 1024).rearrange("p (c n) -> p c n", c=DC), rows(WkvT))], 1024, WS,
                      w1_h[:, :, :].rearrange("p c n -> p (c n)"), w1_l[:, :, :].rearrange("p c n -> p (c n)")))
        for b in range(B):
            i += 1
            loads.append(([(st(i, DC * SC).rearrange("p (c n) -> p c n", c=DC), rows(ctxT[b, :, :]))], DC * SC, 1.0,
                          ctx_h[:, b, :, :].rearrange("p c n -> p (c n)"),
                          ctx_l[:, b, :, :].rearrange("p c n -> p (c n)")))
        i += 1
        cv = st(i, 2048).rearrange("p (c h n) -> p c h n", c=DC, h=KVH)
        loads.append(([(cv[:, c, :, o:o + DH], w[c * P:(c + 1) * P, :].rearrange("p (h n) -> p h n", h=KVH))
                       for c in range(DC) for o, w in ((0, wk_ctx), (DH, wv_ctx))], 2048, WS,
                      wc_h[:, :, :, :].rearrange("p c h n -> p (c h n)"),
                      wc_l[:, :, :, :].rearrange("p c h n -> p (c h n)")))
        for c in range(DC):
            i += 1
            sv = st(i, 3072).rearrange("p (h n) -> p h n", h=KVH)
            loads.append(([(sv[:, :, o:o + n], w[c * P:(c + 1) * P, :].rearrange("p (h n) -> p h n", h=KVH))
                           for o, n, w in ((0, 512, wq), (512, DH, wk), (640, DH, wv))], 3072, WS,
                          wsf_h[:, c, :, :].rearrange("p h n -> p (h n)"),
                          wsf_l[:, c, :, :].rearrange("p h n -> p (h n)")))
        for g in range(2):
            i += 1
            loads.append(([(st(i, 2048).rearrange("p (h n) -> p h n", h=8),
                            wo[g * 1024:(g + 1) * 1024, :].rearrange("(h p) n -> p h n", p=P))], 2048, WS,
                          wo_h[:, g * 8:(g + 1) * 8, :].rearrange("p h n -> p (h n)"),
                          wo_l[:, g * 8:(g + 1) * 8, :].rearrange("p h n -> p (h n)")))
        NL = len(loads)
        load_count = [16 * sum(len(loads[j][0]) for j in range(i % 2, i + 1, 2)) for i in range(NL)]

        def tst(i, n):
            return (wraw, wraw2)[i % 2][:, 0:n]

        kc = lambda t, p="p c n -> p (c n)": t[:, :, :].rearrange(p)
        tloads = [
            ([(tst(0, 2048).rearrange("p (c n) -> p c n", c=DC), rows(w_gateT))], 2048, None, kc(wg3), None),
            ([(tst(1, 2048).rearrange("p (c n) -> p c n", c=DC), rows(w_upT))], 2048, None, kc(wu3), None),
            ([(tst(2, 2048).rearrange("p (c n) -> p c n", c=FF // P), rows(w_downT))], 2048, None, kc(wd3), None),
            ([(tst(3, 1024)[:, 512 * k:512 * k + 512].rearrange("p (c n) -> p c n", c=DC), rows(w))
              for k, w in enumerate((WqT, WgT))], 1024, WS,
             wqg_h[:, :, :, :].rearrange("p k c n -> p (k c n)"), wqg_l[:, :, :, :].rearrange("p k c n -> p (k c n)")),
            ([(tst(4, 512).rearrange("p (c n) -> p c n", c=DC), rows(WoT))], 512, WS, kc(wo1_h), kc(wo1_l)),
            ([(tst(5, 16).rearrange("p (c n) -> p c n", c=DC), rows(routerT))], 16, WS, kc(rt_h), kc(rt_l)),
            ([(tst(6, 4096)[:, 2048 * k:2048 * k + 2048].rearrange("p (c n) -> p c n", c=DC), rows(w))
              for k, w in enumerate((e_gate, e_up))], 4096, WS,
             eg_h[:, :, :, :].rearrange("p k c n -> p (k c n)"), eg_l[:, :, :, :].rearrange("p k c n -> p (k c n)")),
            ([(tst(7, 2048).rearrange("p (e n) -> p e n", e=NE), e_down.rearrange("e p n -> p e n"))], 2048, WS,
             kc(ed_h), kc(ed_l)),
        ]
        NTL = len(tloads)
        tload_count = [16 * sum(len(tloads[j][0]) for j in range(i % 2, i + 1, 2)) for i in range(NTL)]
        NTERN = 3

        def flat(t):
            return t[:, :, :].rearrange("p a b -> p (a b)")

        def wait(eng, semaphore, value):
            if not isinstance(value, int) or value > 0:
                eng.wait_ge(semaphore, value)

        def l1_walk(eng, step, end=None):
            def batch(b):
                n = b * CT
                step(n, 0, CREM)
                step(n + 1, 1, P)
                with eng.Fori(0, (CT - 3) // 2) as i:
                    step(n + i * 2 + 2, 0, P)
                    step(n + i * 2 + 3, 1, P)
                step(n + CT - 1, 0, P)
                if end:
                    end(b)
            batch(0)
            with eng.Fori(1, B) as b:
                batch(b)

        def piece_slots(p):
            return {"q0": REP, "q1": REP, "self": LT, "rem": 1}.get(PIECES[p], 2)

        def piece_rows(p):
            kind = PIECES[p]
            if kind in ("q0", "q1"):
                lt = int(kind[1])
                return qr[:, lt * REP:(lt + 1) * REP, :]
            t = {"self": CT, "rem": CT - 1}[kind] if isinstance(kind, str) else 2 * kind[1]
            return kvr[:, t:t + piece_slots(p), 0:DH]

        def kq_view(s, kT, qT):
            bank = TB + s % 2
            if s in (0, 6):
                lt = s // 6
                return qT[:, lt * REP:(lt + 1) * REP, :].rearrange("p h n -> p (h n)"), PS[:, bank, :], False
            if s == 4:
                return kT[:, (CT - 1) * P:SC], PS[:, bank, 0:CREM], True
            if s == 5:
                return kT[:, CT * P:KEYS], PS[:, bank, 0:LT * P], False
            return kT[:, (s - 1) * BANK:s * BANK], PS[:, bank, :], True

        GB = [4, 6, 0, 2]
        both = lambda j: j // 2 * 2 + 2
        ps16 = lambda bank: PS[:, bank, :].bitcast(F16)

        def tail_pe(pe, three):
            mm = pe.matmul
            pe.wait_ge(lane_sum, NG)
            pe.wait_ge(x1_done, NG)
            pe.transpose(PS[0:1, 0, 0:3 * LANES], lanes[:, 0:1], ident[0:3 * LANES, 0:3 * LANES]).then_inc(lane_tr, 1)
            pe.wait_ge(lane_tot, 1)
            mm(PS[:, 1, 0:NTERN], ones[0:1, :], lsum[:, 3 * LANES:], start=True, stop=True).then_inc(lane_b, 1)
            pe.wait_ge(tw_const, 64)
            pe.wait_ge(tw_lo, NTL)
            pe.wait_ge(tw_made, 1)
            with pe.Fori(0, 2) as hf:
                def normed(n, count):
                    pe.wait_ge(tl["norm"][n], count)
                    for c in range(DC):
                        for j in range(4):
                            last = pe.transpose(PS[:, c, j * P:(j + 1) * P], xn4[:, j, c * P:(c + 1) * P], ident[:, :])
                        last.then_inc(tl["tr"][n], 1)
                    pe.wait_ge(tl["lo"][n], hf * 2 + 2)

                def tok(j):
                    return [(xnT_h[:, c, j * P:(j + 1) * P], xnT_l[:, c, j * P:(j + 1) * P]) for c in range(DC)]

                def gate_up(n):
                    for j in range(4):
                        if j >= 2:
                            pe.wait_ge(gu_h[n], hf * 4 + j - 1)
                        elif j == 0 and n == 0:
                            pe.wait_ge(qt_ev[0], hf * 2 + 2)
                        g0 = 4 - 4 * (j % 2)
                        for k in range(4):
                            o, w0 = PS[:, g0 + k, :], (k % 2) * BANK
                            for c in range(DC):
                                if n == 0:
                                    w = (wg3, wu3)[k // 2]
                                    last = mm(o, qiT[:, 0, c * BANK + j * P:c * BANK + (j + 1) * P],
                                              w[:, c, w0:w0 + BANK], start=c == 0, stop=c == DC - 1)
                                else:
                                    last = three(o, tok(j)[c], (eg_h[:, k // 2, c, w0:w0 + BANK],
                                                                eg_l[:, k // 2, c, w0:w0 + BANK]), c == 0, c == DC - 1)
                        last.then_inc(gu_mm[n], 1)
                    for j in range(4):
                        pe.wait_ge(gu_h[n], hf * 4 + max(j + 1, 3 if j < 2 else 4))
                        for f in range(8):
                            last = pe.transpose(PS[:, GB[j] + f // 4, (f % 4) * P:(f % 4 + 1) * P],
                                                hh[:, j, f * P:(f + 1) * P], ident[:, :])
                        last.then_inc(ht_tr[n], 1)

                normed(0, hf * 4 + 4)
                for j in range(4):
                    for c in range(DC):
                        for w in range(2):
                            last = mm(PS[:, 2 + j // 2, (j % 2) * D:(j % 2 + 1) * D], tok(j)[c][w], H0[:, c, :],
                                      start=c + w == 0, stop=c + w == DC)
                    last.then_inc(fw_mm[0], 1)
                pe.wait_ge(fw_q[0], hf + 1)
                for c in range(DC):
                    for j in range(4):
                        last = pe.transpose(ps16(c)[:, j * P:(j + 1) * P], qi[:, j, c * P:(c + 1) * P], ident16[:, :])
                    last.then_inc(qt_tr[0], 1)
                gate_up(0)
                for j in range(4):
                    pe.wait_ge(ht_lo[0], hf * 4 + j + 1)
                    for k in range(2):
                        for f in range(8):
                            for w, t in enumerate((hT_h, hT_l)):
                                last = mm(PS[:, GB[j] + k, :], t[:, j, f * P:(f + 1) * P],
                                          H1[:, f, k * BANK:(k + 1) * BANK], start=f + w == 0, stop=f + w == 8)
                    last.then_inc(fw_mm[1], 1)
                for j in range(4):
                    pe.wait_ge(fw_q[1], hf * 4 + j + 1)
                    for f in range(8):
                        last = pe.transpose(ps16(GB[j])[:, f * P:(f + 1) * P], qi[:, j, f * P:(f + 1) * P], ident16[:, :])
                    last.then_inc(qt_tr[1], 1)
                for j in range(4):
                    pe.wait_ge(qt_ev[1], hf * 4 + j + 1)
                    for f in range(8):
                        last = mm(PS[:, GB[j] + 1, 0:D], qiT[:, j, f * P:(f + 1) * P], wd3[:, f, :],
                                  start=f == 0, stop=f == 7)
                    last.then_inc(dn_mm[0], 1)

                normed(1, hf * 4 + 4)
                for k in range(DC):
                    for c in range(DC):
                        last = three(PS[:, 4 + k, :],
                                     (wqg_h[:, 0, c, k * P:(k + 1) * P], wqg_l[:, 0, c, k * P:(k + 1) * P]),
                                     (xnT_h[:, c, :], xnT_l[:, c, :]), c == 0, c == DC - 1)
                    last.then_inc(lq_mm, 1)
                for j in range(4):
                    o = PS[:, 2 + j // 2, (j % 2) * D:(j % 2 + 1) * D]
                    mm(o, ones[0:1, :], bgs[:, :], start=True, stop=False)
                    for c in range(DC):
                        last = three(o, tok(j)[c], (wqg_h[:, 1, c, :], wqg_l[:, 1, c, :]), False, c == DC - 1)
                    last.then_inc(lg_mm, 1)
                pe.wait_ge(lq_f, hf * 2 + 2)
                for j in range(4):
                    for k in range(DC):
                        last = mm(PS[:, (6, 7, 4, 5)[j], k * 136:(k + 1) * 136],
                                  hh[:, 0, k * BANK + j * P:k * BANK + (j + 1) * P],
                                  R1[:, ds(hf * 2 + j // 2, 1), k, :].rearrange("p a n -> p (a n)"),
                                  start=True, stop=True)
                    last.then_inc(la_mm, 1)
                normed(3, hf + 1)
                for j in range(4):
                    for c in range(DC):
                        last = three(PS[:, 2 + j // 2, (j % 2) * D:(j % 2 + 1) * D], tok(j)[c],
                                     (wo1_h[:, c, :], wo1_l[:, c, :]), c == 0, c == DC - 1)
                    last.then_inc(lo_mm, 1)

                normed(2, hf * 4 + 4)
                for j in range(4):
                    for c in range(DC):
                        last = three(PS[:, 4, j * NE:(j + 1) * NE], tok(j)[c], (rt_h[:, c, :], rt_l[:, c, :]),
                                     c == 0, c == DC - 1)
                last.then_inc(rt_mm, 1)
                pe.wait_ge(rt_sub, hf + 1)
                gate_up(1)
                for j in range(4):
                    pe.wait_ge(ht_lo[1], hf * 4 + j + 1)
                    for f in range(NE):
                        last = three(PS[:, GB[j], 0:D], (hT_h[:, j, f * P:(f + 1) * P], hT_l[:, j, f * P:(f + 1) * P]),
                                     (ed_h[:, f, :], ed_l[:, f, :]), f == 0, f == NE - 1)
                    last.then_inc(dn_mm[1], 1)

        def tail_act(act, copy):
            act.wait_ge(x1_done, NG)
            for i in range(NTERN, NTL):
                parts, n, scale, hi, lo = tloads[i]
                act.wait_ge(tw_in[i % 2], tload_count[i])
                copy(hi, tst(i, n), scale).then_inc(tw_hi, 1)
            act.wait_ge(tw_lo, NTERN)
            with act.Fori(0, 2) as hf:
                def hi_part(n):
                    for c in range(DC):
                        act.wait_ge(tl["tr"][n], hf * 2 + c + 1)
                        copy(xnT_h[:, c, :], PS[:, c, :]).then_inc(tl["hi"][n], 1)

                def gate_up(n):
                    for j in range(4):
                        act.wait_ge(gu_mm[n], hf * 4 + j + 1)
                        if j >= 2:
                            act.wait_ge(gu_h[n], hf * 4 + j - 1)
                        g0 = 4 - 4 * (j % 2)
                        act.activation(sil[:, j % 2, :], PS[:, g0:g0 + 2, :].rearrange("p b n -> p (b n)"), ACT.Silu,
                                       scale=dq[:, 0, j:j + 1] if n == 0 else 1 / WS).then_inc(gu_silu[n], 1)
                    for j in range(4):
                        act.wait_ge(ht_tr[n], hf * 4 + j + 1)
                        copy(hT_h[:, j, :], PS[:, GB[j]:GB[j] + 2, :].rearrange("p b n -> p (b n)"))\
                            .then_inc(ht_hi[n], 1)

                hi_part(0)
                for c in range(DC):
                    act.wait_ge(qt_tr[0], hf * 2 + c + 1)
                    copy(qiT[:, 0, c * BANK:(c + 1) * BANK], ps16(c)[:, 0:BANK]).then_inc(qt_ev[0], 1)
                gate_up(0)
                for j in range(4):
                    act.wait_ge(qt_tr[1], hf * 4 + j + 1)
                    copy(qiT[:, j, :], ps16(GB[j])).then_inc(qt_ev[1], 1)
                hi_part(1)
                for k in range(DC):
                    act.wait_ge(lq_mm, hf * 2 + k + 1)
                    copy(sil[:, 0, k * BANK:(k + 1) * BANK], PS[:, 4 + k, :], 1 / WS).then_inc(lq_copy, 1)
                for k in range(DC):
                    act.wait_ge(lq_min, hf * 2 + k + 1)
                    e = sil[:, 1, k * BANK:(k + 1) * BANK]
                    act.activation(e, e, ACT.Exp).then_inc(lq_exp, 1)
                for j in range(4):
                    act.wait_ge(lg_mm, hf * 4 + both(j))
                    act.activation(sg[:, j, :], PS[:, 2 + j // 2, (j % 2) * D:(j % 2 + 1) * D], ACT.Sigmoid,
                                   scale=1 / WS).then_inc(lg_sig, 1)
                hi_part(3)
                hi_part(2)
                act.wait_ge(rt_sub, hf + 1)
                act.activation(pb[:, :, :], lg[:, :, :], ACT.Exp).then_inc(rt_exp, 1)
                gate_up(1)

        def tail_pool(pool):
            with pool.Fori(0, 2) as hf:
                for n in range(3):
                    pool.wait_ge(tl["agg"][n], hf + 1)
                    pool.tensor_tensor(rstd[:, 0:4], mv[:, 0:4, 1], eps_ln[:, 0:4], ALU.add).then_inc(ln_var, 1)
                    pool.wait_ge(ln_var, hf * 3 + n + 2)
                    pool.tensor_tensor(rstd[:, 0:4], rstd[:, 0:4], mhalf[:, 0:4], ALU.pow).then_inc(tl["rstd"][n], 1)

        def tail_dve(dve, steps):
            done, count = [steps], [0]

            def link(ins):
                done[0] = done[0] + 1
                count[0] += 1
                ins.then_inc(dve_step, 1)
                dve.wait_ge(dve_step, done[0])

            dve.wait_ge(lane_tr, 1)
            dve.reduce_sum(lsum[:, 3 * LANES:], PS[0:1, 0, 0:3 * LANES].rearrange("p (i j) -> p i j", j=LANES), AX_X)\
               .then_inc(lane_tot, 1)
            dve.wait_ge(lane_b, 1)
            link(dve.tensor_scalar(wmean[:, 0:NTERN], PS[:, 1, 0:NTERN], 1.0 / (FF * D), EPS_Q, ALU.mult, ALU.max))
            for i, (parts, n, scale, hi, lo) in enumerate(tloads):
                w = tst(i, n)
                if i < NTERN:
                    dve.wait_ge(tw_in[i % 2], tload_count[i])
                    dve.tensor_scalar(thr[:, 2 * i:2 * i + 1], wmean[:, i:i + 1], 0.5, None, ALU.mult)
                    link(dve.tensor_scalar(thr[:, 2 * i + 1:2 * i + 2], wmean[:, i:i + 1], -0.5, None, ALU.mult))
                    link(dve.tensor_scalar(tern[:, :], w, thr[:, 2 * i + 1:2 * i + 2], None, ALU.is_lt))
                    dve.scalar_tensor_tensor(hi, w, thr[:, 2 * i:2 * i + 1], tern[:, :], ALU.is_gt, ALU.subtract)\
                       .then_inc(tw_lo, 1)
                    dve.wait_ge(tw_lo, i + 1)
                else:
                    dve.wait_ge(tw_hi, i - NTERN + 1)
                    dve.scalar_tensor_tensor(lo, w, scale, hi, ALU.mult, ALU.subtract).then_inc(tw_lo, 1)
            dve.wait_ge(tw_const, 64)
            dve.tensor_copy(ident16[:, :], ident[:, :])
            dve.tensor_scalar(bgs[:, :], bgs[:, :], WS, None, ALU.mult).then_inc(tw_made, 1)

            base = done[0]
            with dve.Fori(0, 2) as hf:
                done[0] = hf * TAIL_LINKS + base
                count[0] = 0

                def norm(n):
                    dve.memset(idle[:, 0:1], 0.0)
                    for j in range(4):
                        ins = dve.bn_stats(stat[:, j, :], xs[:, ds(hf * 1024 + j * D, D)])
                    link(ins)
                    dve.memset(idle[:, 1:2], 0.0)
                    for j in range(4):
                        ins = dve.bn_aggr(mv[:, j, :], stat[:, j, :])
                    ins.then_inc(tl["agg"][n], 1)
                    dve.wait_ge(tl["rstd"][n], hf + 1)
                    for j in range(4):
                        dve.tensor_scalar(xn4[:, j, :], xs[:, ds(hf * 1024 + j * D, D)], mv[:, j, 0:1],
                                          rstd[:, j:j + 1], ALU.subtract, ALU.mult).then_inc(tl["norm"][n], 1)

                def lo_part(n):
                    for c in range(DC):
                        dve.wait_ge(tl["hi"][n], hf * 2 + c + 1)
                        dve.tensor_tensor(xnT_l[:, c, :], PS[:, c, :], xnT_h[:, c, :], ALU.subtract)\
                           .then_inc(tl["lo"][n], 1)

                def h_lo(n):
                    for j in range(4):
                        dve.wait_ge(ht_hi[n], hf * 4 + j + 1)
                        dve.tensor_tensor(hT_l[:, j, :], PS[:, GB[j]:GB[j] + 2, :].rearrange("p b n -> p (b n)"),
                                          hT_h[:, j, :], ALU.subtract).then_inc(ht_lo[n], 1)

                def quant_scales(weights):
                    link(dve.tensor_scalar(am[:, 0, :], am[:, 0, :], EPS_Q, None, ALU.max))
                    link(dve.reciprocal(am[:, 1, :], am[:, 0, :]))
                    for k, w in enumerate(weights):
                        dve.tensor_scalar(dq[:, k, :], am[:, 0, :], wmean[:, w:w + 1], 1.0 / 127.0, ALU.mult, ALU.mult)
                    link(dve.tensor_scalar(am[:, 2, :], am[:, 1, :], 127.0, None, ALU.mult))

                def add_to_x(o, j, scale, done_sem):
                    at = xs[:, ds(hf * 1024 + j * D, D)]
                    dve.scalar_tensor_tensor(at, o, scale, at, ALU.mult, ALU.add).then_inc(done_sem, 1)

                norm(0)
                lo_part(0)
                for j in range(4):
                    dve.wait_ge(fw_mm[0], hf * 4 + both(j))
                    ins = dve.tensor_reduce(am[:, 0, j:j + 1], PS[:, 2 + j // 2, (j % 2) * D:(j % 2 + 1) * D], AX_X,
                                            ALU.max, apply_absolute_value=True)
                link(ins)
                quant_scales((0, 1))
                for j in range(4):
                    ins = dve.tensor_scalar(qf[:, 0, j * D:(j + 1) * D], PS[:, 2 + j // 2, (j % 2) * D:(j % 2 + 1) * D],
                                            am[:, 2, j:j + 1], MAGIC, ALU.mult, ALU.add)
                link(ins)
                dve.tensor_scalar(qi[:, :, 0:D], qf[:, 0, :].rearrange("p (j n) -> p j n", j=4), MAGIC, 127.0,
                                  ALU.subtract, ALU.min).then_inc(fw_q[0], 1)
                for j in range(4):
                    dve.wait_ge(gu_silu[0], hf * 4 + j + 1)
                    g0 = 4 - 4 * (j % 2)
                    dve.scalar_tensor_tensor(hh[:, j, :], PS[:, g0 + 2:g0 + 4, :].rearrange("p b n -> p (b n)"),
                                             dq[:, 1, j:j + 1], sil[:, j % 2, :], ALU.mult, ALU.mult)\
                       .then_inc(gu_h[0], 1)
                h_lo(0)
                for j in range(4):
                    dve.wait_ge(fw_mm[1], hf * 4 + j + 1)
                    y = PS[:, GB[j]:GB[j] + 2, :].rearrange("p b n -> p (b n)")
                    ins = dve.tensor_reduce(am[:, 0, j:j + 1], y, AX_X, ALU.max, apply_absolute_value=True)
                link(ins)
                quant_scales((2,))
                for j in range(4):
                    y = PS[:, GB[j]:GB[j] + 2, :].rearrange("p b n -> p (b n)")
                    link(dve.tensor_scalar(qf[:, j % 2, :], y, am[:, 2, j:j + 1], MAGIC, ALU.mult, ALU.add))
                    dve.tensor_scalar(qi[:, j, :], qf[:, j % 2, :], MAGIC, 127.0, ALU.subtract, ALU.min)\
                       .then_inc(fw_q[1], 1)
                for j in range(4):
                    dve.wait_ge(dn_mm[0], hf * 4 + j + 1)
                    add_to_x(PS[:, GB[j] + 1, 0:D], j, dq[:, 0, j:j + 1], dn_x[0])
                dve.wait_ge(dn_x[0], hf * 4 + 4)

                norm(1)
                lo_part(1)
                for k in range(DC):
                    dve.wait_ge(lq_copy, hf * 2 + k + 1)
                    dve.tensor_scalar_min(sil[:, 1, k * BANK:(k + 1) * BANK], sil[:, 0, k * BANK:(k + 1) * BANK], 0.0)\
                       .then_inc(lq_min, 1)
                for k in range(DC):
                    dve.wait_ge(lq_exp, hf * 2 + k + 1)
                    dve.scalar_tensor_tensor(hh[:, 0, k * BANK:(k + 1) * BANK], sil[:, 0, k * BANK:(k + 1) * BANK], 0.0,
                                             sil[:, 1, k * BANK:(k + 1) * BANK], ALU.max, ALU.add).then_inc(lq_f, 1)
                heads = lambda j: PS[:, (6, 7, 4, 5)[j], 0:2 * 136].rearrange("p (k n) -> p k n", k=DC)
                for j in range(4):
                    dve.wait_ge(la_mm, hf * 4 + j + 1)
                    ins = dve.tensor_scalar(z[:, j, :].rearrange("p (k h) -> p k h", k=DC), heads(j)[:, :, P:136],
                                            EPS_Z, None, ALU.add)
                link(ins)
                link(dve.reciprocal(z[:, :, :], z[:, :, :]))
                for j in range(4):
                    for k in range(DC):
                        ins = dve.tensor_tensor(
                            xn4[:, j, k * P:(k + 1) * P].rearrange("p (h e) -> p h e", h=8),
                            heads(j)[:, k, 0:P].rearrange("p (h e) -> p h e", h=8),
                            z[:, j, k * 8:(k + 1) * 8].unsqueeze(2).broadcast_to([P, 8, 16]), ALU.mult)
                link(ins)
                dve.wait_ge(lg_sig, hf * 4 + 4)
                dve.tensor_tensor(flat(xn4), flat(xn4), flat(sg), ALU.mult).then_inc(tl["norm"][3], 1)
                lo_part(3)
                for j in range(4):
                    dve.wait_ge(lo_mm, hf * 4 + both(j))
                    add_to_x(PS[:, 2 + j // 2, (j % 2) * D:(j % 2 + 1) * D], j, 1 / WS, lo_x)
                dve.wait_ge(lo_x, hf * 4 + 4)

                norm(2)
                lo_part(2)
                dve.wait_ge(rt_mm, hf + 1)
                link(dve.tensor_scalar(flat(lg), PS[:, 4, 0:4 * NE], 1 / WS, None, ALU.mult))
                link(dve.reduce_max(r4[:, 0, :], lg[:, :, :], AX_X))
                over = lambda r: r.unsqueeze(2).broadcast_to([P, 4, NE])
                dve.tensor_tensor(lg[:, :, :], lg[:, :, :], over(r4[:, 0, :]), ALU.subtract).then_inc(rt_sub, 1)
                dve.wait_ge(rt_exp, hf + 1)
                link(dve.reduce_sum(r4[:, 1, :], pb[:, :, :], AX_X))
                link(dve.reciprocal(r4[:, 2, :], r4[:, 1, :]))
                link(dve.tensor_tensor(pb[:, :, :], pb[:, :, :], over(r4[:, 2, :]), ALU.mult))
                pe_ = flat(pb).unsqueeze(2).broadcast_to([P, 4 * NE, NE])
                pj_ = pb[:, :, :].unsqueeze(2).broadcast_to([P, 4, NE, NE])
                g4 = lambda t: t[:, :, :].rearrange("p t (e j) -> p t e j", e=NE)
                pe4 = pb[:, :, :].unsqueeze(3).broadcast_to([P, 4, NE, NE])
                dve.tensor_tensor(g4(gt), pj_, pe4, ALU.is_gt)
                link(dve.tensor_tensor(g4(eq), pj_, pe4, ALU.is_equal))
                link(dve.tensor_tensor(flat(eq), flat(eq), flat(lower), ALU.mult))
                link(dve.tensor_tensor(flat(gt), flat(gt), flat(eq), ALU.add))
                link(dve.reduce_sum(flat(rk), flat(gt).rearrange("p (a j) -> p a j", j=NE), AX_X))
                link(dve.scalar_tensor_tensor(flat(rk), flat(rk), 1.5, flat(pb), ALU.is_lt, ALU.mult))
                link(dve.reduce_sum(r4[:, 1, :], rk[:, :, :], AX_X))
                link(dve.reciprocal(r4[:, 2, :], r4[:, 1, :]))
                dve.scalar_tensor_tensor(pb[:, :, :], rk[:, :, :], 1 / WS, over(r4[:, 2, :]), ALU.mult, ALU.mult)\
                   .then_inc(rt_w, 1)
                dve.wait_ge(rt_w, hf + 1)
                for j in range(4):
                    dve.wait_ge(gu_silu[1], hf * 4 + j + 1)
                    g0 = 4 - 4 * (j % 2)
                    up = PS[:, g0 + 2:g0 + 4, :].rearrange("p b n -> p (b n)")
                    for e in range(NE):
                        ins = dve.scalar_tensor_tensor(hh[:, j, e * P:(e + 1) * P], up[:, e * P:(e + 1) * P],
                                                       pb[:, j, e:e + 1], sil[:, j % 2, e * P:(e + 1) * P],
                                                       ALU.mult, ALU.mult)
                    ins.then_inc(gu_h[1], 1)
                h_lo(1)
                for j in range(4):
                    dve.wait_ge(dn_mm[1], hf * 4 + j + 1)
                    add_to_x(PS[:, GB[j], 0:D], j, 1 / WS, dn_x[1])
                assert count[0] == TAIL_LINKS, count[0]

        block = ctx.enter_context(nc.Block())

        @block.sync
        def _(sp):
            sp.dma_start(ident[:, :], c_ident).then_inc(in_const, 16)
            sp.dma_start(xs[:, :].rearrange("p (t d) -> p t d", t=TILES),
                         x.rearrange("(t p) d -> p t d", p=P)).then_inc(in_x, 16)
            for i, (parts, n, scale, hi, lo) in enumerate(loads):
                if i >= 2:
                    sp.wait_ge(set_lo, i - 1)
                for dst, src in parts:
                    sp.dma_start(dst, src).then_inc(in_w[i % 2], 16)
                if i == 1:
                    for dst, src in ((mask32[:, :, :], c_mask), (cos[:, :, :], c_cos),
                                     (sin[:, :, :], c_sin), (blk[:, :], c_blk),
                                     (nwb[:, 0, :], q_norm.partition_broadcast(P)),
                                     (nwb[:, 1, :], k_norm.partition_broadcast(P)),
                                     (wcol[:, :], k_norm.rearrange("(p a) -> p a", a=1))):
                        sp.dma_start(dst, src).then_inc(in_const, 16)
            sp.dma_start(lanes[:, 1:], w_lanes[:, 0:LANE_N]).then_inc(lane_in, 16)
            with sp.Fori(1, NG) as g:
                sp.wait_ge(lane_sum, g)
                sp.dma_start(lanes[:, 1:], w_lanes[:, ds(g * LANE_N, LANE_N)]).then_inc(lane_in, 16)
            sp.wait_ge(x1_done, NG)
            for i, (parts, n, scale, hi, lo) in enumerate(tloads):
                if i >= 2:
                    sp.wait_ge(tw_lo, i - 1)
                for dst, src in parts:
                    sp.dma_start(dst, src).then_inc(tw_in[i % 2], 16)
                if i == 1:
                    for dst, src in ((H0[:, :, :], c_h256), (H1[:, :, :], c_h1024), (lower[:, :, :], c_lower),
                                     (bgs[:, :], bg.rearrange("(a n) -> a n", a=1))):
                        sp.dma_start(dst, src).then_inc(tw_const, 16)
            outv = out.rearrange("(t p) d -> p t d", p=P)
            for hf in range(2):
                sp.wait_ge(dn_x[1], 4 * hf + 4)
                sp.dma_start(outv[:, 4 * hf:4 * hf + 4, :],
                             xs[:, hf * 1024:hf * 1024 + 1024].rearrange("p (t d) -> p t d", t=4)).then_inc(in_out, 16)
            sp.wait_ge(in_out, 32)

        @block.tensor
        def _(pe):
            mm = pe.matmul

            def three(o, lhs, rhs, start, stop):
                (ah, al), (bh, bl) = lhs, rhs
                mm(o, ah, bh, start=start, stop=False)
                mm(o, ah, bl, start=False, stop=False)
                return mm(o, al, bh, start=False, stop=stop)

            pe.wait_ge(in_const, 16)
            for k in range(4):
                c, half = k // 2, k % 2
                pe.wait_ge(ln_out, 4 * half + 4)
                for j in range(4):
                    t = 4 * half + j
                    last = pe.transpose(PS[:, TB + k % 2 if k < 2 else OB + k % 2, j * P:(j + 1) * P],
                                        xn[:, t * D + c * P:t * D + (c + 1) * P], ident[:, :])
                last.then_inc(ln_tr, 1)

            def l1_proj(b, n, par, nrows, col):
                wait(pe, l1_copy, n if nrows == CREM else n - 1)
                for c in range(DC):
                    last = three(PS[0:nrows, SB + par, :],
                                 (ctx_h[:, b, c, ds(col, nrows)], ctx_l[:, b, c, ds(col, nrows)]),
                                 (w1_h[:, c, :], w1_l[:, c, :]), c == 0, c == DC - 1)
                last.then_inc(l1_mm, 1)

            def l1_summary(n, par, nrows, first, final):
                pe.wait_ge(l1_k, n + 1)
                for c in range(DC):
                    last = mm(PS[:, TB + c, 0:129], kf_s[0:nrows, par, c * P:(c + 1) * P],
                              vf_s[0:nrows, par, c, :], start=first, stop=final)
                last.then_inc(l1_sum, 1)

            pe.wait_ge(set_lo, 1 + B)
            pe.wait_ge(ln_lo, 4)
            def l1_batch(b):
                n = b * CT
                wait(pe, l1_R, b)
                l1_proj(b, n, 0, CREM, (CT - 1) * P)
                l1_proj(b, n + 1, 1, P, 0)
                l1_summary(n, 0, CREM, True, False)
                with pe.Fori(0, (CT - 3) // 2) as i:
                    l1_proj(b, n + i * 2 + 2, 0, P, i * (2 * P) + P)
                    l1_summary(n + i * 2 + 1, 1, P, False, False)
                    l1_proj(b, n + i * 2 + 3, 1, P, i * (2 * P) + 2 * P)
                    l1_summary(n + i * 2 + 2, 0, P, False, False)
                l1_proj(b, n + CT - 1, 0, P, (CT - 2) * P)
                l1_summary(n + CT - 2, 1, P, False, False)
                l1_summary(n + CT - 1, 0, P, False, True)

            l1_batch(0)
            with pe.Fori(1, B) as b:
                l1_batch(b)

            def piece(p, g):
                b, kv = g // KVH, g % KVH
                kind = PIECES[p]
                wait(pe, pc_copy, g * NP + p)
                if kind in ("q0", "q1"):
                    lt = int(kind[1])
                    jobs = [(PS[:, XB, :], xT_h, xT_l, (b * L + lt * P), P, wsf_h, wsf_l, 0, 512)]
                elif kind == "self":
                    jobs = [(PS[:, XB, lt * 256:lt * 256 + 256], xT_h, xT_l, (b * L + lt * P), P, wsf_h, wsf_l, 512, 256)
                            for lt in range(LT)]
                elif kind == "rem":
                    jobs = [(PS[0:CREM, XB, 0:256], None, None, (CT - 1) * P, CREM, wc_h, wc_l, 0, 256)]
                else:
                    jobs = [(PS[:, XB, j * 256:j * 256 + 256], None, None, (2 * kind[1] + j) * P, P, wc_h, wc_l, 0, 256)
                            for j in range(2)]
                for o, ah, al, col, n, bh, bl, w0, wn in jobs:
                    for c in range(DC):
                        if ah is None:
                            lhs = (ctx_h[:, b, c, col:col + n], ctx_l[:, b, c, col:col + n])
                        else:
                            lhs = (ah[:, c, ds(col, n)], al[:, c, ds(col, n)])
                        last = three(o, lhs, (bh[:, c, kv, w0:w0 + wn], bl[:, c, kv, w0:w0 + wn]),
                                     c == 0, c == DC - 1)
                last.then_inc(pc_mm, 1)

            def transpose_kq(g):
                for s in range(KQ_STEPS):
                    if s < 2:
                        wait(pe, ot_lo, g * 2)
                    else:
                        pe.wait_ge(kq_lo, g * KQ_STEPS + s - 1)
                    bank = TB + s % 2
                    if s in (0, 6):
                        lt = s // 6
                        pe.wait_ge(rope_done, g * 5 + (3 if lt == 0 else 5))
                        for j in range(REP):
                            last = pe.transpose(PS[:, bank, j * P:(j + 1) * P], qr[:, lt * REP + j, :], ident[:, :])
                    elif s == 4:
                        pe.wait_ge(pc_norm, g * NP + 4)
                        last = pe.transpose(PS[:, bank, 0:CREM], kvr[0:CREM, CT - 1, 0:DH], ident[0:CREM, 0:CREM])
                    elif s == 5:
                        for j in range(LT):
                            last = pe.transpose(PS[:, bank, j * P:(j + 1) * P], kvr[:, CT + j, 0:DH], ident[:, :])
                    else:
                        t0 = 4 * (s - 1)
                        pe.wait_ge(pc_norm, g * NP + 4 + 2 * s)
                        for j in range(4):
                            last = pe.transpose(PS[:, bank, j * P:(j + 1) * P], kvr[:, t0 + j, 0:DH], ident[:, :])
                    last.then_inc(kq_tr, 1)

            def qk(u, c, g):
                h, lt = u // LT, u % LT
                if u > 0:
                    pe.wait_ge(exp_done, g * (UNITS * CHUNKS) + (u - 1) * CHUNKS + c + 1)
                elif c == 0:
                    pe.wait_ge(kq_lo, g * KQ_STEPS + 5)
                elif c == CHUNKS - 1:
                    pe.wait_ge(kq_lo, g * KQ_STEPS + 6)
                if u == 1 and c == 0:
                    pe.wait_ge(kq_lo, g * KQ_STEPS + 7)
                n = cols(lt, c)
                o = PS[:, SB + c, 0:n]
                qs = lt * REP + h
                if c == CHUNKS - 1:
                    mm(o, identb[:, :], mask[:, lt, 0:n], start=True, stop=False)
                three(o, (qT_h[:, qs, :], qT_l[:, qs, :]),
                      (kT_h[:, c * BANK:c * BANK + n], kT_l[:, c * BANK:c * BANK + n]),
                      c < CHUNKS - 1, True).then_inc(qk_done, 1)

            def transpose_p(u, c, g):
                n = g * (UNITS * CHUNKS) + u * CHUNKS + c
                pe.wait_ge(exp_done, n + 1)
                if u * CHUNKS + c >= 2:
                    pe.wait_ge(pt_lo, n - 1)
                for j in range(cols(u % LT, c) // P):
                    last = pe.transpose(PS[:, TB + c % 2, j * P:(j + 1) * P],
                                        pr[:, c * BANK + j * P:c * BANK + (j + 1) * P], ident[:, :])
                last.then_inc(pt_tr, 1)

            def pv(u, c, g):
                n = g * (UNITS * CHUNKS) + u * CHUNKS + c
                pe.wait_ge(pt_lo, n + 1)
                if u == 0:
                    pe.wait_ge(vs_lo, g * CHUNKS + c + 1)
                if c == 0 and u > 0:
                    pe.wait_ge(o_done, g * UNITS + u)
                tiles = cols(u % LT, c) // P
                for j in range(tiles):
                    t = c * 4 + j
                    first, final = c == 0 and j == 0, c == CHUNKS - 1 and j == tiles - 1
                    ph, pl = pT_h[:, c, j * P:(j + 1) * P], pT_l[:, c, j * P:(j + 1) * P]
                    mm(PS[:, OB, 0:DH + 1], ph, v_h[:, t, :], start=first, stop=False)
                    mm(PS[:, OB, 0:DH], ph, v_l[:, t, :], start=False, stop=False)
                    last = mm(PS[:, OB, 0:DH + 1], pl, v_h[:, t, :], start=False, stop=final)
                if c == CHUNKS - 1:
                    last.then_inc(pv_done, 1)

            def attention(g, prepare):
                for c in range(CHUNKS):
                    qk(0, c, g)
                for u in range(UNITS):
                    todo = list(PIECES_AT[u]) if prepare else []
                    for c in range(CHUNKS):
                        transpose_p(u, c, g)
                        if u + 1 < UNITS:
                            qk(u + 1, c, g)
                        if c >= 1:
                            pv(u, c - 1, g)
                        if c % 2 and todo:
                            piece(todo.pop(0), g + 1)
                    pv(u, CHUNKS - 1, g)

            def out_proj(g):
                kv = g % KVH
                for lt in range(LT):
                    pe.wait_ge(o_done, (g + 1) * UNITS)
                    for h in range(REP):
                        last = pe.transpose(PS[:, TB + lt, h * P:(h + 1) * P], o_s[:, lt, h, :], ident[:, :])
                    last.then_inc(ot_tr, 1)
                for lt in range(LT):
                    pe.wait_ge(ot_lo, g * 2 + lt + 1)
                    for h in range(REP):
                        last = three(PS[:, OB, lt * D:(lt + 1) * D],
                                     (oT_h[:, lt, h * P:(h + 1) * P], oT_l[:, lt, h * P:(h + 1) * P]),
                                     (wo_h[:, ds(kv * REP + h, 1), :].rearrange("p a n -> p (a n)"),
                                      wo_l[:, ds(kv * REP + h, 1), :].rearrange("p a n -> p (a n)")),
                                     h == 0, h == REP - 1)
                last.then_inc(oj_mm, 1)

            pe.wait_ge(set_lo, NL)
            pe.wait_ge(made_const, 2)
            for p in range(NP):
                piece(p, 0)
            transpose_kq(0)
            with pe.Fori(0, NG - 1) as g:
                attention(g, True)
                out_proj(g)
                transpose_kq(g + 1)
                pe.wait_ge(x1_done, g + 1)
            attention(NG - 1, False)
            out_proj(NG - 1)
            tail_pe(pe, three)

        @block.scalar
        def _(act):
            copy = lambda o, i, scale=1.0: act.activation(o, i, ACT.Copy, scale=scale)

            def set_hi_part(i):
                parts, n, scale, hi, lo = loads[i]
                act.wait_ge(in_w[i % 2], load_count[i])
                copy(hi, stage[i % 2][:, 0:n], scale).then_inc(set_hi, 1)

            for k in range(4):
                c, half = k // 2, k % 2
                if k == 0:
                    set_hi_part(0)
                act.wait_ge(ln_tr, k + 1)
                copy(xT_h[:, c, half * BANK:(half + 1) * BANK],
                     PS[:, TB + k % 2 if k < 2 else OB + k % 2, :]).then_inc(ln_hi, 1)
            for i in range(1, NL):
                set_hi_part(i)

            def l1_step(n, par, nrows):
                act.wait_ge(l1_mm, n + 1)
                if par == 0 and nrows == CREM:
                    wait(act, l1_k, n)
                    wait(act, l1_sum, n)
                else:
                    wait(act, l1_k, n - 1)
                    wait(act, l1_sum, n - 1)
                copy(kv_s[0:nrows, par, 0:256], PS[0:nrows, SB + par, 0:256], 1 / WS)
                copy(vf_s[0:nrows, par, :, 0:P],
                     PS[0:nrows, SB + par, 256:512].rearrange("p (c n) -> p c n", c=DC), 1 / WS).then_inc(l1_copy, 1)
                act.wait_ge(l1_min, n + 1)
                act.activation(ex_s[0:nrows, par, :], ex_s[0:nrows, par, :], ACT.Exp).then_inc(l1_exp, 1)

            act.wait_ge(made_const, 1)
            l1_walk(act, l1_step)

            def piece_copy(p, g):
                kind = PIECES[p]
                act.wait_ge(pc_mm, g * NP + p + 1)
                if p == 0:
                    wait(act, vs_lo, g * CHUNKS)
                if kind in ("q0", "q1"):
                    lt = int(kind[1])
                    o, i = qr[:, lt * REP:(lt + 1) * REP, :], PS[:, XB, :].rearrange("p (h d) -> p h d", h=REP)
                elif kind == "self":
                    o, i = kvr[:, CT:CT + LT, :], PS[:, XB, :].rearrange("p (t d) -> p t d", t=LT)
                elif kind == "rem":
                    o, i = kvr[0:CREM, CT - 1, :], PS[0:CREM, XB, 0:256]
                else:
                    t = 2 * kind[1]
                    o, i = kvr[:, t:t + 2, :], PS[:, XB, :].rearrange("p (t d) -> p t d", t=2)
                copy(o, i, 1 / WS).then_inc(pc_copy, 1)

            def split_kq(g):
                for s in range(KQ_STEPS):
                    act.wait_ge(kq_tr, g * KQ_STEPS + s + 1)
                    o, i, w = kq_view(s, kT_h, qT_h)
                    if w:
                        act.activation(o, i, ACT.Copy, scale=wcol[:, 0:1]).then_inc(kq_hi, 1)
                    else:
                        copy(o, i).then_inc(kq_hi, 1)

            def split_v(g):
                for c in range(CHUNKS):
                    t0, t1 = 4 * c, min(4 * c + 4, KT_N)
                    if c == 0:
                        act.wait_ge(pc_copy, (g + 1) * NP)
                    copy(v_h[:, t0:t1, 0:DH], kvr[:, t0:t1, DH:2 * DH]).then_inc(vs_hi, 1)

            def exp(u, c, g):
                n = g * (UNITS * CHUNKS) + u * CHUNKS + c
                if c == 0:
                    act.wait_ge(nb_done, g * UNITS + u + 1)
                w = cols(u % LT, c)
                act.activation(pr[:, c * BANK:c * BANK + w], PS[:, SB + c, 0:w], ACT.Exp,
                               bias=nb[:, u % 2:u % 2 + 1], scale=SCALE).then_inc(exp_done, 1)

            def p_hi(u, c, g):
                act.wait_ge(pt_tr, g * (UNITS * CHUNKS) + u * CHUNKS + c + 1)
                w = cols(u % LT, c)
                copy(pT_h[:, c, 0:w], PS[:, TB + c % 2, 0:w]).then_inc(pt_hi, 1)

            def attention(g, prepare):
                for u in range(UNITS):
                    todo = list(PIECES_AT[u]) if prepare else []
                    exp(u, 0, g)
                    exp(u, 1, g)
                    for c in range(CHUNKS):
                        p_hi(u, c, g)
                        if c + 2 < CHUNKS:
                            exp(u, c + 2, g)
                        if c >= 2 and todo:
                            piece_copy(todo.pop(0), g + 1)

            def split_out(g):
                for lt in range(LT):
                    act.wait_ge(ot_tr, g * 2 + lt + 1)
                    copy(oT_h[:, lt, :], PS[:, TB + lt, :]).then_inc(ot_hi, 1)

            act.wait_ge(made_const, 2)
            for p in range(NP):
                piece_copy(p, 0)
            split_kq(0)
            split_v(0)
            with act.Fori(0, NG - 1) as g:
                attention(g, True)
                split_out(g)
                split_kq(g + 1)
                split_v(g + 1)
            attention(NG - 1, False)
            split_out(NG - 1)
            tail_act(act, copy)

        @block.vector
        def _(dve):
            steps = [0]

            def link(ins):
                steps[0] += 1
                ins.then_inc(dve_step, 1)
                dve.wait_ge(dve_step, steps[0])

            dve.memset(ones[:, :], 1.0)
            dve.memset(lanes[:, 0:1], 0.0)
            for t, value in ((mhalf, -0.5), (eps_ln, EPS_LN), (eps_rms, EPS_RMS), (per_dh, 1.0 / DH)):
                dve.memset(t[:, :], value)
            dve.memset(vf_s[:, :, :, :], 1.0).then_inc(made_const, 1)

            dve.wait_ge(in_x, 16)
            for t in range(TILES):
                dve.bn_stats(stat[:, t, :], xs[:, t * D:(t + 1) * D]).then_inc(ln_stat, 1)
            for t in range(TILES):
                dve.wait_ge(ln_stat, t + 1)
                dve.bn_aggr(mv[:, t, :], stat[:, t, :]).then_inc(ln_agg, 1)

            def set_lo_part(i):
                parts, n, scale, hi, lo = loads[i]
                dve.wait_ge(set_hi, i + 1)
                dve.scalar_tensor_tensor(lo, stage[i % 2][:, 0:n], scale, hi, ALU.mult, ALU.subtract)\
                   .then_inc(set_lo, 1)

            dve.wait_ge(ln_rstd, 1)
            for t in range(TILES):
                dve.tensor_scalar(xn[:, t * D:(t + 1) * D], xs[:, t * D:(t + 1) * D], mv[:, t, 0:1],
                                  rstd[:, t:t + 1], ALU.subtract, ALU.mult).then_inc(ln_out, 1)
            for k in range(4):
                c, half = k // 2, k % 2
                if k == 0:
                    set_lo_part(0)
                dve.wait_ge(ln_hi, k + 1)
                dve.tensor_tensor(xT_l[:, c, half * BANK:(half + 1) * BANK],
                                  PS[:, TB + k % 2 if k < 2 else OB + k % 2, :],
                                  xT_h[:, c, half * BANK:(half + 1) * BANK], ALU.subtract).then_inc(ln_lo, 1)
            for i in range(1, NL):
                set_lo_part(i)

            dve.wait_ge(in_const, 16 * 8)
            dve.tensor_copy(identb[:, :], ident[:, :])
            dve.tensor_copy(mask[:, :, :], mask32[:, :, :])
            for k in range(2):
                for lt in range(LT):
                    dve.tensor_tensor(tab[:, 2 * k, lt, :], cos[:, lt, :], nwb[:, k, :], ALU.mult)
                    for a, o in ((0, 64), (64, 0)):
                        dve.tensor_tensor(tab[:, 2 * k + 1, lt, a:a + 64], sin[:, lt, a:a + 64],
                                          nwb[:, k, o:o + 64], ALU.mult).then_inc(tab_made, 1)

            def l1_step(n, par, nrows):
                dve.wait_ge(l1_copy, n + 1)
                dve.tensor_scalar_min(ex_s[0:nrows, par, :], kv_s[0:nrows, par, 0:256], 0.0).then_inc(l1_min, 1)
                dve.wait_ge(l1_exp, n + 1)
                dve.scalar_tensor_tensor(kf_s[0:nrows, par, :], kv_s[0:nrows, par, 0:256], 0.0,
                                         ex_s[0:nrows, par, :], ALU.max, ALU.add).then_inc(l1_k, 1)

            def l1_end(b):
                dve.wait_ge(l1_sum, b * CT + CT)
                for c in range(DC):
                    last = dve.tensor_tensor(R1[:, ds(b, 1), c, 0:P].rearrange("p a n -> p (a n)"),
                                             PS[:, TB + c, 0:P], blk[:, 0:P], ALU.mult)
                    last = dve.tensor_scalar(R1[:, ds(b, 1), c, P:136].rearrange("p a n -> p (a n)"),
                                             blk[:, P:136], PS[:, TB + c, P:P + 1], None, ALU.mult)
                last.then_inc(l1_R, 1)

            l1_walk(dve, l1_step, l1_end)

            dve.wait_ge(set_lo, NL)
            dve.wait_ge(l1_sum, B * CT)
            dve.wait_ge(tab_made, 8)
            dve.memset(kvr[:, CT - 1, :], 0.0)
            dve.memset(v_h[:, :, :], 1.0)
            dve.memset(kT_h[:, SC:CT * P], 0.0)
            dve.memset(kT_l[:, SC:CT * P], 0.0).then_inc(made_const, 1)

            def piece_sum(p, g):
                n = piece_slots(p)
                dve.wait_ge(pc_sq, g * NP + p + 1)
                dve.reduce_sum(ss[:, 0:n], sq[:, 0:n, :], AX_X).then_inc(pc_ss, 1)

            def split_kq(g):
                for s in range(KQ_STEPS):
                    dve.wait_ge(kq_hi, g * KQ_STEPS + s + 1)
                    hi, i, w = kq_view(s, kT_h, qT_h)
                    lo, _, _ = kq_view(s, kT_l, qT_l)
                    if w:
                        dve.scalar_tensor_tensor(lo, i, wcol[:, 0:1], hi, ALU.mult, ALU.subtract).then_inc(kq_lo, 1)
                    else:
                        dve.tensor_tensor(lo, i, hi, ALU.subtract).then_inc(kq_lo, 1)

            def split_v(c, g):
                t0, t1 = 4 * c, min(4 * c + 4, KT_N)
                dve.wait_ge(vs_hi, g * CHUNKS + c + 1)
                dve.tensor_tensor(v_l[:, t0:t1, :], kvr[:, t0:t1, DH:2 * DH], v_h[:, t0:t1, 0:DH], ALU.subtract)\
                   .then_inc(vs_lo, 1)

            def chunk_max(u, c, g):
                dve.wait_ge(qk_done, g * (UNITS * CHUNKS) + u * CHUNKS + c + 1)
                dve.reduce_max(mx[:, c:c + 1], PS[:, SB + c, 0:cols(u % LT, c)], AX_X).then_inc(mx_part, 1)

            def row_max(u, g):
                dve.wait_ge(mx_part, g * (UNITS * CHUNKS) + u * CHUNKS + CHUNKS)
                dve.reduce_max(mr[:, :], mx[:, :], AX_X).then_inc(mx_all, 1)
                dve.wait_ge(mx_all, g * UNITS + u + 1)
                dve.tensor_scalar(nb[:, u % 2:u % 2 + 1], mr[:, :], -SCALE, PSCALE_LN, ALU.mult, ALU.add)\
                   .then_inc(nb_done, 1)

            def p_lo(u, c, g):
                dve.wait_ge(pt_hi, g * (UNITS * CHUNKS) + u * CHUNKS + c + 1)
                w = cols(u % LT, c)
                dve.tensor_tensor(pT_l[:, c, 0:w], PS[:, TB + c % 2, 0:w], pT_h[:, c, 0:w], ALU.subtract)\
                   .then_inc(pt_lo, 1)

            def lane_step(g):
                dve.wait_ge(lane_in, g * 16 + 16)
                dve.tensor_reduce(lanes[:, 0:1], lanes[:, :], AX_X, ALU.add, apply_absolute_value=True)\
                   .then_inc(lane_sum, 1)

            def out_norm(u, g):
                h, lt = u // LT, u % LT
                dve.wait_ge(pv_done, g * UNITS + u + 1)
                dve.reciprocal(rden[:, :], PS[:, OB, DH:DH + 1]).then_inc(rd_done, 1)
                dve.wait_ge(rd_done, g * UNITS + u + 1)
                dve.tensor_scalar(o_s[:, lt, h, :], PS[:, OB, 0:DH], rden[:, 0:1], None, ALU.mult)\
                   .then_inc(o_done, 1)

            def attention(g, prepare):
                for c in range(CHUNKS):
                    chunk_max(0, c, g)
                row_max(0, g)
                for c in range(CHUNKS):
                    split_v(c, g)
                for u in range(UNITS):
                    for c in range(CHUNKS):
                        p_lo(u, c, g)
                        if u + 1 < UNITS:
                            chunk_max(u + 1, c, g)
                    if u + 1 < UNITS:
                        row_max(u + 1, g)
                    if u == 1:
                        lane_step(g)
                    if prepare:
                        for p in PIECES_AT[u][:-1]:
                            piece_sum(p, g + 1)
                    out_norm(u, g)
                    if prepare:
                        piece_sum(PIECES_AT[u][-1], g + 1)

            def out_proj(g):
                for lt in range(LT):
                    dve.wait_ge(ot_hi, g * 2 + lt + 1)
                    dve.tensor_tensor(oT_l[:, lt, :], PS[:, TB + lt, :], oT_h[:, lt, :], ALU.subtract)\
                       .then_inc(ot_lo, 1)

            def residual(g):
                dve.wait_ge(oj_mm, g + 1)
                at = xs[:, ds(g // KVH * BANK, BANK)]
                dve.scalar_tensor_tensor(at, PS[:, OB, :], 1 / WS, at, ALU.mult, ALU.add).then_inc(x1_done, 1)

            for p in range(NP):
                piece_sum(p, 0)
            split_kq(0)
            with dve.Fori(0, NG - 1) as g:
                attention(g, True)
                out_proj(g)
                residual(g)
                split_kq(g + 1)
            attention(NG - 1, False)
            out_proj(NG - 1)
            residual(NG - 1)
            tail_dve(dve, steps[0])

        @block.gpsimd
        def _(pool):
            pool.wait_ge(ln_agg, TILES)
            pool.wait_ge(made_const, 1)
            pool.tensor_tensor(rstd[:, :], mv[:, :, 1], eps_ln[:, :], ALU.add).then_inc(ln_var, 1)
            pool.wait_ge(ln_var, 1)
            pool.tensor_tensor(rstd[:, :], rstd[:, :], mhalf[:, 0:TILES], ALU.pow).then_inc(ln_rstd, 1)

            PER_PIECE, PER_ROPE = 3, 3
            PER_G = NP * PER_PIECE + 5 * PER_ROPE

            def prepare(g, events):
                done = [g * PER_G]

                def step(ins):
                    done[0] = done[0] + 1
                    ins.then_inc(pool_step, 1)
                    pool.wait_ge(pool_step, done[0])

                for kind, p in events:
                    if kind == "piece":
                        n = piece_slots(p)
                        v = piece_rows(p)
                        pool.wait_ge(pc_copy, g * NP + p + 1)
                        wait(pool, pc_ss, g * NP + p)
                        pool.tensor_tensor(sq[:, 0:n, :], v, v, ALU.mult).then_inc(pc_sq, 1)
                        pool.wait_ge(pc_ss, g * NP + p + 1)
                        wait(pool, pc_norm, g * NP + p)
                        step(pool.tensor_tensor(rs[:, 0:n], ss[:, 0:n], per_dh[:, 0:n], ALU.mult))
                        step(pool.tensor_tensor(rs[:, 0:n], rs[:, 0:n], eps_rms[:, 0:n], ALU.add))
                        step(pool.tensor_tensor(rs[:, 0:n], rs[:, 0:n], mhalf[:, 0:n], ALU.pow))
                        pool.tensor_tensor(v, v, rs[:, 0:n].unsqueeze(2).broadcast_to([P, n, DH]), ALU.mult)\
                            .then_inc(pc_norm, 1)
                    else:
                        r = ROPES.index(p)
                        pool.wait_ge(pc_norm, g * NP + {"k": 2, "q0": 1, "q1": 3}[p[:2]])
                        wait(pool, rope_done, g * len(ROPES) + r)
                        if p == "k":
                            v = kvr[:, CT:CT + LT, 0:DH]
                            cs, sn = tab[:, 2, :, :], tab[:, 3, :, :]
                        else:
                            lt, j = int(p[1]), int(p[2])
                            v = qr[:, lt * REP + 2 * j:lt * REP + 2 * j + 2, :]
                            cs, sn = (tab[:, k, lt:lt + 1, :].broadcast_to([P, 2, DH]) for k in (0, 1))
                        step(pool.tensor_tensor(rot[:, 0, :, :], v, cs, ALU.mult))
                        pool.tensor_tensor(rot[:, 1, :, 0:64], v[:, :, 64:DH], sn[:, :, 0:64], ALU.mult)\
                            .then_inc(pool_step, 1)
                        done[0] = done[0] + 1
                        step(pool.tensor_tensor(rot[:, 1, :, 64:DH], v[:, :, 0:64], sn[:, :, 64:DH], ALU.mult))
                        pool.tensor_tensor(v, rot[:, 0, :, :], rot[:, 1, :, :], ALU.add).then_inc(rope_done, 1)

            events = []
            for u in range(UNITS):
                events += [("piece", p) for p in PIECES_AT[u]] + [("rope", r) for r in ROPE_AT.get(u, [])]
            pool.wait_ge(made_const, 2)
            prepare(0, events)
            with pool.Fori(1, NG) as g:
                prepare(g, events)
            tail_pool(pool)


def _hadamard(n):
    i = np.arange(n)
    bits = i[:, None] & i[None, :]
    parity = np.zeros((n, n), np.int64)
    for k in range(n.bit_length()):
        parity ^= (bits >> k) & 1
    return (1.0 - 2.0 * parity) / np.sqrt(n)


def _constants():
    ident = np.eye(P, dtype=np.float32)
    mask = np.zeros((P, LT, width(1)), np.float32)
    for lt in range(LT):
        mask[:, lt, SC - LAST:CT * P - LAST] = -1e30
        first = (CT + lt) * P - LAST
        mask[:, lt, first:first + P] = np.where(np.arange(P)[None, :] > np.arange(P)[:, None], -1e30, 0)
    inv = np.float32(1.0) / np.float32(10000.0) ** (np.arange(0, DH, 2, dtype=np.float32) / np.float32(DH))
    angle = np.outer(np.arange(L, dtype=np.float32), inv).astype(np.float32)
    cos = np.concatenate([np.cos(angle)] * 2, -1).astype(np.float32)
    sin = np.concatenate([-np.sin(angle), np.sin(angle)], -1).astype(np.float32)
    tiles = lambda a, n: np.ascontiguousarray(a.reshape(n, P, -1).transpose(1, 0, 2))
    blk = np.zeros((P, 136), np.float32)
    blk[:, 0:P] = np.arange(P)[:, None] // 16 == np.arange(P)[None, :] // 16
    blk[:, P:] = np.arange(P)[:, None] // 16 == np.arange(8)[None, :]
    lower = np.broadcast_to(np.tile((np.arange(NE)[None, :] < np.arange(NE)[:, None]).astype(np.float32), (4, 1)),
                            (P, 4 * NE, NE))
    return dict(c_ident=ident, c_mask=mask,
                c_cos=tiles(cos, LT), c_sin=tiles(sin, LT), c_h256=tiles(_hadamard(D), DC).astype(np.float16),
                c_h1024=tiles(_hadamard(FF), FF // P).astype(np.float16), c_blk=blk,
                c_lower=np.ascontiguousarray(lower))


def kernel(**inputs):
    import numpy as _np
    import concourse.bacc as _bacc
    from concourse import mybir as _mybir
    from concourse.bass_utils import run_bass_kernel_spmd as _run

    a = {n: _np.asarray(v) for n, v in inputs.items()}
    gu = a["L1_ffn_expert_gate_up"]
    laid = dict(
        x=a["x"].reshape(B * L, D), ctxT=a["ctx_2048"].transpose(0, 2, 1),
        wq=a["L0_xattn_wq"], wk=a["L0_xattn_wk"], wv=a["L0_xattn_wv"], wo=a["L0_xattn_wo"],
        wk_ctx=a["L0_xattn_wk_ctx"], wv_ctx=a["L0_xattn_wv_ctx"],
        q_norm=a["L0_xattn_q_norm_w"], k_norm=a["L0_xattn_k_norm_w"],
        w_gateT=a["L0_ffn_w_gate"].T, w_upT=a["L0_ffn_w_up"].T, w_downT=a["L0_ffn_w_down"].T,
        WqT=a["L1_xattn_Wq"].T, WgT=a["L1_xattn_Wg"].T, bg=a["L1_xattn_bg"], WkvT=a["L1_xattn_Wkv"].T,
        WoT=a["L1_xattn_Wo"].T, routerT=a["L1_ffn_router_gate"].T,
        w_lanes=_np.concatenate([a[n].reshape(-1, LANES).T for n in
                        ("L0_ffn_w_gate", "L0_ffn_w_up", "L0_ffn_w_down")]),
        e_gate=gu[:, :, 0::2].transpose(1, 0, 2).reshape(D, NE * FI),
        e_up=gu[:, :, 1::2].transpose(1, 0, 2).reshape(D, NE * FI), e_down=a["L1_ffn_expert_down"], **_constants())
    nc = _bacc.Bacc("TRN2", target_bir_lowering=False, num_devices=1)
    arrays, args = {}, {}
    for name, v in laid.items():
        v = _np.ascontiguousarray(v)
        arrays[f"in_{name}"] = v
        args[name] = nc.dram_tensor(f"in_{name}", v.shape, _mybir.dt.from_np(v.dtype), kind="ExternalInput").ap()
    out = nc.dram_tensor("out_x", (B * L, D), _mybir.dt.float32, kind="ExternalOutput").ap()
    build(nc, *args.values(), out)
    r = _run(nc, [arrays], core_ids=[0])
    return r.results[0]["out_x"].reshape(B, L, D)
```

```python
from contextlib import ExitStack

import numpy as np

import concourse.bass as bass
from concourse import mybir

ALU = mybir.AluOpType
ACT = mybir.ActivationFunctionType
F32 = mybir.dt.float32
F16 = mybir.dt.float16
BF16 = mybir.dt.bfloat16
AX_X = mybir.AxisListType.X
ds = bass.ds

P = 128
B, L, D = 4, 256, 256
SC = 1601
HEADS, KVH, DH = 16, 4, 128
REP = HEADS // KVH
NG = B * KVH
DC = D // P
LT = L // P
TILES = B * LT
CT = -(-SC // P)
CREM = SC - (CT - 1) * P
KT_N = CT + LT
KEYS = KT_N * P
BANK = 512
CHUNKS = -(-KEYS // BANK)
LAST = (CHUNKS - 1) * BANK
UNITS = REP * LT
FF = 1024
NE, FI = 8, 128
WS = 64.0
PSCALE_LN = 10 * float(np.log(2.0))
SCALE = 1.0 / float(np.sqrt(DH))
LANES = 16
LANE_N = FF * D // LANES // NG
LANE_AT = 2
TAIL_LINKS = 31
MAGIC = 1.5 * 2.0 ** 23
EPS_LN, EPS_RMS, EPS_Q, EPS_Z = 1e-5, 1e-6, 1e-5, 1e-6
PIECES = ["q0", "self", "q1", "rem"] + [("ctx", i) for i in range((CT - 1) // 2)]
NP = len(PIECES)
STAGES = 4
KQ_STEPS = 7
JOBS_AT = [[("out", 0), ("out", 1), ("out", 2)],
           [("piece", 0), ("piece", 1)],
           [("piece", 2), ("piece", 3)],
           [("piece", 4), ("piece", 5), ("kq", 0)],
           [("piece", 6), ("kq", 5), ("piece", 7)],
           [("piece", 8), ("kq", 1), ("piece", 9)],
           [("kq", 2), ("kq", 4), ("kq", 3)],
           [("kq", 6)]]
OUT_JOBS = JOBS_AT[0]
LAST_JOBS_AT = [[], [("weight", 0)], [("weight", 1)], [("mean", 0), ("mean", 1), ("weight", 2)],
                [("weight", 3), ("weight", 4)], [("weight", 5)], [("weight", 6)], [("weight", 7)]]
PREP_JOBS = [j for jobs in JOBS_AT[1:] for j in jobs]
KQ_AT = {s: [j for j in PREP_JOBS if j[0] == "kq"].index(("kq", s)) for s in range(KQ_STEPS)}
KV_PIECES = [p for p in range(NP) if PIECES[p] not in ("q0", "q1")]
POOL_ORDER = [0, 1, "q00", "q01", 2, 3, "k", 4, 5, "q10", 6, 7, "q11", 8, 9]
ROPES = [e for e in POOL_ORDER if isinstance(e, str)]

def width(lt):
    return (CT + lt + 1) * P - LAST


def cols(lt, c):
    return BANK if c < CHUNKS - 1 else width(lt)


def build(nc, x, ctxT, wq, wk, wv, wo, wk_ctx, wv_ctx, q_norm, k_norm, w_gateT, w_upT, w_downT,
          WqT, WgT, bg, WkvT, WoT, routerT, w_lanes, e_gate, e_up, e_down,
          c_ident, c_mask, c_cos, c_sin, c_h256, c_blk, c_lower, out):
    main = ExitStack()
    with ExitStack() as ctx:
        def sb(name, shape, dt, at=ctx):
            return at.enter_context(nc.sbuf_tensor(name, shape, dt))

        def sem(name):
            return ctx.enter_context(nc.semaphore(name))

        PS = ctx.enter_context(nc.psum_tensor("PS", [P, 8, BANK], F32))
        SB, TB, OB, XB = 0, 4, 6, 7
        xs = sb("xs", [P, TILES * D], F32)
        R1 = sb("R1", [P, B, DC, 136], F32)
        ident = sb("ident", [P, P], F32)
        ident16 = sb("ident16", [P, P], F16)
        ones = sb("ones", [P, P], F32)
        mhalf = sb("mhalf", [P, TILES], F32)
        eps_ln = sb("eps_ln", [P, TILES], F32)
        eps_rms = sb("eps_rms", [P, TILES], F32)
        per_dh = sb("per_dh", [P, TILES], F32)
        lanes = sb("lanes", [3 * LANES, 1 + LANE_N], F32)
        lsum = sb("lsum", [1, 3 * LANES + 3], F32)
        idle = sb("idle", [P, 6], F32)
        stat = sb("stat", [P, TILES, 6], F32)
        mv = sb("mv", [P, TILES, 2], F32)
        rstd = sb("rstd", [P, TILES], F32)
        wmean = sb("wmean", [P, 4], F32)
        thr = sb("thr", [P, 8], F32)
        identb = sb("identb", [P, P], BF16)
        mask = sb("mask", [P, LT, width(1)], BF16)
        wcol = sb("wcol", [P, 1], F32)
        wo_h = sb("wo_h", [P, HEADS, D], F16)
        wo_l = sb("wo_l", [P, HEADS, D], F16)

        def sm(name, shape, dt):
            return sb(name, shape, dt, main)

        tab = sm("tab", [P, 4, LT, DH], F32)
        ctx_h = sm("ctx_h", [P, B, DC, SC], F16)
        ctx_l = sm("ctx_l", [P, B, DC, SC], F16)
        wc_h = sm("wc_h", [P, DC, KVH, 256], F16)
        wc_l = sm("wc_l", [P, DC, KVH, 256], F16)
        wsf_h = sm("wsf_h", [P, DC, KVH, 768], F16)
        wsf_l = sm("wsf_l", [P, DC, KVH, 768], F16)
        xT_h = sm("xT_h", [P, DC, TILES * P], F16)
        xT_l = sm("xT_l", [P, DC, TILES * P], F16)

        setup = ExitStack()
        w1_h = sb("w1_h", [P, DC, 512], F16, setup)
        w1_l = sb("w1_l", [P, DC, 512], F16, setup)
        blk = sb("blk", [P, 136], F32, setup)
        stage = [sb(f"stage{i}", [P, SC], F32, setup) for i in range(STAGES)]
        xn = sb("xn", [P, TILES * D], F32, setup)
        mask32 = sb("mask32", [P, LT, width(1)], F32, setup)
        nwb = sb("nwb", [P, 2, DH], F32, setup)
        cos = sb("cos", [P, LT, DH], F32, setup)
        sin = sb("sin", [P, LT, DH], F32, setup)
        k_s = sb("k_s", [P, 2, 256], F32, setup)
        ex_s = sb("ex_s", [P, 2, 256], F32, setup)
        kf_s = sb("kf_s", [P, 2, 256], F32, setup)
        vf_s = sb("vf_s", [P, 2, DC, 129], F32, setup)
        setup.close()

        kr = sm("kr", [P, KT_N, DH], F32)
        qr = sm("qr", [P, UNITS, DH], F32)
        sq = sm("sq", [P, 2, REP, DH], BF16)
        ss = sm("ss", [P, 2, REP], F32)
        rs = sm("rs", [P, REP], F32)
        rot = sm("rot", [P, 2, 2, DH], F32)
        kT_h = sm("kT_h", [P, 2, KEYS], F16)
        kT_l = sm("kT_l", [P, 2, KEYS], F16)
        qT_h = sm("qT_h", [P, 2, UNITS, P], F16)
        qT_l = sm("qT_l", [P, 2, UNITS, P], F16)
        v_h = sm("v_h", [P, 2, KT_N, DH + 1], F16)
        v_l = sm("v_l", [P, 2, KT_N, DH], F16)
        pr = sm("pr", [P, KEYS], F32)
        pT_h = sm("pT_h", [P, CHUNKS, BANK], F16)
        pT_l = sm("pT_l", [P, CHUNKS, BANK], F16)
        mx = sm("mx", [P, CHUNKS], F32)
        mr = sm("mr", [P, 1], F32)
        nb = sm("nb", [P, 2], F32)
        rden = sm("rden", [P, 1], F32)
        o_s = sm("o_s", [P, LT, REP, DH], F32)
        oT_h = sm("oT_h", [P, LT, BANK], F16)
        oT_l = sm("oT_l", [P, LT, BANK], F16)
        main.close()

        wg3 = sb("wg3", [P, DC, FF], F16)
        wu3 = sb("wu3", [P, DC, FF], F16)
        wd3 = sb("wd3", [P, FF // P, D], F16)
        wqg_h = sb("wqg_h", [P, 2, DC, D], F16)
        wqg_l = sb("wqg_l", [P, 2, DC, D], F16)
        wo1_h = sb("wo1_h", [P, DC, D], F16)
        wo1_l = sb("wo1_l", [P, DC, D], F16)
        rt_h = sb("rt_h", [P, DC, NE], F16)
        rt_l = sb("rt_l", [P, DC, NE], F16)
        eg_h = sb("eg_h", [P, 2, DC, NE * FI], F16)
        eg_l = sb("eg_l", [P, 2, DC, NE * FI], F16)
        ed_h = sb("ed_h", [P, NE, D], F16)
        ed_l = sb("ed_l", [P, NE, D], F16)
        H0 = sb("H0", [P, DC, D], F16)
        lower = sb("lower", [P, 4 * NE, NE], F32)
        bgs = sb("bgs", [1, D], F32)
        staging = ExitStack()
        wraw = sb("wraw", [P, 4096], F32, staging)
        wraw2 = sb("wraw2", [P, 4096], F32, staging)
        tern = sb("tern", [P, 2048], F32, staging)
        staging.close()
        xn4 = sb("xn4", [P, 4, D], F32)
        xnT_h = sb("xnT_h", [P, DC, BANK], F16)
        xnT_l = sb("xnT_l", [P, DC, BANK], F16)
        am = sb("am", [P, 4, 4], F32)
        dq = sb("dq", [P, 4, 4], F32)
        qf = sb("qf", [P, 2, FF], F32)
        qi = sb("qi", [P, 4, FF], F16)
        qiT = sb("qiT", [P, 4, FF], F16)
        sil = sb("sil", [P, 2, FF], F32)
        hh = sb("hh", [P, 4, FF], F32)
        hT_h = sb("hT_h", [P, 4, FF], F16)
        hT_l = sb("hT_l", [P, 4, FF], F16)
        sg = sb("sg", [P, 4, D], F32)
        z = sb("z", [P, 4, 16], F32)
        lg = sb("lg", [P, 4, NE], F32)
        pb = sb("pb", [P, 4, NE], F32)
        gt = sb("gt", [P, 4, NE * NE], F32)
        eq = sb("eq", [P, 4, NE * NE], F32)
        rk = sb("rk", [P, 4, NE], F32)
        r4 = sb("r4", [P, 4, 4], F32)

        in_const, in_x, in_out = sem("in_const"), sem("in_x"), sem("out_stored")
        in_w = [sem(f"in_w{i}") for i in range(STAGES)]
        set_hi, set_lo = sem("set_hi"), sem("set_lo")
        made_const = sem("made_const")
        ln_stat, ln_agg, ln_var, ln_rstd, ln_out, ln_tr, ln_hi, ln_lo = (
            sem(f"ln0_{n}") for n in ("stat", "agg", "var", "rstd", "out", "tr", "hi", "lo"))
        tab_made = sem("tab_made")
        l1_mm, l1_copy, l1_min, l1_v, l1_exp, l1_k, l1_sum, l1_R = (
            sem(f"l1_{n}") for n in ("mm", "copy", "min", "v", "exp", "k", "sum", "R"))
        pc_mm, pc_copy, pc_norm = (sem(f"pc_{n}") for n in ("mm", "copy", "norm"))
        pool_step, rope_done, rs_made = sem("pool_step"), sem("rope_done"), sem("rs_made")
        kq_tr, kq_hi, kq_lo, vs_hi, vs_lo = (sem(n) for n in ("kq_tr", "kq_hi", "kq_lo", "vs_hi", "vs_lo"))
        qk_done, mx_part, mx_all, nb_done, exp_done = (
            sem(n) for n in ("qk_done", "mx_part", "mx_all", "nb_done", "exp_done"))
        pt_tr, pt_hi, pt_lo, pv_done, rd_done, o_done = (
            sem(n) for n in ("pt_tr", "pt_hi", "pt_lo", "pv_done", "rd_done", "o_done"))
        ot_tr, ot_hi, ot_lo, oj_mm, x1_done = (sem(n) for n in ("ot_tr", "ot_hi", "ot_lo", "oj_mm", "x1_done"))
        dve_step, act_step = sem("dve_step"), sem("act_step")
        lane_in, lane_sum, lane_tr, lane_tot, lane_b = (
            sem(n) for n in ("lane_in", "lane_sum", "lane_tr", "lane_tot", "lane_b"))
        tw_in = [sem(f"tw_in{i}") for i in range(2)]
        tw_const, tw_hi, tw_lo, tw_made = (sem(f"tw_{n}") for n in ("const", "hi", "lo", "made"))
        mean_out = sem("mean_out")
        tl = {n: [sem(f"t{n}{i}") for i in range(4)]
              for n in ("agg", "rstd", "norm", "tr", "hi", "lo")}
        fw_mm, fw_q, qt_tr, qt_ev = ([sem(f"{n}{i}") for i in range(2)]
                                     for n in ("fw_mm", "fw_q", "qt_tr", "qt_ev"))
        gu_mm, gu_silu, gu_h, ht_tr, ht_hi, ht_lo, dn_mm, dn_x = (
            [sem(f"{n}{i}") for i in range(2)]
            for n in ("gu_mm", "gu_silu", "gu_h", "ht_tr", "ht_hi", "ht_lo", "dn_mm", "dn_x"))
        lq_mm, lg_mm, lq_copy, lq_min, lq_exp, lq_f, lg_sig, la_mm, la_out, lo_mm, lo_x = (
            sem(n) for n in ("lq_mm", "lg_mm", "lq_copy", "lq_min", "lq_exp", "lq_f", "lg_sig",
                             "la_mm", "la_out", "lo_mm", "lo_x"))
        bf1, bf2 = sem("bf1"), sem("bf2")
        rt_mm, rt_sub, rt_exp, rt_w = (sem(n) for n in ("rt_mm", "rt_sub", "rt_exp", "rt_w"))

        rows = lambda t: t.rearrange("(c p) n -> p c n", p=P)
        loads = []

        def st(n):
            return stage[len(loads) % STAGES][:, 0:n]

        loads.append(([(st(1024).rearrange("p (c n) -> p c n", c=DC), rows(WkvT))], 1024, WS,
                      w1_h[:, :, :].rearrange("p c n -> p (c n)"), w1_l[:, :, :].rearrange("p c n -> p (c n)")))

        def load_ctx(b):
            for c in range(DC):
                loads.append(([(st(SC), ctxT[b, c * P:(c + 1) * P, :])], SC, 1.0, ctx_h[:, b, c, :], ctx_l[:, b, c, :]))

        load_ctx(0)
        load_ctx(1)
        for c in range(DC):
            cv = st(1024).rearrange("p (h n) -> p h n", h=KVH)
            loads.append(([(cv[:, :, o:o + DH], w[c * P:(c + 1) * P, :].rearrange("p (h n) -> p h n", h=KVH))
                           for o, w in ((0, wk_ctx), (DH, wv_ctx))], 1024, WS,
                          wc_h[:, c, :, :].rearrange("p h n -> p (h n)"), wc_l[:, c, :, :].rearrange("p h n -> p (h n)")))
        for c in range(DC):
            load_ctx(2 + c)
            for h0 in range(0, KVH, 2):
                sv = st(1536).rearrange("p (h n) -> p h n", h=2)
                loads.append(([(sv[:, :, o:o + n],
                                w[c * P:(c + 1) * P, :].rearrange("p (h n) -> p h n", h=KVH)[:, h0:h0 + 2, :])
                               for o, n, w in ((0, 512, wq), (512, DH, wk), (640, DH, wv))], 1536, WS,
                              wsf_h[:, c, h0:h0 + 2, :].rearrange("p h n -> p (h n)"),
                              wsf_l[:, c, h0:h0 + 2, :].rearrange("p h n -> p (h n)")))
        for h0 in range(0, HEADS, 4):
            loads.append(([(st(1024).rearrange("p (h n) -> p h n", h=4),
                            wo[h0 * P:(h0 + 4) * P, :].rearrange("(h p) n -> p h n", p=P))], 1024, WS,
                          wo_h[:, h0:h0 + 4, :].rearrange("p h n -> p (h n)"),
                          wo_l[:, h0:h0 + 4, :].rearrange("p h n -> p (h n)")))
        NL = len(loads)
        FIRST = 1 + DC
        assert NL == FIRST + 4 * B
        load_count = [16 * sum(len(loads[j][0]) for j in range(i % STAGES, i + 1, STAGES)) for i in range(NL)]

        def tst(i, n):
            return (wraw, wraw2)[i % 2][:, 0:n]

        kc = lambda t, p="p c n -> p (c n)": t[:, :, :].rearrange(p)
        tloads = [
            ([(tst(0, 1024)[:, 512 * k:512 * k + 512].rearrange("p (c n) -> p c n", c=DC), rows(w))
              for k, w in enumerate((WqT, WgT))], 1024, WS,
             wqg_h[:, :, :, :].rearrange("p k c n -> p (k c n)"), wqg_l[:, :, :, :].rearrange("p k c n -> p (k c n)")),
            ([(tst(1, 4096)[:, 2048 * k:2048 * k + 2048].rearrange("p (c n) -> p c n", c=DC), rows(w))
              for k, w in enumerate((e_gate, e_up))], 4096, WS,
             eg_h[:, :, :, :].rearrange("p k c n -> p (k c n)"), eg_l[:, :, :, :].rearrange("p k c n -> p (k c n)")),
            ([(tst(2, 512).rearrange("p (c n) -> p c n", c=DC), rows(WoT))], 512, WS, kc(wo1_h), kc(wo1_l)),
            ([(tst(3, 2048).rearrange("p (e n) -> p e n", e=NE), e_down.rearrange("e p n -> p e n"))], 2048, WS,
             kc(ed_h), kc(ed_l)),
            ([(tst(4, 16).rearrange("p (c n) -> p c n", c=DC), rows(routerT))], 16, WS, kc(rt_h), kc(rt_l)),
            ([(tst(5, 2048).rearrange("p (c n) -> p c n", c=DC), rows(w_gateT))], 2048, None, kc(wg3), None),
            ([(tst(6, 2048).rearrange("p (c n) -> p c n", c=DC), rows(w_upT))], 2048, None, kc(wu3), None),
            ([(tst(7, 2048).rearrange("p (c n) -> p c n", c=FF // P), rows(w_downT))], 2048, None, kc(wd3), None),
        ]
        NTL = len(tloads)
        tload_count = [16 * sum(len(tloads[j][0]) for j in range(i % 2, i + 1, 2)) for i in range(NTL)]
        NTERN = 3

        def flat(t):
            return t[:, :, :].rearrange("p a b -> p (a b)")

        def wait(eng, semaphore, value):
            if not isinstance(value, int) or value > 0:
                eng.wait_ge(semaphore, value)

        def l1_walk(eng, step, split, after=None):
            for b in range(B):
                n = b * CT
                step(n, b % 2, CREM)
                step(n + 1, (b + 1) % 2, P)
                if after and b:
                    after(b - 1)
                split(FIRST + 4 * b)
                with eng.Fori(0, 2) as i:
                    step(n + i * 2 + 2, b % 2, P)
                    step(n + i * 2 + 3, (b + 1) % 2, P)
                split(FIRST + 4 * b + 1)
                with eng.Fori(0, (CT - 7) // 2) as i:
                    step(n + i * 2 + 6, b % 2, P)
                    step(n + i * 2 + 7, (b + 1) % 2, P)
                split(FIRST + 4 * b + 2)
                step(n + CT - 1, b % 2, P)
                split(FIRST + 4 * b + 3)
            if after:
                after(B - 1)

        def piece_slots(p):
            return {"q0": REP, "q1": REP, "self": LT, "rem": 1}.get(PIECES[p], 2)

        def piece_rows(p):
            kind = PIECES[p]
            if kind in ("q0", "q1"):
                lt = int(kind[1])
                return qr[:, lt * REP:(lt + 1) * REP, :]
            return kr[:, piece_tile(p):piece_tile(p) + piece_slots(p), :]

        def piece_tile(p):
            kind = PIECES[p]
            return {"self": CT, "rem": CT - 1}[kind] if isinstance(kind, str) else 2 * kind[1]

        def kq_view(s, kT, qT, par, bank):
            if s in (0, 6):
                lt = s // 6
                return qT[:, par, lt * REP:(lt + 1) * REP, :].rearrange("p h n -> p (h n)"), PS[:, bank, :], False
            if s == 4:
                return kT[:, par, (CT - 1) * P:SC], PS[:, bank, 0:CREM], True
            if s == 5:
                return kT[:, par, CT * P:KEYS], PS[:, bank, 0:LT * P], False
            return kT[:, par, (s - 1) * BANK:s * BANK], PS[:, bank, :], True

        PREP_BANKS = [XB, OB, TB, TB + 1]

        def prep_bank(n):
            return PREP_BANKS[(n - len(PREP_JOBS) + 1) % len(PREP_BANKS)]

        def rope_operands(r):
            if r == "k":
                return kr[:, CT:CT + LT, :], tab[:, 2, :, :], tab[:, 3, :, :]
            lt, j = int(r[1]), int(r[2])
            t = lt * REP + 2 * j
            return (qr[:, t:t + 2, :], *(tab[:, k, lt:lt + 1, :].broadcast_to([P, 2, DH]) for k in (0, 1)))

        def pieces_done(p, g):
            return g * NP + p + 1

        def kq_done(steps, g):
            return g * KQ_STEPS + max(KQ_AT[s] for s in steps) + 1

        def v_done(p, g):
            return g * len(KV_PIECES) + KV_PIECES.index(p) + 1

        def wait_bank(pe, job, g):
            kind, i = job
            if kind == "piece" and i in KV_PIECES:
                pe.wait_ge(vs_lo, v_done(i, g))
            elif kind == "piece":
                pe.wait_ge(pc_copy, pieces_done(i, g))
            elif kind == "kq":
                pe.wait_ge(kq_lo, kq_done([i], g))
            elif kind == "mean":
                pe.wait_ge(lane_tot if i == 0 else mean_out, 1)
            elif i == 2:
                pe.wait_ge(x1_done, g + 1)
            else:
                pe.wait_ge(ot_lo, g * 2 + i + 1)

        def groups(eng, group):
            group(0, 0, True, False)
            with eng.Fori(0, NG // 2 - 1) as i:
                group(2 * i + 1, 1, False, False)
                group(2 * i + 2, 0, False, False)
            group(NG - 1, (NG - 1) % 2, False, True)

        def jobs_of(u, first, last):
            if u == 0:
                return [] if first else OUT_JOBS
            return LAST_JOBS_AT[u] if last else JOBS_AT[u]

        def run_job(g, par, job, kinds):
            kind, i = job
            if kind in ("weight", "mean"):
                kinds[kind](i)
            elif kind == "out":
                kinds[kind](i, g - 1)
            else:
                kinds[kind](i, g + 1, 1 - par)

        GB = [4, 6, 0, 2]
        both = lambda j: j // 2 * 2 + 2
        ps16 = lambda bank: PS[:, bank, :].bitcast(F16)

        def tail_pe(pe, three):
            mm = pe.matmul
            pe.wait_ge(tw_const, 48)
            pe.wait_ge(tw_lo, NTL)
            pe.wait_ge(tw_made, 1)
            with pe.Fori(0, 2) as hf:
                def normed(n):
                    for j in range(4):
                        pe.wait_ge(tl["norm"][n], hf * 4 + j + 1 if n < 3 else hf + 1)
                        for c in range(DC):
                            last = pe.transpose(PS[:, c, j * P:(j + 1) * P], xn4[:, j, c * P:(c + 1) * P], ident[:, :])
                            if j == 3:
                                last.then_inc(tl["tr"][n], 1)
                    pe.wait_ge(tl["lo"][n], hf * 2 + 2)

                def tok(j):
                    return [(xnT_h[:, c, j * P:(j + 1) * P], xnT_l[:, c, j * P:(j + 1) * P]) for c in range(DC)]

                def gate_up(n):
                    for j in range(4):
                        if j >= 2:
                            pe.wait_ge(gu_h[n], hf * 4 + j - 1)
                        elif j == 0 and n == 0:
                            pe.wait_ge(qt_ev[0], hf * 2 + 2)
                        g0 = 4 - 4 * (j % 2)
                        for k in range(4):
                            o, w0 = PS[:, g0 + k, :], (k % 2) * BANK
                            for c in range(DC):
                                if n == 0:
                                    w = (wg3, wu3)[k // 2]
                                    last = mm(o, qiT[:, 0, c * BANK + j * P:c * BANK + (j + 1) * P],
                                              w[:, c, w0:w0 + BANK], start=c == 0, stop=c == DC - 1)
                                else:
                                    last = three(o, tok(j)[c], (eg_h[:, k // 2, c, w0:w0 + BANK],
                                                                eg_l[:, k // 2, c, w0:w0 + BANK]), c == 0, c == DC - 1)
                        last.then_inc(gu_mm[n], 1)
                    for j in range(4):
                        pe.wait_ge(gu_h[n], hf * 4 + max(j + 1, 3 if j < 2 else 4))
                        if n == 0:
                            pe.wait_ge(bf2, hf * 4 + j + 1)
                        for f in range(8):
                            last = pe.transpose(PS[:, GB[j] + f // 4, (f % 4) * P:(f % 4 + 1) * P],
                                                hh[:, j, f * P:(f + 1) * P], ident[:, :])
                        last.then_inc(ht_tr[n], 1)

                normed(0)
                for j in range(4):
                    for c in range(DC):
                        for w in range(2):
                            last = mm(PS[:, 2 + j // 2, (j % 2) * D:(j % 2 + 1) * D], tok(j)[c][w], H0[:, c, :],
                                      start=c + w == 0, stop=c + w == DC)
                    last.then_inc(fw_mm[0], 1)
                pe.wait_ge(fw_q[0], hf + 1)
                for c in range(DC):
                    for j in range(4):
                        last = pe.transpose(ps16(c)[:, j * P:(j + 1) * P], qi[:, j, c * P:(c + 1) * P], ident16[:, :])
                    last.then_inc(qt_tr[0], 1)
                gate_up(0)
                for j in range(4):
                    pe.wait_ge(ht_lo[0], hf * 4 + j + 1)
                    for k in range(FF // D):
                        for c in range(DC):
                            f = k * DC + c
                            for w, t in enumerate((hT_h, hT_l)):
                                last = mm(PS[:, GB[j] + k // 2, (k % 2) * D:(k % 2 + 1) * D],
                                          t[:, j, f * P:(f + 1) * P], H0[:, c, :],
                                          start=c + w == 0, stop=c + w == DC)
                    last.then_inc(fw_mm[1], 1)
                for j in range(4):
                    pe.wait_ge(fw_q[1], hf * 4 + j + 1)
                    for f in range(8):
                        last = pe.transpose(ps16(GB[j])[:, f * P:(f + 1) * P], qi[:, j, f * P:(f + 1) * P], ident16[:, :])
                    last.then_inc(qt_tr[1], 1)
                for j in range(4):
                    pe.wait_ge(qt_ev[1], hf * 4 + j + 1)
                    for f in range(8):
                        last = mm(PS[:, GB[j] + 1, 0:D], qiT[:, j, f * P:(f + 1) * P], wd3[:, f, :],
                                  start=f == 0, stop=f == 7)
                    last.then_inc(dn_mm[0], 1)

                normed(1)
                for k in range(DC):
                    for c in range(DC):
                        last = three(PS[:, 4 + k, :],
                                     (wqg_h[:, 0, c, k * P:(k + 1) * P], wqg_l[:, 0, c, k * P:(k + 1) * P]),
                                     (xnT_h[:, c, :], xnT_l[:, c, :]), c == 0, c == DC - 1)
                    last.then_inc(lq_mm, 1)
                for j in range(4):
                    o = PS[:, 2 + j // 2, (j % 2) * D:(j % 2 + 1) * D]
                    mm(o, ones[0:1, :], bgs[:, :], start=True, stop=False)
                    for c in range(DC):
                        last = three(o, tok(j)[c], (wqg_h[:, 1, c, :], wqg_l[:, 1, c, :]), False, c == DC - 1)
                    last.then_inc(lg_mm, 1)
                pe.wait_ge(lq_f, hf * 2 + 2)
                for j in range(4):
                    for k in range(DC):
                        last = mm(PS[:, (6, 7, 4, 5)[j], k * 136:(k + 1) * 136],
                                  hh[:, 0, k * BANK + j * P:k * BANK + (j + 1) * P],
                                  R1[:, ds(hf * 2 + j // 2, 1), k, :].rearrange("p a n -> p (a n)"),
                                  start=True, stop=True)
                    last.then_inc(la_mm, 1)
                normed(3)
                for j in range(4):
                    for c in range(DC):
                        last = three(PS[:, 2 + j // 2, (j % 2) * D:(j % 2 + 1) * D], tok(j)[c],
                                     (wo1_h[:, c, :], wo1_l[:, c, :]), c == 0, c == DC - 1)
                    last.then_inc(lo_mm, 1)

                normed(2)
                for j in range(4):
                    for c in range(DC):
                        last = three(PS[:, 4, j * NE:(j + 1) * NE], tok(j)[c], (rt_h[:, c, :], rt_l[:, c, :]),
                                     c == 0, c == DC - 1)
                last.then_inc(rt_mm, 1)
                pe.wait_ge(rt_sub, hf + 1)
                gate_up(1)
                for j in range(4):
                    pe.wait_ge(ht_lo[1], hf * 4 + j + 1)
                    for f in range(NE):
                        last = three(PS[:, GB[j], 0:D], (hT_h[:, j, f * P:(f + 1) * P], hT_l[:, j, f * P:(f + 1) * P]),
                                     (ed_h[:, f, :], ed_l[:, f, :]), f == 0, f == NE - 1)
                    last.then_inc(dn_mm[1], 1)

        def tail_act(act, copy):
            act.wait_ge(x1_done, NG)
            act.wait_ge(x1_done, NG)
            act.wait_ge(tw_lo, NTL)
            with act.Fori(0, 2) as hf:
                def hi_part(n):
                    for c in range(DC):
                        act.wait_ge(tl["tr"][n], hf * 2 + c + 1)
                        copy(xnT_h[:, c, :], PS[:, c, :]).then_inc(tl["hi"][n], 1)

                def gate_up(n):
                    for j in range(4):
                        act.wait_ge(gu_mm[n], hf * 4 + j + 1)
                        if j >= 2:
                            act.wait_ge(gu_h[n], hf * 4 + j - 1)
                        g0 = 4 - 4 * (j % 2)
                        act.activation(sil[:, j % 2, :], PS[:, g0:g0 + 2, :].rearrange("p b n -> p (b n)"), ACT.Silu,
                                       scale=dq[:, 0, j:j + 1] if n == 0 else 1 / WS).then_inc(gu_silu[n], 1)
                    for j in range(4):
                        act.wait_ge(ht_tr[n], hf * 4 + j + 1)
                        copy(hT_h[:, j, :], PS[:, GB[j]:GB[j] + 2, :].rearrange("p b n -> p (b n)"))\
                            .then_inc(ht_hi[n], 1)

                hi_part(0)
                for c in range(DC):
                    act.wait_ge(qt_tr[0], hf * 2 + c + 1)
                    copy(qiT[:, 0, c * BANK:(c + 1) * BANK], ps16(c)[:, 0:BANK]).then_inc(qt_ev[0], 1)
                gate_up(0)
                for j in range(4):
                    act.wait_ge(qt_tr[1], hf * 4 + j + 1)
                    copy(qiT[:, j, :], ps16(GB[j])).then_inc(qt_ev[1], 1)
                hi_part(1)
                for k in range(DC):
                    act.wait_ge(lq_mm, hf * 2 + k + 1)
                    copy(sil[:, 0, k * BANK:(k + 1) * BANK], PS[:, 4 + k, :], 1 / WS).then_inc(lq_copy, 1)
                for k in range(DC):
                    act.wait_ge(lq_min, hf * 2 + k + 1)
                    e = sil[:, 1, k * BANK:(k + 1) * BANK]
                    act.activation(e, e, ACT.Exp).then_inc(lq_exp, 1)
                for j in range(4):
                    act.wait_ge(lg_mm, hf * 4 + both(j))
                    act.activation(sg[:, j, :], PS[:, 2 + j // 2, (j % 2) * D:(j % 2 + 1) * D], ACT.Sigmoid,
                                   scale=1 / WS).then_inc(lg_sig, 1)
                hi_part(3)
                hi_part(2)
                act.wait_ge(rt_sub, hf + 1)
                act.activation(pb[:, :, :], lg[:, :, :], ACT.Exp).then_inc(rt_exp, 1)
                gate_up(1)

        def tail_pool(pool):
            with pool.Fori(0, 2) as hf:
                for n in range(3):
                    if n == 1:
                        for j in range(4):
                            pool.wait_ge(gu_h[0], hf * 4 + j + 1)
                            if j >= 2:
                                pool.wait_ge(bf2, hf * 4 + j - 1)
                            a, o = (t.rearrange("p (h n) -> p h n", h=2) for t in (hh[:, j, :], qf[:, j % 2, :]))
                            pool.tensor_tensor(o[:, 0, :], a[:, 0, :], a[:, 1, :], ALU.add)
                            pool.tensor_tensor(o[:, 1, :], a[:, 0, :], a[:, 1, :], ALU.subtract).then_inc(bf1, 1)
                    pool.wait_ge(tl["agg"][n], hf + 1)
                    pool.tensor_tensor(rstd[:, 0:4], mv[:, 0:4, 1], eps_ln[:, 0:4], ALU.add).then_inc(ln_var, 1)
                    pool.wait_ge(ln_var, hf * 3 + n + 2)
                    pool.tensor_tensor(rstd[:, 0:4], rstd[:, 0:4], mhalf[:, 0:4], ALU.pow).then_inc(tl["rstd"][n], 1)

        def tail_dve(dve, steps):
            done, count = [steps], [0]

            def link(ins):
                done[0] = done[0] + 1
                count[0] += 1
                ins.then_inc(dve_step, 1)
                dve.wait_ge(dve_step, done[0])

            dve.wait_ge(tw_const, 48)
            dve.tensor_copy(ident16[:, :], ident[:, :])
            dve.tensor_scalar(bgs[:, :], bgs[:, :], WS, None, ALU.mult).then_inc(tw_made, 1)

            base = done[0]
            with dve.Fori(0, 2) as hf:
                done[0] = hf * TAIL_LINKS + base
                count[0] = 0

                def norm(n):
                    if n == 0:
                        dve.memset(idle[:, 5:6], 0.0)
                        for j in range(4):
                            ins = dve.bn_stats(stat[:, j, :], xs[:, ds(hf * 1024 + j * D, D)])
                        link(ins)
                    dve.memset(idle[:, 4:5], 0.0)
                    for j in range(4):
                        ins = dve.bn_aggr(mv[:, j, :], stat[:, j, :])
                    ins.then_inc(tl["agg"][n], 1)
                    dve.wait_ge(tl["rstd"][n], hf + 1)
                    for j in range(4):
                        dve.tensor_scalar(xn4[:, j, :], xs[:, ds(hf * 1024 + j * D, D)], mv[:, j, 0:1],
                                          rstd[:, j:j + 1], ALU.subtract, ALU.mult).then_inc(tl["norm"][n], 1)

                def lo_part(n):
                    for c in range(DC):
                        dve.wait_ge(tl["hi"][n], hf * 2 + c + 1)
                        dve.tensor_tensor(xnT_l[:, c, :], PS[:, c, :], xnT_h[:, c, :], ALU.subtract)\
                           .then_inc(tl["lo"][n], 1)

                def h_lo(n):
                    for j in range(4):
                        dve.wait_ge(ht_hi[n], hf * 4 + j + 1)
                        dve.tensor_tensor(hT_l[:, j, :], PS[:, GB[j]:GB[j] + 2, :].rearrange("p b n -> p (b n)"),
                                          hT_h[:, j, :], ALU.subtract).then_inc(ht_lo[n], 1)

                def quant_scales(weights):
                    link(dve.tensor_scalar(am[:, 0, :], am[:, 0, :], EPS_Q, None, ALU.max))
                    link(dve.reciprocal(am[:, 1, :], am[:, 0, :]))
                    for k, (w, f) in enumerate(weights):
                        dve.tensor_scalar(dq[:, k, :], am[:, 0, :], wmean[:, w:w + 1], f / 127.0, ALU.mult, ALU.mult)
                    link(dve.tensor_scalar(am[:, 2, :], am[:, 1, :], 127.0, None, ALU.mult))

                def add_to_x(o, j, scale, done_sem):
                    at = xs[:, ds(hf * 1024 + j * D, D)]
                    dve.scalar_tensor_tensor(at, o, scale, at, ALU.mult, ALU.add).then_inc(done_sem, 1)

                def stats(j, done_sem):
                    dve.wait_ge(done_sem, hf * 4 + j + 1)
                    dve.memset(idle[:, j:j + 1], 0.0)
                    ins = dve.bn_stats(stat[:, j, :], xs[:, ds(hf * 1024 + j * D, D)])
                    if j == 3:
                        link(ins)

                norm(0)
                lo_part(0)
                for j in range(4):
                    dve.wait_ge(fw_mm[0], hf * 4 + both(j))
                    ins = dve.tensor_reduce(am[:, 0, j:j + 1], PS[:, 2 + j // 2, (j % 2) * D:(j % 2 + 1) * D], AX_X,
                                            ALU.max, apply_absolute_value=True)
                link(ins)
                quant_scales(((0, 1.0), (1, 0.5)))
                for j in range(4):
                    ins = dve.tensor_scalar(qf[:, 0, j * D:(j + 1) * D], PS[:, 2 + j // 2, (j % 2) * D:(j % 2 + 1) * D],
                                            am[:, 2, j:j + 1], MAGIC, ALU.mult, ALU.add)
                link(ins)
                dve.tensor_scalar(qi[:, :, 0:D], qf[:, 0, :].rearrange("p (j n) -> p j n", j=4), MAGIC, 127.0,
                                  ALU.subtract, ALU.min).then_inc(fw_q[0], 1)
                def butterfly(j):
                    dve.wait_ge(bf1, hf * 4 + j + 1)
                    a, o = (t.rearrange("p (h q n) -> p h q n", h=2, q=2) for t in (qf[:, j % 2, :], hh[:, j, :]))
                    dve.tensor_tensor(o[:, :, 0, :], a[:, :, 0, :], a[:, :, 1, :], ALU.add)
                    dve.tensor_tensor(o[:, :, 1, :], a[:, :, 0, :], a[:, :, 1, :], ALU.subtract).then_inc(bf2, 1)

                for j in range(4):
                    dve.wait_ge(gu_silu[0], hf * 4 + j + 1)
                    g0 = 4 - 4 * (j % 2)
                    dve.scalar_tensor_tensor(hh[:, j, :], PS[:, g0 + 2:g0 + 4, :].rearrange("p b n -> p (b n)"),
                                             dq[:, 1, j:j + 1], sil[:, j % 2, :], ALU.mult, ALU.mult)\
                       .then_inc(gu_h[0], 1)
                    if j:
                        butterfly(j - 1)
                butterfly(3)
                h_lo(0)
                for j in range(4):
                    dve.wait_ge(fw_mm[1], hf * 4 + j + 1)
                    y = PS[:, GB[j]:GB[j] + 2, :].rearrange("p b n -> p (b n)")
                    ins = dve.tensor_reduce(am[:, 0, j:j + 1], y, AX_X, ALU.max, apply_absolute_value=True)
                link(ins)
                quant_scales(((2, 1.0),))
                for j in range(4):
                    y = PS[:, GB[j]:GB[j] + 2, :].rearrange("p b n -> p (b n)")
                    link(dve.tensor_scalar(qf[:, j % 2, :], y, am[:, 2, j:j + 1], MAGIC, ALU.mult, ALU.add))
                    dve.tensor_scalar(qi[:, j, :], qf[:, j % 2, :], MAGIC, 127.0, ALU.subtract, ALU.min)\
                       .then_inc(fw_q[1], 1)
                for j in range(4):
                    dve.wait_ge(dn_mm[0], hf * 4 + j + 1)
                    add_to_x(PS[:, GB[j] + 1, 0:D], j, dq[:, 0, j:j + 1], dn_x[0])
                    if j:
                        stats(j - 1, dn_x[0])
                stats(3, dn_x[0])

                norm(1)
                lo_part(1)
                for k in range(DC):
                    dve.wait_ge(lq_copy, hf * 2 + k + 1)
                    dve.tensor_scalar_min(sil[:, 1, k * BANK:(k + 1) * BANK], sil[:, 0, k * BANK:(k + 1) * BANK], 0.0)\
                       .then_inc(lq_min, 1)
                for k in range(DC):
                    dve.wait_ge(lq_exp, hf * 2 + k + 1)
                    dve.scalar_tensor_tensor(hh[:, 0, k * BANK:(k + 1) * BANK], sil[:, 0, k * BANK:(k + 1) * BANK], 0.0,
                                             sil[:, 1, k * BANK:(k + 1) * BANK], ALU.max, ALU.add).then_inc(lq_f, 1)
                heads = lambda j: PS[:, (6, 7, 4, 5)[j], 0:2 * 136].rearrange("p (k n) -> p k n", k=DC)
                for j in range(4):
                    dve.wait_ge(la_mm, hf * 4 + j + 1)
                    ins = dve.tensor_scalar(z[:, j, :].rearrange("p (k h) -> p k h", k=DC), heads(j)[:, :, P:136],
                                            EPS_Z, None, ALU.add)
                link(ins)
                link(dve.reciprocal(z[:, :, :], z[:, :, :]))
                for j in range(4):
                    for k in range(DC):
                        ins = dve.tensor_tensor(
                            xn4[:, j, k * P:(k + 1) * P].rearrange("p (h e) -> p h e", h=8),
                            heads(j)[:, k, 0:P].rearrange("p (h e) -> p h e", h=8),
                            z[:, j, k * 8:(k + 1) * 8].unsqueeze(2).broadcast_to([P, 8, 16]), ALU.mult)
                link(ins)
                dve.wait_ge(lg_sig, hf * 4 + 4)
                dve.tensor_tensor(flat(xn4), flat(xn4), flat(sg), ALU.mult).then_inc(tl["norm"][3], 1)
                lo_part(3)
                for j in range(4):
                    dve.wait_ge(lo_mm, hf * 4 + both(j))
                    add_to_x(PS[:, 2 + j // 2, (j % 2) * D:(j % 2 + 1) * D], j, 1 / WS, lo_x)
                    if j:
                        stats(j - 1, lo_x)
                stats(3, lo_x)

                norm(2)
                lo_part(2)
                dve.wait_ge(rt_mm, hf + 1)
                link(dve.tensor_scalar(flat(lg), PS[:, 4, 0:4 * NE], 1 / WS, None, ALU.mult))
                link(dve.reduce_max(r4[:, 0, :], lg[:, :, :], AX_X))
                over = lambda r: r.unsqueeze(2).broadcast_to([P, 4, NE])
                dve.tensor_tensor(lg[:, :, :], lg[:, :, :], over(r4[:, 0, :]), ALU.subtract).then_inc(rt_sub, 1)
                dve.wait_ge(rt_exp, hf + 1)
                link(dve.reduce_sum(r4[:, 1, :], pb[:, :, :], AX_X))
                link(dve.reciprocal(r4[:, 2, :], r4[:, 1, :]))
                link(dve.tensor_tensor(pb[:, :, :], pb[:, :, :], over(r4[:, 2, :]), ALU.mult))
                pe_ = flat(pb).unsqueeze(2).broadcast_to([P, 4 * NE, NE])
                pj_ = pb[:, :, :].unsqueeze(2).broadcast_to([P, 4, NE, NE])
                g4 = lambda t: t[:, :, :].rearrange("p t (e j) -> p t e j", e=NE)
                pe4 = pb[:, :, :].unsqueeze(3).broadcast_to([P, 4, NE, NE])
                dve.tensor_tensor(g4(gt), pj_, pe4, ALU.is_gt)
                link(dve.tensor_tensor(g4(eq), pj_, pe4, ALU.is_equal))
                link(dve.tensor_tensor(flat(eq), flat(eq), flat(lower), ALU.mult))
                link(dve.tensor_tensor(flat(gt), flat(gt), flat(eq), ALU.add))
                link(dve.reduce_sum(flat(rk), flat(gt).rearrange("p (a j) -> p a j", j=NE), AX_X))
                link(dve.scalar_tensor_tensor(flat(rk), flat(rk), 1.5, flat(pb), ALU.is_lt, ALU.mult))
                link(dve.reduce_sum(r4[:, 1, :], rk[:, :, :], AX_X))
                link(dve.reciprocal(r4[:, 2, :], r4[:, 1, :]))
                dve.scalar_tensor_tensor(pb[:, :, :], rk[:, :, :], 1 / WS, over(r4[:, 2, :]), ALU.mult, ALU.mult)\
                   .then_inc(rt_w, 1)
                dve.wait_ge(rt_w, hf + 1)
                for j in range(4):
                    dve.wait_ge(gu_silu[1], hf * 4 + j + 1)
                    g0 = 4 - 4 * (j % 2)
                    up = PS[:, g0 + 2:g0 + 4, :].rearrange("p b n -> p (b n)")
                    for e in range(NE):
                        ins = dve.scalar_tensor_tensor(hh[:, j, e * P:(e + 1) * P], up[:, e * P:(e + 1) * P],
                                                       pb[:, j, e:e + 1], sil[:, j % 2, e * P:(e + 1) * P],
                                                       ALU.mult, ALU.mult)
                    ins.then_inc(gu_h[1], 1)
                h_lo(1)
                for j in range(4):
                    dve.wait_ge(dn_mm[1], hf * 4 + j + 1)
                    add_to_x(PS[:, GB[j], 0:D], j, 1 / WS, dn_x[1])
                assert count[0] == TAIL_LINKS, count[0]

        block = ctx.enter_context(nc.Block())

        @block.sync
        def _(sp):
            sp.dma_start(ident[:, :], c_ident).then_inc(in_const, 16)
            sp.dma_start(xs[:, :].rearrange("p (t d) -> p t d", t=TILES),
                         x.rearrange("(t p) d -> p t d", p=P)).then_inc(in_x, 16)
            for i, (parts, n, scale, hi, lo) in enumerate(loads):
                if i >= STAGES:
                    sp.wait_ge(set_lo, i - STAGES + 1)
                for dst, src in parts:
                    sp.dma_start(dst, src).then_inc(in_w[i % STAGES], 16)
                if i == FIRST:
                    for dst, src in ((mask32[:, :, :], c_mask), (cos[:, :, :], c_cos),
                                     (sin[:, :, :], c_sin), (blk[:, :], c_blk),
                                     (nwb[:, 0, :], q_norm.partition_broadcast(P)),
                                     (nwb[:, 1, :], k_norm.partition_broadcast(P)),
                                     (wcol[:, :], k_norm.rearrange("(p a) -> p a", a=1))):
                        sp.dma_start(dst, src).then_inc(in_const, 16)
            sp.dma_start(lanes[:, 1:], w_lanes[:, 0:LANE_N]).then_inc(lane_in, 16)
            with sp.Fori(1, NG) as g:
                sp.wait_ge(lane_sum, g)
                sp.dma_start(lanes[:, 1:], w_lanes[:, ds(g * LANE_N, LANE_N)]).then_inc(lane_in, 16)
            sp.wait_ge(kq_lo, NG * KQ_STEPS)
            for i, (parts, n, scale, hi, lo) in enumerate(tloads):
                if i >= 2:
                    sp.wait_ge(tw_lo, i - 1)
                for dst, src in parts:
                    sp.dma_start(dst, src).then_inc(tw_in[i % 2], 16)
                if i == 1:
                    for dst, src in ((H0[:, :, :], c_h256), (lower[:, :, :], c_lower),
                                     (bgs[:, :], bg.rearrange("(a n) -> a n", a=1))):
                        sp.dma_start(dst, src).then_inc(tw_const, 16)
            outv = out.rearrange("(t p) d -> p t d", p=P)
            for hf in range(2):
                sp.wait_ge(dn_x[1], 4 * hf + 4)
                sp.dma_start(outv[:, 4 * hf:4 * hf + 4, :],
                             xs[:, hf * 1024:hf * 1024 + 1024].rearrange("p (t d) -> p t d", t=4)).then_inc(in_out, 16)
            sp.wait_ge(in_out, 32)

        @block.tensor
        def _(pe):
            mm = pe.matmul

            def three(o, lhs, rhs, start, stop):
                (ah, al), (bh, bl) = lhs, rhs
                mm(o, ah, bh, start=start, stop=False)
                mm(o, ah, bl, start=False, stop=False)
                return mm(o, al, bh, start=False, stop=stop)

            pe.wait_ge(in_const, 16)
            for k in range(4):
                c, half = k // 2, k % 2
                pe.wait_ge(ln_out, 4 * half + 4)
                for j in range(4):
                    t = 4 * half + j
                    last = pe.transpose(PS[:, TB + k % 2 if k < 2 else OB + k % 2, j * P:(j + 1) * P],
                                        xn[:, t * D + c * P:t * D + (c + 1) * P], ident[:, :])
                last.then_inc(ln_tr, 1)

            def l1_proj(b, n, par, nrows, col):
                wait(pe, l1_v, n - 1)
                for c in range(DC):
                    last = three(PS[0:nrows, SB + par, :],
                                 (ctx_h[:, b, c, ds(col, nrows)], ctx_l[:, b, c, ds(col, nrows)]),
                                 (w1_h[:, c, :], w1_l[:, c, :]), c == 0, c == DC - 1)
                last.then_inc(l1_mm, 1)

            def l1_summary(b, n, par, nrows, first, final):
                pe.wait_ge(l1_k, n + 1)
                for c in range(DC):
                    last = mm(PS[:, (TB, OB)[b % 2] + c, 0:129], kf_s[0:nrows, par, c * P:(c + 1) * P],
                              vf_s[0:nrows, par, c, :], start=first, stop=final)
                last.then_inc(l1_sum, 1)

            def l1_last(b, t):
                l1_summary(b, b * CT + t, (b + t) % 2, P, False, t == CT - 1)

            pe.wait_ge(ln_lo, 4)
            for b in range(B):
                n = b * CT
                p0, p1 = b % 2, (b + 1) % 2
                pe.wait_ge(set_lo, FIRST if b == 0 else FIRST + 4 * (b - 1) + 2)
                l1_proj(b, n, p0, CREM, (CT - 1) * P)
                if b:
                    l1_last(b - 1, CT - 2)
                l1_proj(b, n + 1, p1, P, 0)
                if b:
                    l1_last(b - 1, CT - 1)
                l1_proj(b, n + 2, p0, P, P)
                wait(pe, l1_R, b - 1)
                l1_summary(b, n, p0, CREM, True, False)
                with pe.Fori(0, (CT - 3) // 2) as i:
                    l1_proj(b, n + i * 2 + 3, p1, P, i * (2 * P) + 2 * P)
                    l1_summary(b, n + i * 2 + 1, p1, P, False, False)
                    l1_proj(b, n + i * 2 + 4, p0, P, i * (2 * P) + 3 * P)
                    l1_summary(b, n + i * 2 + 2, p0, P, False, False)
            l1_last(B - 1, CT - 2)
            l1_last(B - 1, CT - 1)

            def piece(p, g, par, bank=XB):
                b, kv = g // KVH, g % KVH
                kind = PIECES[p]
                if kind in ("q0", "q1"):
                    lt = int(kind[1])
                    jobs = [(PS[:, bank, :], xT_h, xT_l, (b * L + lt * P), P, wsf_h, wsf_l, 0, 512)]
                elif kind == "self":
                    jobs = [(PS[:, bank, lt * 256:lt * 256 + 256], xT_h, xT_l, (b * L + lt * P), P, wsf_h, wsf_l, 512, 256)
                            for lt in range(LT)]
                elif kind == "rem":
                    jobs = [(PS[0:CREM, bank, 0:256], None, None, (CT - 1) * P, CREM, wc_h, wc_l, 0, 256)]
                else:
                    jobs = [(PS[:, bank, j * 256:j * 256 + 256], None, None, (2 * kind[1] + j) * P, P, wc_h, wc_l, 0, 256)
                            for j in range(2)]
                for o, ah, al, col, n, bh, bl, w0, wn in jobs:
                    for c in range(DC):
                        if ah is None:
                            lhs = (ctx_h[:, b, c, col:col + n], ctx_l[:, b, c, col:col + n])
                        else:
                            lhs = (ah[:, c, ds(col, n)], al[:, c, ds(col, n)])
                        last = three(o, lhs, (bh[:, c, kv, w0:w0 + wn], bl[:, c, kv, w0:w0 + wn]),
                                     c == 0, c == DC - 1)
                last.then_inc(pc_mm, 1)

            def transpose_kq(s, g, par, bank=XB):
                if s in (0, 6):
                    lt = s // 6
                    pe.wait_ge(rope_done, g * len(ROPES) + ROPES.index(f"q{lt}1") + 1)
                    for j in range(REP):
                        last = pe.transpose(PS[:, bank, j * P:(j + 1) * P], qr[:, lt * REP + j, :], ident[:, :])
                elif s == 4:
                    pe.wait_ge(pc_norm, pieces_done(3, g))
                    last = pe.transpose(PS[:, bank, 0:CREM], kr[0:CREM, CT - 1, :], ident[0:CREM, 0:CREM])
                elif s == 5:
                    pe.wait_ge(rope_done, g * len(ROPES) + ROPES.index("k") + 1)
                    for j in range(LT):
                        last = pe.transpose(PS[:, bank, j * P:(j + 1) * P], kr[:, CT + j, :], ident[:, :])
                else:
                    pe.wait_ge(pc_norm, pieces_done(3 + 2 * s, g))
                    for j in range(4):
                        last = pe.transpose(PS[:, bank, j * P:(j + 1) * P], kr[:, 4 * (s - 1) + j, :], ident[:, :])
                last.then_inc(kq_tr, 1)

            def out_proj(i, g):
                kv = g % KVH
                if i < LT:
                    pe.wait_ge(o_done, (g + 1) * UNITS)
                    for h in range(REP):
                        last = pe.transpose(PS[:, XB, h * P:(h + 1) * P], o_s[:, i, h, :], ident[:, :])
                    last.then_inc(ot_tr, 1)
                    return
                for lt in range(LT):
                    for h in range(REP):
                        last = three(PS[:, XB, lt * D:(lt + 1) * D],
                                     (oT_h[:, lt, h * P:(h + 1) * P], oT_l[:, lt, h * P:(h + 1) * P]),
                                     (wo_h[:, ds(kv * REP + h, 1), :].rearrange("p a n -> p (a n)"),
                                      wo_l[:, ds(kv * REP + h, 1), :].rearrange("p a n -> p (a n)")),
                                     h == 0, h == REP - 1)
                last.then_inc(oj_mm, 1)

            def qk(u, c, g, par):
                h, lt = u // LT, u % LT
                wait(pe, exp_done, g * (UNITS * CHUNKS) + (u - 1) * CHUNKS + c + 1)
                if u == 0:
                    pe.wait_ge(kq_lo, kq_done([[0, 1], [2], [3], [4, 5]][c], g))
                if u == 1 and c == 0:
                    pe.wait_ge(kq_lo, kq_done([6], g))
                n = cols(lt, c)
                o = PS[:, SB + c, 0:n]
                qs = lt * REP + h
                if c == CHUNKS - 1:
                    mm(o, identb[:, :], mask[:, lt, 0:n], start=True, stop=False)
                three(o, (qT_h[:, par, qs, :], qT_l[:, par, qs, :]),
                      (kT_h[:, par, c * BANK:c * BANK + n], kT_l[:, par, c * BANK:c * BANK + n]),
                      c < CHUNKS - 1, True).then_inc(qk_done, 1)

            def transpose_p(u, c, g):
                n = g * (UNITS * CHUNKS) + u * CHUNKS + c
                pe.wait_ge(exp_done, n + 1)
                wait(pe, pt_lo, n - 1)
                for j in range(cols(u % LT, c) // P):
                    last = pe.transpose(PS[:, TB + c % 2, j * P:(j + 1) * P],
                                        pr[:, c * BANK + j * P:c * BANK + (j + 1) * P], ident[:, :])
                last.then_inc(pt_tr, 1)

            def pv(u, c, g, par):
                n = g * (UNITS * CHUNKS) + u * CHUNKS + c
                pe.wait_ge(pt_lo, n + 1)
                if c == 0:
                    if u == 0:
                        pe.wait_ge(vs_lo, v_done(NP - 1, g))
                    wait(pe, o_done, g * UNITS + u)
                tiles = cols(u % LT, c) // P
                for j in range(tiles):
                    t = c * 4 + j
                    first, final = c == 0 and j == 0, c == CHUNKS - 1 and j == tiles - 1
                    ph, pl = pT_h[:, c, j * P:(j + 1) * P], pT_l[:, c, j * P:(j + 1) * P]
                    mm(PS[:, OB, 0:DH + 1], ph, v_h[:, par, t, :], start=first, stop=False)
                    mm(PS[:, OB, 0:DH], ph, v_l[:, par, t, :], start=False, stop=False)
                    last = mm(PS[:, OB, 0:DH + 1], pl, v_h[:, par, t, :], start=False, stop=final)
                if c == CHUNKS - 1:
                    last.then_inc(pv_done, 1)

            def mean(i):
                if i == 0:
                    pe.wait_ge(lane_sum, NG)
                    pe.transpose(PS[0:1, XB, 0:3 * LANES], lanes[:, 0:1], ident[0:3 * LANES, 0:3 * LANES])\
                      .then_inc(lane_tr, 1)
                else:
                    mm(PS[:, XB, 0:NTERN], ones[0:1, :], lsum[:, 3 * LANES:], start=True, stop=True).then_inc(lane_b, 1)

            kinds = {"out": out_proj, "piece": piece, "kq": transpose_kq, "mean": mean}

            def group(g, par, first, last):
                before = [(PREP_JOBS[-1], g)]
                for u in range(UNITS):
                    todo = list(jobs_of(u, first, last))

                    def job():
                        if todo and todo[0][0] == "weight":
                            todo.pop(0)
                        elif todo:
                            wait_bank(pe, *before[0])
                            before[0] = (todo[0], g - 1 if todo[0][0] == "out" else g + 1)
                            run_job(g, par, todo.pop(0), kinds)

                    for c in range(CHUNKS):
                        transpose_p(u, c, g)
                        if u + 1 < UNITS:
                            qk(u + 1, c, g, par)
                        elif not last:
                            qk(0, c, g + 1, 1 - par)
                        if c == 1:
                            job()
                    pv(u, 0, g, par)
                    job()
                    pv(u, 1, g, par)
                    pv(u, 2, g, par)
                    pv(u, 3, g, par)
                    job()

            pe.wait_ge(set_lo, NL)
            pe.wait_ge(made_const, 2)
            pe.wait_ge(l1_R, B)
            for n, (kind, i) in enumerate(PREP_JOBS):
                if n >= len(PREP_BANKS):
                    wait_bank(pe, PREP_JOBS[n - len(PREP_BANKS)], 0)
                kinds[kind](i, 0, 0, prep_bank(n))
            for c in range(CHUNKS):
                qk(0, c, 0, 0)
            groups(pe, group)
            for n, (kind, i) in enumerate(OUT_JOBS):
                wait_bank(pe, OUT_JOBS[n - 1] if n else ("mean", 1), NG - 1)
                kinds[kind](i, NG - 1)
            pe.wait_ge(x1_done, NG)
            tail_pe(pe, three)

        @block.scalar
        def _(act):
            copy = lambda o, i, scale=1.0: act.activation(o, i, ACT.Copy, scale=scale)

            def set_hi_part(i):
                parts, n, scale, hi, lo = loads[i]
                act.wait_ge(in_w[i % STAGES], load_count[i])
                copy(hi, stage[i % STAGES][:, 0:n], scale).then_inc(set_hi, 1)

            for k in range(4):
                c, half = k // 2, k % 2
                if k == 0:
                    set_hi_part(0)
                act.wait_ge(ln_tr, k + 1)
                copy(xT_h[:, c, half * BANK:(half + 1) * BANK],
                     PS[:, TB + k % 2 if k < 2 else OB + k % 2, :]).then_inc(ln_hi, 1)
            for i in range(1, FIRST):
                set_hi_part(i)

            def l1_step(n, par, nrows):
                act.wait_ge(l1_mm, n + 1)
                wait(act, l1_k, n - 1)
                copy(k_s[0:nrows, par, :], PS[0:nrows, SB + par, 0:256], 1 / WS).then_inc(l1_copy, 1)
                act.wait_ge(l1_min, n + 1)
                act.activation(ex_s[0:nrows, par, :], ex_s[0:nrows, par, :], ACT.Exp).then_inc(l1_exp, 1)

            act.wait_ge(made_const, 1)
            l1_walk(act, l1_step, set_hi_part)

            def piece_out(p, g, par, bank=XB):
                kind = PIECES[p]
                q = kind in ("q0", "q1")
                wait(act, pc_norm, pieces_done(p, g) - 2)
                act.wait_ge(pc_mm, pieces_done(p, g))
                rows, w = (CREM if kind == "rem" else P), (DH if q else 2 * DH)
                for j in range(piece_slots(p)):
                    act.activation(sq[0:rows, p % 2, j, :], PS[0:rows, bank, j * w:j * w + DH], ACT.Square,
                                   scale=1 / WS, accum_out=ss[0:rows, p % 2, j:j + 1])
                v = PS[0:rows, bank, 0:piece_slots(p) * w].rearrange("p (t d) -> p t d", d=w)
                copy(piece_rows(p)[0:rows, :, :], v[:, :, 0:DH], 1 / WS).then_inc(pc_copy, 1)
                if not q:
                    t = piece_tile(p)
                    copy(v_h[0:rows, par, t:t + piece_slots(p), 0:DH], v[:, :, DH:], 1 / WS).then_inc(vs_hi, 1)

            def kq_hi_part(s, g, par, bank=XB):
                act.wait_ge(kq_tr, kq_done([s], g))
                o, i, w = kq_view(s, kT_h, qT_h, par, bank)
                act.activation(o, i, ACT.Copy, scale=wcol[:, 0:1] if w else 1.0).then_inc(kq_hi, 1)

            def exp(u, c, g):
                n = g * (UNITS * CHUNKS) + u * CHUNKS + c
                if c == 0:
                    act.wait_ge(nb_done, g * UNITS + u + 1)
                w = cols(u % LT, c)
                act.activation(pr[:, c * BANK:c * BANK + w], PS[:, SB + c, 0:w], ACT.Exp,
                               bias=nb[:, u % 2:u % 2 + 1], scale=SCALE).then_inc(exp_done, 1)

            def p_hi(u, c, g):
                act.wait_ge(pt_tr, g * (UNITS * CHUNKS) + u * CHUNKS + c + 1)
                w = cols(u % LT, c)
                copy(pT_h[:, c, 0:w], PS[:, TB + c % 2, 0:w]).then_inc(pt_hi, 1)

            def out_hi_part(i, g):
                if i < LT:
                    wait(act, oj_mm, g)
                    act.wait_ge(ot_tr, g * 2 + i + 1)
                    copy(oT_h[:, i, :], PS[:, XB, :]).then_inc(ot_hi, 1)

            def weight_hi_part(i):
                parts, n, scale, hi, lo = tloads[i]
                if i < NTL - NTERN:
                    act.wait_ge(tw_in[i % 2], tload_count[i])
                    copy(hi, tst(i, n), scale).then_inc(tw_hi, 1)

            kinds = {"out": out_hi_part, "piece": piece_out, "kq": kq_hi_part,
                     "weight": weight_hi_part, "mean": lambda i: None}

            def group(g, par, first, last):
                for u in range(UNITS):
                    todo = list(jobs_of(u, first, last))

                    def job():
                        if todo:
                            run_job(g, par, todo.pop(0), kinds)

                    p_hi(u, 0, g)
                    exp(u, 2, g)
                    p_hi(u, 1, g)
                    exp(u, 3, g)
                    job()
                    p_hi(u, 2, g)
                    p_hi(u, 3, g)
                    job()
                    if u + 1 < UNITS or not last:
                        nu, ng = ((u + 1, g) if u + 1 < UNITS else (0, g + 1))
                        exp(nu, 0, ng)
                        exp(nu, 1, ng)
                    job()

            act.wait_ge(made_const, 2)
            for n, (kind, i) in enumerate(PREP_JOBS):
                kinds[kind](i, 0, 0, prep_bank(n))
            exp(0, 0, 0)
            exp(0, 1, 0)
            groups(act, group)
            for kind, i in OUT_JOBS:
                kinds[kind](i, NG - 1)
            tail_act(act, copy)

        @block.vector
        def _(dve):
            steps = [0]

            def link(ins):
                steps[0] += 1
                ins.then_inc(dve_step, 1)
                dve.wait_ge(dve_step, steps[0])

            dve.memset(ones[:, :], 1.0)
            dve.memset(lanes[:, 0:1], 0.0)
            for t, value in ((mhalf, -0.5), (eps_ln, EPS_LN), (eps_rms, EPS_RMS), (per_dh, 1.0 / DH)):
                dve.memset(t[:, :], value)
            dve.memset(vf_s[:, :, :, :], 1.0).then_inc(made_const, 1)

            dve.wait_ge(in_x, 16)
            for t in range(TILES):
                dve.bn_stats(stat[:, t, :], xs[:, t * D:(t + 1) * D]).then_inc(ln_stat, 1)
            for t in range(TILES):
                dve.wait_ge(ln_stat, t + 1)
                dve.bn_aggr(mv[:, t, :], stat[:, t, :]).then_inc(ln_agg, 1)

            def set_lo_part(i):
                parts, n, scale, hi, lo = loads[i]
                dve.wait_ge(set_hi, i + 1)
                dve.scalar_tensor_tensor(lo, stage[i % STAGES][:, 0:n], scale, hi, ALU.mult, ALU.subtract)\
                   .then_inc(set_lo, 1)

            dve.wait_ge(ln_rstd, 1)
            for t in range(TILES):
                dve.tensor_scalar(xn[:, t * D:(t + 1) * D], xs[:, t * D:(t + 1) * D], mv[:, t, 0:1],
                                  rstd[:, t:t + 1], ALU.subtract, ALU.mult).then_inc(ln_out, 1)
            for k in range(4):
                c, half = k // 2, k % 2
                if k == 0:
                    set_lo_part(0)
                dve.wait_ge(ln_hi, k + 1)
                dve.tensor_tensor(xT_l[:, c, half * BANK:(half + 1) * BANK],
                                  PS[:, TB + k % 2 if k < 2 else OB + k % 2, :],
                                  xT_h[:, c, half * BANK:(half + 1) * BANK], ALU.subtract).then_inc(ln_lo, 1)
            for i in range(1, FIRST):
                set_lo_part(i)

            def tables():
                dve.tensor_copy(identb[:, :], ident[:, :])
                dve.tensor_copy(mask[:, :, :], mask32[:, :, :])
                for k in range(2):
                    for lt in range(LT):
                        dve.tensor_tensor(tab[:, 2 * k, lt, :], cos[:, lt, :], nwb[:, k, :], ALU.mult)
                        for a, o in ((0, 64), (64, 0)):
                            dve.tensor_tensor(tab[:, 2 * k + 1, lt, a:a + 64], sin[:, lt, a:a + 64],
                                              nwb[:, k, o:o + 64], ALU.mult).then_inc(tab_made, 1)

            def l1_step(n, par, nrows):
                dve.wait_ge(l1_copy, n + 1)
                dve.tensor_scalar_min(ex_s[0:nrows, par, :], k_s[0:nrows, par, :], 0.0).then_inc(l1_min, 1)
                wait(dve, l1_sum, n - 1)
                dve.tensor_scalar(vf_s[0:nrows, par, :, 0:P],
                                  PS[0:nrows, SB + par, 256:512].rearrange("p (c n) -> p c n", c=DC),
                                  1 / WS, None, ALU.mult).then_inc(l1_v, 1)
                dve.wait_ge(l1_exp, n + 1)
                dve.scalar_tensor_tensor(kf_s[0:nrows, par, :], k_s[0:nrows, par, :], 0.0,
                                         ex_s[0:nrows, par, :], ALU.max, ALU.add).then_inc(l1_k, 1)

            def l1_end(b):
                if b == 0:
                    dve.wait_ge(in_const, 16 * 8)
                if b == B - 1:
                    tables()
                dve.wait_ge(l1_sum, b * CT + CT)
                bank = (TB, OB)[b % 2]
                for c in range(DC):
                    dve.tensor_tensor(R1[:, b, c, 0:P], PS[:, bank + c, 0:P], blk[:, 0:P], ALU.mult)
                    last = dve.tensor_scalar(R1[:, b, c, P:136], blk[:, P:136], PS[:, bank + c, P:P + 1], None, ALU.mult)
                last.then_inc(l1_R, 1)

            l1_walk(dve, l1_step, set_lo_part, l1_end)

            dve.wait_ge(set_lo, NL)
            dve.wait_ge(l1_sum, B * CT)
            dve.wait_ge(tab_made, 8)
            dve.memset(kr[:, CT - 1, :], 0.0)
            dve.memset(ss[:, :, :], 1.0)
            for par in range(2):
                dve.memset(v_h[:, par, CT - 1, 0:DH], 1.0)
                dve.memset(v_h[:, par, :, DH:DH + 1], 1.0)
                dve.memset(v_l[:, par, CT - 1, :], 0.0)
                dve.memset(kT_h[:, par, SC:CT * P], 0.0)
                last = dve.memset(kT_l[:, par, SC:CT * P], 0.0)
            last.then_inc(made_const, 1)

            def piece_lo(p, g, par, bank=XB):
                if p in KV_PIECES:
                    t, n = piece_tile(p), piece_slots(p)
                    rows = CREM if PIECES[p] == "rem" else P
                    dve.wait_ge(vs_hi, v_done(p, g))
                    v = PS[0:rows, bank, 0:n * 2 * DH].rearrange("p (t d) -> p t d", d=2 * DH)[:, :, DH:]
                    dve.scalar_tensor_tensor(v_l[0:rows, par, t:t + n, :], v, 1 / WS, v_h[0:rows, par, t:t + n, 0:DH],
                                             ALU.mult, ALU.subtract).then_inc(vs_lo, 1)

            def kq_lo_part(s, g, par, bank=XB):
                dve.wait_ge(kq_hi, kq_done([s], g))
                hi, i, w = kq_view(s, kT_h, qT_h, par, bank)
                lo, _, _ = kq_view(s, kT_l, qT_l, par, bank)
                if w:
                    dve.scalar_tensor_tensor(lo, i, wcol[:, 0:1], hi, ALU.mult, ALU.subtract).then_inc(kq_lo, 1)
                else:
                    dve.tensor_tensor(lo, i, hi, ALU.subtract).then_inc(kq_lo, 1)

            def chunk_max(u, c, g):
                dve.wait_ge(qk_done, g * (UNITS * CHUNKS) + u * CHUNKS + c + 1)
                dve.reduce_max(mx[:, c:c + 1], PS[:, SB + c, 0:cols(u % LT, c)], AX_X).then_inc(mx_part, 1)

            def row_max(u, g):
                dve.wait_ge(mx_part, g * (UNITS * CHUNKS) + u * CHUNKS + CHUNKS)
                dve.reduce_max(mr[:, :], mx[:, :], AX_X).then_inc(mx_all, 1)
                dve.wait_ge(mx_all, g * UNITS + u + 1)
                dve.tensor_scalar(nb[:, u % 2:u % 2 + 1], mr[:, :], -SCALE, PSCALE_LN, ALU.mult, ALU.add)\
                   .then_inc(nb_done, 1)

            def p_lo(u, c, g):
                dve.wait_ge(pt_hi, g * (UNITS * CHUNKS) + u * CHUNKS + c + 1)
                w = cols(u % LT, c)
                dve.tensor_tensor(pT_l[:, c, 0:w], PS[:, TB + c % 2, 0:w], pT_h[:, c, 0:w], ALU.subtract)\
                   .then_inc(pt_lo, 1)

            def lane_step(g):
                dve.wait_ge(lane_in, g * 16 + 16)
                dve.tensor_reduce(lanes[:, 0:1], lanes[:, :], AX_X, ALU.add, apply_absolute_value=True)\
                   .then_inc(lane_sum, 1)

            def out_norm(u, g):
                h, lt = u // LT, u % LT
                if u == 0:
                    wait(dve, ot_tr, 2 * g)
                dve.wait_ge(pv_done, g * UNITS + u + 1)
                dve.reciprocal(rden[:, :], PS[:, OB, DH:DH + 1]).then_inc(rd_done, 1)
                dve.wait_ge(rd_done, g * UNITS + u + 1)
                dve.tensor_scalar(o_s[:, lt, h, :], PS[:, OB, 0:DH], rden[:, 0:1], None, ALU.mult)\
                   .then_inc(o_done, 1)

            def out_lo_part(i, g):
                if i < LT:
                    dve.wait_ge(ot_hi, g * 2 + i + 1)
                    dve.tensor_tensor(oT_l[:, i, :], PS[:, XB, :], oT_h[:, i, :], ALU.subtract).then_inc(ot_lo, 1)
                    return
                dve.wait_ge(oj_mm, g + 1)
                wait(dve, x1_done, g)
                at = xs[:, ds(g // KVH * BANK, BANK)]
                dve.scalar_tensor_tensor(at, PS[:, XB, :], 1 / WS, at, ALU.mult, ALU.add).then_inc(x1_done, 1)

            def mean(i):
                if i == 0:
                    dve.wait_ge(lane_tr, 1)
                    dve.reduce_sum(lsum[:, 3 * LANES:],
                                   PS[0:1, XB, 0:3 * LANES].rearrange("p (i j) -> p i j", j=LANES), AX_X)\
                       .then_inc(lane_tot, 1)
                    return
                dve.wait_ge(lane_b, 1)
                dve.tensor_scalar(wmean[:, 0:NTERN], PS[:, XB, 0:NTERN], 1.0 / (FF * D), EPS_Q, ALU.mult, ALU.max)\
                   .then_inc(mean_out, 1)
                dve.wait_ge(mean_out, 1)
                dve.tensor_scalar(thr[:, 0:NTERN], wmean[:, 0:NTERN], 0.5, None, ALU.mult)
                link(dve.tensor_scalar(thr[:, 4:4 + NTERN], wmean[:, 0:NTERN], -0.5, None, ALU.mult))

            def weight_lo_part(i):
                parts, n, scale, hi, lo = tloads[i]
                w, t = tst(i, n), i - (NTL - NTERN)
                if t < 0:
                    dve.wait_ge(tw_hi, i + 1)
                    dve.scalar_tensor_tensor(lo, w, scale, hi, ALU.mult, ALU.subtract).then_inc(tw_lo, 1)
                    return
                dve.wait_ge(tw_in[i % 2], tload_count[i])
                link(dve.tensor_scalar(tern[:, :], w, thr[:, 4 + t:5 + t], None, ALU.is_lt))
                dve.scalar_tensor_tensor(hi, w, thr[:, t:t + 1], tern[:, :], ALU.is_gt, ALU.subtract)\
                   .then_inc(tw_lo, 1)
                dve.wait_ge(tw_lo, i + 1)

            kinds = {"out": out_lo_part, "piece": piece_lo, "kq": kq_lo_part,
                     "weight": weight_lo_part, "mean": mean}

            def group(g, par, first, last):
                for u in range(UNITS):
                    todo = list(jobs_of(u, first, last))

                    def job():
                        if todo:
                            run_job(g, par, todo.pop(0), kinds)

                    if u > 0:
                        out_norm(u - 1, g)
                    elif not first:
                        out_norm(UNITS - 1, g - 1)
                    nu, ng = ((u + 1, g) if u + 1 < UNITS else (0, g + 1))
                    for c in range(CHUNKS):
                        p_lo(u, c, g)
                        if u + 1 < UNITS or not last:
                            chunk_max(nu, c, ng)
                        if c == 1:
                            job()
                    if u + 1 < UNITS or not last:
                        row_max(nu, ng)
                    if u == LANE_AT:
                        lane_step(g)
                    job()
                    job()

            def norm(p):
                n, v = piece_slots(p), piece_rows(p)
                dve.wait_ge(rs_made, p + 1)
                dve.tensor_tensor(v, v, rs[:, 0:n].unsqueeze(2).broadcast_to([P, n, DH]), ALU.mult).then_inc(pc_norm, 1)

            def rope(r):
                v, cs, sn = rope_operands(r)
                dve.wait_ge(pc_norm, {"k": 2, "q0": 1, "q1": 3}[r[:2]])
                wait(dve, rope_done, ROPES.index(r))
                dve.tensor_tensor(rot[:, 0, :, :], v, cs, ALU.mult)
                dve.tensor_tensor(rot[:, 1, :, 0:64], v[:, :, 64:DH], sn[:, :, 0:64], ALU.mult)
                link(dve.tensor_tensor(rot[:, 1, :, 64:DH], v[:, :, 0:64], sn[:, :, 64:DH], ALU.mult))
                dve.tensor_tensor(v, rot[:, 0, :, :], rot[:, 1, :, :], ALU.add).then_inc(rope_done, 1)

            todo = list(POOL_ORDER)
            for n, (kind, i) in enumerate(PREP_JOBS):
                kinds[kind](i, 0, 0, prep_bank(n))
                while kind == "piece" and todo and (isinstance(todo[0], str) or todo[0] < i):
                    e = todo.pop(0)
                    rope(e) if isinstance(e, str) else norm(e)
                if kind == "piece" and i == NP - 1:
                    norm(todo.pop(0))
            for c in range(CHUNKS):
                chunk_max(0, c, 0)
            row_max(0, 0)
            groups(dve, group)
            out_norm(UNITS - 1, NG - 1)
            for kind, i in OUT_JOBS:
                kinds[kind](i, NG - 1)
            tail_dve(dve, steps[0])

        @block.gpsimd
        def _(pool):
            pool.wait_ge(ln_agg, TILES)
            pool.wait_ge(made_const, 1)
            pool.tensor_tensor(rstd[:, :], mv[:, :, 1], eps_ln[:, :], ALU.add).then_inc(ln_var, 1)
            pool.wait_ge(ln_var, 1)
            pool.tensor_tensor(rstd[:, :], rstd[:, :], mhalf[:, 0:TILES], ALU.pow).then_inc(ln_rstd, 1)

            PER_PIECE, PER_ROPE = 3, 3
            PER_G = NP * PER_PIECE + len(ROPES) * PER_ROPE

            def prepare(g, first=False):
                done = [0 if first else (g - 1) * PER_G + NP * (PER_PIECE - 1)]

                def step(ins):
                    done[0] = done[0] + 1
                    ins.then_inc(pool_step, 1)
                    pool.wait_ge(pool_step, done[0])

                for p in POOL_ORDER:
                    if first and isinstance(p, str):
                        continue
                    if not isinstance(p, str):
                        n = piece_slots(p)
                        v = piece_rows(p)
                        pool.wait_ge(pc_copy, pieces_done(p, g))
                        wait(pool, pc_norm, g * NP + p)
                        step(pool.tensor_tensor(rs[:, 0:n], ss[:, p % 2, 0:n], per_dh[:, 0:n], ALU.mult))
                        step(pool.tensor_tensor(rs[:, 0:n], rs[:, 0:n], eps_rms[:, 0:n], ALU.add))
                        last = pool.tensor_tensor(rs[:, 0:n], rs[:, 0:n], mhalf[:, 0:n], ALU.pow)
                        if first:
                            last.then_inc(rs_made, 1)
                            continue
                        step(last)
                        pool.tensor_tensor(v, v, rs[:, 0:n].unsqueeze(2).broadcast_to([P, n, DH]), ALU.mult)\
                            .then_inc(pc_norm, 1)
                    else:
                        r = ROPES.index(p)
                        pool.wait_ge(pc_norm, g * NP + {"k": 2, "q0": 1, "q1": 3}[p[:2]])
                        wait(pool, rope_done, g * len(ROPES) + r)
                        v, cs, sn = rope_operands(p)
                        step(pool.tensor_tensor(rot[:, 0, :, :], v, cs, ALU.mult))
                        pool.tensor_tensor(rot[:, 1, :, 0:64], v[:, :, 64:DH], sn[:, :, 0:64], ALU.mult)\
                            .then_inc(pool_step, 1)
                        done[0] = done[0] + 1
                        step(pool.tensor_tensor(rot[:, 1, :, 64:DH], v[:, :, 0:64], sn[:, :, 64:DH], ALU.mult))
                        pool.tensor_tensor(v, rot[:, 0, :, :], rot[:, 1, :, :], ALU.add).then_inc(rope_done, 1)

            pool.wait_ge(made_const, 2)
            prepare(0, True)
            with pool.Fori(1, NG) as g:
                prepare(g)
            tail_pool(pool)


def _hadamard(n):
    i = np.arange(n)
    bits = i[:, None] & i[None, :]
    parity = np.zeros((n, n), np.int64)
    for k in range(n.bit_length()):
        parity ^= (bits >> k) & 1
    return (1.0 - 2.0 * parity) / np.sqrt(n)


def _constants():
    ident = np.eye(P, dtype=np.float32)
    mask = np.zeros((P, LT, width(1)), np.float32)
    for lt in range(LT):
        mask[:, lt, SC - LAST:CT * P - LAST] = -1e30
        first = (CT + lt) * P - LAST
        mask[:, lt, first:first + P] = np.where(np.arange(P)[None, :] > np.arange(P)[:, None], -1e30, 0)
    inv = np.float32(1.0) / np.float32(10000.0) ** (np.arange(0, DH, 2, dtype=np.float32) / np.float32(DH))
    angle = np.outer(np.arange(L, dtype=np.float32), inv).astype(np.float32)
    cos = np.concatenate([np.cos(angle)] * 2, -1).astype(np.float32)
    sin = np.concatenate([-np.sin(angle), np.sin(angle)], -1).astype(np.float32)
    tiles = lambda a, n: np.ascontiguousarray(a.reshape(n, P, -1).transpose(1, 0, 2))
    blk = np.zeros((P, 136), np.float32)
    blk[:, 0:P] = np.arange(P)[:, None] // 16 == np.arange(P)[None, :] // 16
    blk[:, P:] = np.arange(P)[:, None] // 16 == np.arange(8)[None, :]
    lower = np.broadcast_to(np.tile((np.arange(NE)[None, :] < np.arange(NE)[:, None]).astype(np.float32), (4, 1)),
                            (P, 4 * NE, NE))
    return dict(c_ident=ident, c_mask=mask,
                c_cos=tiles(cos, LT), c_sin=tiles(sin, LT), c_h256=tiles(_hadamard(D), DC).astype(np.float16),
                c_blk=blk,
                c_lower=np.ascontiguousarray(lower))


def kernel(**inputs):
    import numpy as _np
    import concourse.bacc as _bacc
    from concourse import mybir as _mybir
    from concourse.bass_utils import run_bass_kernel_spmd as _run

    a = {n: _np.asarray(v) for n, v in inputs.items()}
    gu = a["L1_ffn_expert_gate_up"]
    laid = dict(
        x=a["x"].reshape(B * L, D), ctxT=a["ctx_2048"].transpose(0, 2, 1),
        wq=a["L0_xattn_wq"], wk=a["L0_xattn_wk"], wv=a["L0_xattn_wv"], wo=a["L0_xattn_wo"],
        wk_ctx=a["L0_xattn_wk_ctx"], wv_ctx=a["L0_xattn_wv_ctx"],
        q_norm=a["L0_xattn_q_norm_w"], k_norm=a["L0_xattn_k_norm_w"],
        w_gateT=a["L0_ffn_w_gate"].T, w_upT=a["L0_ffn_w_up"].T, w_downT=a["L0_ffn_w_down"].T,
        WqT=a["L1_xattn_Wq"].T, WgT=a["L1_xattn_Wg"].T, bg=a["L1_xattn_bg"], WkvT=a["L1_xattn_Wkv"].T,
        WoT=a["L1_xattn_Wo"].T, routerT=a["L1_ffn_router_gate"].T,
        w_lanes=_np.concatenate([a[n].reshape(-1, LANES).T for n in
                        ("L0_ffn_w_gate", "L0_ffn_w_up", "L0_ffn_w_down")]),
        e_gate=gu[:, :, 0::2].transpose(1, 0, 2).reshape(D, NE * FI),
        e_up=gu[:, :, 1::2].transpose(1, 0, 2).reshape(D, NE * FI), e_down=a["L1_ffn_expert_down"], **_constants())
    nc = _bacc.Bacc("TRN2", target_bir_lowering=False, num_devices=1)
    arrays, args = {}, {}
    for name, v in laid.items():
        v = _np.ascontiguousarray(v)
        arrays[f"in_{name}"] = v
        args[name] = nc.dram_tensor(f"in_{name}", v.shape, _mybir.dt.from_np(v.dtype), kind="ExternalInput").ap()
    out = nc.dram_tensor("out_x", (B * L, D), _mybir.dt.float32, kind="ExternalOutput").ap()
    build(nc, *args.values(), out)
    r = _run(nc, [arrays], core_ids=[0])
    return r.results[0]["out_x"].reshape(B, L, D)
```

```python
from contextlib import ExitStack

import numpy as np

import concourse.bass as bass
from concourse import mybir

ALU = mybir.AluOpType
ACT = mybir.ActivationFunctionType
F32 = mybir.dt.float32
F16 = mybir.dt.float16
BF16 = mybir.dt.bfloat16
AX_X = mybir.AxisListType.X
ds = bass.ds

P = 128
B, L, D = 4, 256, 256
SC = 1601
HEADS, KVH, DH = 16, 4, 128
REP = HEADS // KVH
NG = B * KVH
DC = D // P
LT = L // P
TILES = B * LT
CT = -(-SC // P)
CREM = SC - (CT - 1) * P
KT_N = CT + LT
KEYS = KT_N * P
BANK = 512
CHUNKS = -(-KEYS // BANK)
LAST = (CHUNKS - 1) * BANK
UNITS = REP * LT
FF = 1024
NE, FI = 8, 128
WS = 64.0
PSCALE_LN = 10 * float(np.log(2.0))
SCALE = 1.0 / float(np.sqrt(DH))
LANES = 16
LANE_N = FF * D // LANES // NG
LANE_AT = 2
MAGIC = 1.5 * 2.0 ** 23
EPS_LN, EPS_RMS, EPS_Q, EPS_Z = 1e-5, 1e-6, 1e-5, 1e-6
PIECES = ["q0", "self", "q1", "rem"] + [("ctx", i) for i in range((CT - 1) // 2)]
NP = len(PIECES)
STAGES = 4
KQ_STEPS = 7
JOBS_AT = [[("out", 0), ("out", 1), ("out", 2)],
           [("piece", 0), ("piece", 1)],
           [("piece", 2), ("piece", 3)],
           [("piece", 4), ("kq", 0), ("piece", 5)],
           [("piece", 6), ("kq", 5), ("piece", 7)],
           [("piece", 8), ("kq", 4), ("piece", 9)],
           [("kq", 1), ("kq", 2), ("kq", 3)],
           [("kq", 6)]]
OUT_JOBS = JOBS_AT[0]
LAST_JOBS_AT = [[]] + [[("weight", i) for i in w] for w in ((0, 1, 2), (3, 4), (), (6, 7, 8), (9, 10), (11, 12), (13, 14))]
LAST_JOBS_AT[3] = [("mean", 0), ("mean", 1), ("weight", 5)]
PREP_JOBS = [j for jobs in JOBS_AT[1:] for j in jobs]
KQ_AT = {s: [j for j in PREP_JOBS if j[0] == "kq"].index(("kq", s)) for s in range(KQ_STEPS)}
KV_PIECES = [p for p in range(NP) if PIECES[p] not in ("q0", "q1")]
POOL_ORDER = [0, 1, "q00", "q01", 2, 3, "k", 4, 5, "q10", 6, 7, "q11", 8, 9]
ROPES = [e for e in POOL_ORDER if isinstance(e, str)]

def width(lt):
    return (CT + lt + 1) * P - LAST


def cols(lt, c):
    return BANK if c < CHUNKS - 1 else width(lt)


def build(nc, x, ctxT, wq, wk, wv, wo, wk_ctx, wv_ctx, q_norm, k_norm, w_gateT, w_upT, w_downT,
          WqT, WgT, bg, WkvT, WoT, routerT, w_lanes, e_gate, e_up, e_down,
          c_ident, c_mask, c_cos, c_sin, c_h256, c_blk, c_lower, out):
    main = ExitStack()
    with ExitStack() as ctx:
        def sb(name, shape, dt, at=ctx):
            return at.enter_context(nc.sbuf_tensor(name, shape, dt))

        def sem(name):
            return ctx.enter_context(nc.semaphore(name))

        PS = ctx.enter_context(nc.psum_tensor("PS", [P, 8, BANK], F32))
        SB, TB, OB, XB = 0, 4, 6, 7
        xs = sb("xs", [P, TILES * D], F32)
        R1 = sb("R1", [P, B, DC, 136], F32)
        ident = sb("ident", [P, P], F32)
        ident16 = sb("ident16", [P, P], F16)
        ones = sb("ones", [P, P], F32)
        mhalf = sb("mhalf", [P, TILES], F32)
        eps_ln = sb("eps_ln", [P, TILES], F32)
        eps_rms = sb("eps_rms", [P, TILES], F32)
        per_dh = sb("per_dh", [P, TILES], F32)
        lanes = sb("lanes", [3 * LANES, 1 + LANE_N], F32)
        lsum = sb("lsum", [1, 3 * LANES + 3], F32)
        stat = sb("stat", [P, TILES, 6], F32)
        mv = sb("mv", [P, TILES, 2], F32)
        rstd = sb("rstd", [P, TILES], F32)
        wmean = sb("wmean", [P, 4], F32)
        thr = sb("thr", [P, 8], F32)
        identb = sb("identb", [P, P], BF16)
        mask = sb("mask", [P, LT, width(1)], BF16)
        wcol = sb("wcol", [P, 1], F32)
        wo_h = sb("wo_h", [P, HEADS, D], F16)
        wo_l = sb("wo_l", [P, HEADS, D], F16)

        def sm(name, shape, dt):
            return sb(name, shape, dt, main)

        tab = sm("tab", [P, 4, LT, DH], F32)
        ctx_h = sm("ctx_h", [P, B, DC, SC], F16)
        ctx_l = sm("ctx_l", [P, B, DC, SC], F16)
        wc_h = sm("wc_h", [P, DC, KVH, 256], F16)
        wc_l = sm("wc_l", [P, DC, KVH, 256], F16)
        wsf_h = sm("wsf_h", [P, DC, KVH, 768], F16)
        wsf_l = sm("wsf_l", [P, DC, KVH, 768], F16)
        xT_h = sm("xT_h", [P, DC, TILES * P], F16)
        xT_l = sm("xT_l", [P, DC, TILES * P], F16)

        setup = ExitStack()
        w1_h = sb("w1_h", [P, DC, 512], F16, setup)
        w1_l = sb("w1_l", [P, DC, 512], F16, setup)
        blk = sb("blk", [P, 136], F32, setup)
        stage = [sb(f"stage{i}", [P, SC], F32, setup) for i in range(STAGES)]
        xn = sb("xn", [P, TILES * D], F32, setup)
        mask32 = sb("mask32", [P, LT, width(1)], F32, setup)
        nwb = sb("nwb", [P, 2, DH], F32, setup)
        cos = sb("cos", [P, LT, DH], F32, setup)
        sin = sb("sin", [P, LT, DH], F32, setup)
        k_s = sb("k_s", [P, 2, 256], F32, setup)
        ex_s = sb("ex_s", [P, 2, 256], F32, setup)
        kf_s = sb("kf_s", [P, 2, 256], F32, setup)
        vf_s = sb("vf_s", [P, 2, DC, 129], F32, setup)
        setup.close()

        kr = sm("kr", [P, KT_N, DH], F32)
        qr = sm("qr", [P, UNITS, DH], F32)
        sq = sm("sq", [P, 2, REP, DH], BF16)
        ss = sm("ss", [P, 2, REP], F32)
        rs = sm("rs", [P, REP], F32)
        rot = sm("rot", [P, 2, 2, DH], F32)
        kT_h = sm("kT_h", [P, 2, KEYS], F16)
        kT_l = sm("kT_l", [P, 2, KEYS], F16)
        qT_h = sm("qT_h", [P, 2, UNITS, P], F16)
        qT_l = sm("qT_l", [P, 2, UNITS, P], F16)
        v_h = sm("v_h", [P, 2, KT_N, DH + 1], F16)
        v_l = sm("v_l", [P, 2, KT_N, DH], F16)
        pr = sm("pr", [P, KEYS], F32)
        pT_h = sm("pT_h", [P, CHUNKS, BANK], F16)
        pT_l = sm("pT_l", [P, CHUNKS, BANK], F16)
        mx = sm("mx", [P, CHUNKS], F32)
        mr = sm("mr", [P, 1], F32)
        nb = sm("nb", [P, 2], F32)
        rden = sm("rden", [P, 1], F32)
        o_s = sm("o_s", [P, LT, REP, DH], F32)
        oT_h = sm("oT_h", [P, LT, BANK], F16)
        oT_l = sm("oT_l", [P, LT, BANK], F16)
        main.close()

        wg3 = sb("wg3", [P, DC, FF], F16)
        wu3 = sb("wu3", [P, DC, FF], F16)
        wd3 = sb("wd3", [P, FF // P, D], F16)
        wqg_h = sb("wqg_h", [P, 2, DC, D], F16)
        wqg_l = sb("wqg_l", [P, 2, DC, D], F16)
        wo1_h = sb("wo1_h", [P, DC, D], F16)
        wo1_l = sb("wo1_l", [P, DC, D], F16)
        rt_h = sb("rt_h", [P, DC, NE], F16)
        rt_l = sb("rt_l", [P, DC, NE], F16)
        eg_h = sb("eg_h", [P, 2, DC, NE * FI], F16)
        eg_l = sb("eg_l", [P, 2, DC, NE * FI], F16)
        ed_h = sb("ed_h", [P, NE, D], F16)
        ed_l = sb("ed_l", [P, NE, D], F16)
        H0 = sb("H0", [P, DC, D], F16)
        lower = sb("lower", [P, 4 * NE, NE], F32)
        bgs = sb("bgs", [1, D], F32)
        xn4 = sb("xn4", [P, 4, D], F32)
        xnT_h = sb("xnT_h", [P, DC, BANK], F16)
        xnT_l = sb("xnT_l", [P, DC, BANK], F16)
        am = sb("am", [P, 4, 4], F32)
        dq = sb("dq", [P, 4, 4], F32)
        qf = sb("qf", [P, 2, FF], F32)
        qi = sb("qi", [P, 4, FF], F16)
        qiT = sb("qiT", [P, 4, FF], F16)
        staging = ExitStack()
        tstage = [sb(f"tstage{i}", [P, 1024], F32, staging) for i in range(STAGES)]
        tern = sb("tern", [P, 1024], F32, staging)
        staging.close()
        sil = sb("sil", [P, 2, FF], F32)
        hh = sb("hh", [P, 4, FF], F32)
        hT_h = sb("hT_h", [P, 4, FF], F16)
        hT_l = sb("hT_l", [P, 4, FF], F16)
        sg = sb("sg", [P, 4, D], F32)
        z = sb("z", [P, 4, 16], F32)
        lg = sb("lg", [P, 4, NE], F32)
        pb = sb("pb", [P, 4, NE], F32)
        gt = sb("gt", [P, 4, NE * NE], F32)
        eq = sb("eq", [P, 4, NE * NE], F32)
        rk = sb("rk", [P, 4, NE], F32)
        r4 = sb("r4", [P, 4, 4], F32)

        in_const, in_x, in_out = sem("in_const"), sem("in_x"), sem("out_stored")
        in_w = [sem(f"in_w{i}") for i in range(STAGES)]
        set_hi, set_lo = sem("set_hi"), sem("set_lo")
        made_const = sem("made_const")
        ln_stat, ln_agg, ln_var, ln_rstd, ln_out, ln_tr, ln_hi, ln_lo = (
            sem(f"ln0_{n}") for n in ("stat", "agg", "var", "rstd", "out", "tr", "hi", "lo"))
        tab_made = sem("tab_made")
        l1_mm, l1_copy, l1_min, l1_v, l1_exp, l1_k, l1_sum, l1_R = (
            sem(f"l1_{n}") for n in ("mm", "copy", "min", "v", "exp", "k", "sum", "R"))
        pc_mm, pc_copy, pc_norm = (sem(f"pc_{n}") for n in ("mm", "copy", "norm"))
        pool_step, rope_done, rs_made = sem("pool_step"), sem("rope_done"), sem("rs_made")
        kq_tr, kq_hi, kq_lo, vs_hi, vs_lo = (sem(n) for n in ("kq_tr", "kq_hi", "kq_lo", "vs_hi", "vs_lo"))
        qk_done, mx_part, mx_all, nb_done, exp_done = (
            sem(n) for n in ("qk_done", "mx_part", "mx_all", "nb_done", "exp_done"))
        pt_tr, pt_hi, pt_lo, pv_done, rd_done, o_done = (
            sem(n) for n in ("pt_tr", "pt_hi", "pt_lo", "pv_done", "rd_done", "o_done"))
        ot_tr, ot_hi, ot_lo, oj_mm, x1_done = (sem(n) for n in ("ot_tr", "ot_hi", "ot_lo", "oj_mm", "x1_done"))
        dve_step, act_step = sem("dve_step"), sem("act_step")
        lane_in, lane_sum, lane_tr, lane_tot, lane_b = (
            sem(n) for n in ("lane_in", "lane_sum", "lane_tr", "lane_tot", "lane_b"))
        tw_in = [sem(f"tw_in{i}") for i in range(STAGES)]
        tw_const, tw_hi, tw_lo, tw_made = (sem(f"tw_{n}") for n in ("const", "hi", "lo", "made"))
        mean_out = sem("mean_out")
        tl = {n: [sem(f"t{n}{i}") for i in range(4)]
              for n in ("agg", "rstd", "norm", "tr", "hi", "lo")}
        fw_mm, fw_q, qt_tr, qt_ev = ([sem(f"{n}{i}") for i in range(2)]
                                     for n in ("fw_mm", "fw_q", "qt_tr", "qt_ev"))
        gu_mm, gu_silu, gu_h, ht_tr, ht_hi, ht_lo, dn_mm, dn_x = (
            [sem(f"{n}{i}") for i in range(2)]
            for n in ("gu_mm", "gu_silu", "gu_h", "ht_tr", "ht_hi", "ht_lo", "dn_mm", "dn_x"))
        lq_mm, lg_mm, lq_copy, lq_min, lq_exp, lq_f, lg_sig, la_mm, la_out, lo_mm, lo_x = (
            sem(n) for n in ("lq_mm", "lg_mm", "lq_copy", "lq_min", "lq_exp", "lq_f", "lg_sig",
                             "la_mm", "la_out", "lo_mm", "lo_x"))
        bf1, bf2, q_scale, q_round = sem("bf1"), sem("bf2"), sem("q_scale"), sem("q_round")
        rt_mm, rt_sub, rt_exp, rt_w = (sem(n) for n in ("rt_mm", "rt_sub", "rt_exp", "rt_w"))

        rows = lambda t: t.rearrange("(c p) n -> p c n", p=P)
        loads = []

        def st(n):
            return stage[len(loads) % STAGES][:, 0:n]

        loads.append(([(st(1024).rearrange("p (c n) -> p c n", c=DC), rows(WkvT))], 1024, WS,
                      w1_h[:, :, :].rearrange("p c n -> p (c n)"), w1_l[:, :, :].rearrange("p c n -> p (c n)")))

        def load_ctx(b):
            for c in range(DC):
                loads.append(([(st(SC), ctxT[b, c * P:(c + 1) * P, :])], SC, 1.0, ctx_h[:, b, c, :], ctx_l[:, b, c, :]))

        load_ctx(0)
        load_ctx(1)
        for c in range(DC):
            cv = st(1024).rearrange("p (h n) -> p h n", h=KVH)
            loads.append(([(cv[:, :, o:o + DH], w[c * P:(c + 1) * P, :].rearrange("p (h n) -> p h n", h=KVH))
                           for o, w in ((0, wk_ctx), (DH, wv_ctx))], 1024, WS,
                          wc_h[:, c, :, :].rearrange("p h n -> p (h n)"), wc_l[:, c, :, :].rearrange("p h n -> p (h n)")))
        for c in range(DC):
            load_ctx(2 + c)
            for h0 in range(0, KVH, 2):
                sv = st(1536).rearrange("p (h n) -> p h n", h=2)
                loads.append(([(sv[:, :, o:o + n],
                                w[c * P:(c + 1) * P, :].rearrange("p (h n) -> p h n", h=KVH)[:, h0:h0 + 2, :])
                               for o, n, w in ((0, 512, wq), (512, DH, wk), (640, DH, wv))], 1536, WS,
                              wsf_h[:, c, h0:h0 + 2, :].rearrange("p h n -> p (h n)"),
                              wsf_l[:, c, h0:h0 + 2, :].rearrange("p h n -> p (h n)")))
        for h0 in range(0, HEADS, 4):
            loads.append(([(st(1024).rearrange("p (h n) -> p h n", h=4),
                            wo[h0 * P:(h0 + 4) * P, :].rearrange("(h p) n -> p h n", p=P))], 1024, WS,
                          wo_h[:, h0:h0 + 4, :].rearrange("p h n -> p (h n)"),
                          wo_l[:, h0:h0 + 4, :].rearrange("p h n -> p (h n)")))
        NL = len(loads)
        FIRST = 1 + DC
        assert NL == FIRST + 4 * B
        load_count = [16 * sum(len(loads[j][0]) for j in range(i % STAGES, i + 1, STAGES)) for i in range(NL)]

        tloads = []

        def tst(i, n):
            return tstage[i % STAGES][:, 0:n]

        def tload(n, scale, hi, lo, *parts):
            at, sources = tst(len(tloads), n), []
            for k, w in enumerate(parts):
                m = n // len(parts)
                sources.append((at[:, m * k:m * k + m].rearrange("p (c n) -> p c n", c=w.shape[1]), w))
            tloads.append((sources, n, scale, hi, lo))

        kc = lambda t: t.rearrange("p c n -> p (c n)")
        tload(1024, WS, wqg_h[:, :, :, :].rearrange("p k c n -> p (k c n)"),
              wqg_l[:, :, :, :].rearrange("p k c n -> p (k c n)"), rows(WqT), rows(WgT))
        for k, w in enumerate((e_gate, e_up)):
            for c in range(DC):
                tload(1024, WS, eg_h[:, k, c, :], eg_l[:, k, c, :], rows(w)[:, c:c + 1, :])
        tload(512, WS, kc(wo1_h[:, :, :]), kc(wo1_l[:, :, :]), rows(WoT))
        for e in range(0, NE, 4):
            tload(1024, WS, kc(ed_h[:, e:e + 4, :]), kc(ed_l[:, e:e + 4, :]),
                  e_down[e:e + 4, :, :].rearrange("e p n -> p e n"))
        tload(16, WS, kc(rt_h[:, :, :]), kc(rt_l[:, :, :]), rows(routerT))
        NSPLIT = len(tloads)
        for t, w, m in ((wg3, w_gateT, 1), (wu3, w_upT, 1), (wd3, w_downT, 4)):
            for c in (0, m):
                tload(1024, None, kc(t[:, c:c + m, :]), None, rows(w)[:, c:c + m, :])
        NTL = len(tloads)
        tload_count = [16 * sum(len(tloads[j][0]) for j in range(i % STAGES, i + 1, STAGES)) for i in range(NTL)]
        NTERN = 3

        def flat(t):
            return t[:, :, :].rearrange("p a b -> p (a b)")

        def wait(eng, semaphore, value):
            if not isinstance(value, int) or value > 0:
                eng.wait_ge(semaphore, value)

        def l1_walk(eng, step, split, after=None):
            for b in range(B):
                n = b * CT
                step(n, b % 2, CREM)
                step(n + 1, (b + 1) % 2, P)
                if after and b:
                    after(b - 1)
                split(FIRST + 4 * b)
                with eng.Fori(0, 2) as i:
                    step(n + i * 2 + 2, b % 2, P)
                    step(n + i * 2 + 3, (b + 1) % 2, P)
                split(FIRST + 4 * b + 1)
                with eng.Fori(0, (CT - 9) // 2) as i:
                    step(n + i * 2 + 6, b % 2, P)
                    step(n + i * 2 + 7, (b + 1) % 2, P)
                split(FIRST + 4 * b + 2)
                step(n + CT - 3, b % 2, P)
                step(n + CT - 2, (b + 1) % 2, P)
                split(FIRST + 4 * b + 3)
                step(n + CT - 1, b % 2, P)
            if after:
                after(B - 1)

        def piece_slots(p):
            return {"q0": REP, "q1": REP, "self": LT, "rem": 1}.get(PIECES[p], 2)

        def piece_rows(p):
            kind = PIECES[p]
            if kind in ("q0", "q1"):
                lt = int(kind[1])
                return qr[:, lt * REP:(lt + 1) * REP, :]
            return kr[:, piece_tile(p):piece_tile(p) + piece_slots(p), :]

        def piece_tile(p):
            kind = PIECES[p]
            return {"self": CT, "rem": CT - 1}[kind] if isinstance(kind, str) else 2 * kind[1]

        def kq_view(s, kT, qT, par, bank):
            if s in (0, 6):
                lt = s // 6
                return qT[:, par, lt * REP:(lt + 1) * REP, :].rearrange("p h n -> p (h n)"), PS[:, bank, :], False
            if s == 4:
                return kT[:, par, (CT - 1) * P:SC], PS[:, bank, 0:CREM], True
            if s == 5:
                return kT[:, par, CT * P:KEYS], PS[:, bank, 0:LT * P], False
            return kT[:, par, (s - 1) * BANK:s * BANK], PS[:, bank, :], True

        PREP_BANKS = [XB, OB, TB, TB + 1]

        def prep_bank(n):
            return PREP_BANKS[(n - len(PREP_JOBS) + 1) % len(PREP_BANKS)]

        def rope_operands(r):
            if r == "k":
                return kr[:, CT:CT + LT, :], tab[:, 2, :, :], tab[:, 3, :, :]
            lt, j = int(r[1]), int(r[2])
            t = lt * REP + 2 * j
            return (qr[:, t:t + 2, :], *(tab[:, k, lt:lt + 1, :].broadcast_to([P, 2, DH]) for k in (0, 1)))

        def pieces_done(p, g):
            return g * NP + p + 1

        def kq_done(steps, g):
            return g * KQ_STEPS + max(KQ_AT[s] for s in steps) + 1

        def v_done(p, g):
            return g * len(KV_PIECES) + KV_PIECES.index(p) + 1

        def wait_bank(pe, job, g):
            kind, i = job
            if kind == "piece" and i in KV_PIECES:
                pe.wait_ge(vs_lo, v_done(i, g))
            elif kind == "piece":
                pe.wait_ge(pc_copy, pieces_done(i, g))
            elif kind == "kq":
                pe.wait_ge(kq_lo, kq_done([i], g))
            elif kind == "mean":
                pe.wait_ge(lane_tot if i == 0 else mean_out, 1)
            elif i == 2:
                pe.wait_ge(x1_done, g + 1)
            else:
                pe.wait_ge(ot_lo, g * 2 + i + 1)

        def groups(eng, group):
            group(0, 0, True, False)
            with eng.Fori(0, NG // 2 - 1) as i:
                group(2 * i + 1, 1, False, False)
                group(2 * i + 2, 0, False, False)
            group(NG - 1, (NG - 1) % 2, False, True)

        def jobs_of(u, first, last):
            if u == 0:
                return [] if first else OUT_JOBS
            return LAST_JOBS_AT[u] if last else JOBS_AT[u]

        def run_job(g, par, job, kinds):
            kind, i = job
            if kind in ("weight", "mean"):
                kinds[kind](i)
            elif kind == "out":
                kinds[kind](i, g - 1)
            else:
                kinds[kind](i, g + 1, 1 - par)

        GB = [4, 6, 0, 2]
        both = lambda j: j // 2 * 2 + 2
        FRONT = [(0, 1, 2, 3), (5, 7, 1, 3)]
        ps16 = lambda bank: PS[:, bank, :].bitcast(F16)

        def tail_pe(pe, three):
            mm = pe.matmul
            def normed(n, hf, banks=(0, 1)):
                for j in range(4):
                    pe.wait_ge(tl["norm"][n], hf * 4 + j + 1 if n < 3 else hf * 2 + j // 2 + 1)
                    for c in range(DC):
                        last = pe.transpose(PS[:, banks[j // 2], c * 2 * P + (j % 2) * P:c * 2 * P + (j % 2 + 1) * P],
                                            xn4[:, j, c * P:(c + 1) * P], ident[:, :])
                    if j % 2:
                        last.then_inc(tl["tr"][n], 1)

            def tok(j):
                return [(xnT_h[:, c, j * P:(j + 1) * P], xnT_l[:, c, j * P:(j + 1) * P]) for c in range(DC)]

            def gate_up(n, hf):
                for j in range(4):
                    if j >= 2:
                        pe.wait_ge(gu_h[n], hf * 4 + j - 1)
                    elif n == 0:
                        pe.wait_ge(qt_ev[0], hf * 2 + 2)
                        wait(pe, dn_x[1], hf * 4)
                    g0 = 4 - 4 * (j % 2)
                    for k in range(4):
                        o, w0 = PS[:, g0 + k, :], (k % 2) * BANK
                        for c in range(DC):
                            if n == 0:
                                w = (wg3, wu3)[k // 2]
                                last = mm(o, qiT[:, 0, c * BANK + j * P:c * BANK + (j + 1) * P],
                                          w[:, c, w0:w0 + BANK], start=c == 0, stop=c == DC - 1)
                            else:
                                last = three(o, tok(j)[c], (eg_h[:, k // 2, c, w0:w0 + BANK],
                                                            eg_l[:, k // 2, c, w0:w0 + BANK]), c == 0, c == DC - 1)
                    last.then_inc(gu_mm[n], 1)
                for j in range(4):
                    pe.wait_ge(gu_h[n], hf * 4 + max(j + 1, 3 if j < 2 else 4))
                    if n == 0:
                        pe.wait_ge(bf2, hf * 4 + j + 1)
                    for f in range(8):
                        last = pe.transpose(PS[:, GB[j] + f // 4, (f % 4) * P:(f % 4 + 1) * P],
                                            hh[:, j, f * P:(f + 1) * P], ident[:, :])
                    last.then_inc(ht_tr[n], 1)

            def rotate(hf):
                for j in range(4):
                    pe.wait_ge(tl["lo"][0], hf * 2 + j // 2 + 1)
                    for c in range(DC):
                        for w in range(2):
                            last = mm(PS[:, FRONT[hf][2 + j // 2], (j % 2) * D:(j % 2 + 1) * D], tok(j)[c][w],
                                      H0[:, c, :], start=c + w == 0, stop=c + w == DC)
                    last.then_inc(fw_mm[0], 1)

            def transpose_quantised(hf):
                pe.wait_ge(fw_q[0], hf + 1)
                for c in range(DC):
                    for j in range(4):
                        last = pe.transpose(ps16(FRONT[hf][c])[:, j * P:(j + 1) * P], qi[:, j, c * P:(c + 1) * P],
                                            ident16[:, :])
                    last.then_inc(qt_tr[0], 1)

            def rest(hf):
                gate_up(0, hf)
                for j in range(4):
                    pe.wait_ge(ht_lo[0], hf * 4 + j + 1)
                    for k in range(FF // D):
                        for c in range(DC):
                            f = k * DC + c
                            for w, t in enumerate((hT_h, hT_l)):
                                last = mm(PS[:, GB[j] + k // 2, (k % 2) * D:(k % 2 + 1) * D],
                                          t[:, j, f * P:(f + 1) * P], H0[:, c, :],
                                          start=c + w == 0, stop=c + w == DC)
                    last.then_inc(fw_mm[1], 1)
                for j in range(4):
                    pe.wait_ge(fw_q[1], hf * 4 + j + 1)
                    for f in range(8):
                        last = pe.transpose(ps16(GB[j])[:, f * P:(f + 1) * P], qi[:, j, f * P:(f + 1) * P], ident16[:, :])
                    last.then_inc(qt_tr[1], 1)
                for j in range(4):
                    pe.wait_ge(qt_ev[1], hf * 4 + j + 1)
                    for f in range(8):
                        last = mm(PS[:, GB[j] + 1, 0:D], qiT[:, j, f * P:(f + 1) * P], wd3[:, f, :],
                                  start=f == 0, stop=f == 7)
                    last.then_inc(dn_mm[0], 1)

                normed(1, hf)
                pe.wait_ge(tl["lo"][1], hf * 2 + 2)
                for k in range(DC):
                    for c in range(DC):
                        last = three(PS[:, 4 + k, :],
                                     (wqg_h[:, 0, c, k * P:(k + 1) * P], wqg_l[:, 0, c, k * P:(k + 1) * P]),
                                     (xnT_h[:, c, :], xnT_l[:, c, :]), c == 0, c == DC - 1)
                    last.then_inc(lq_mm, 1)
                for j in range(4):
                    o = PS[:, 2 + j // 2, (j % 2) * D:(j % 2 + 1) * D]
                    mm(o, ones[0:1, :], bgs[:, :], start=True, stop=False)
                    for c in range(DC):
                        last = three(o, tok(j)[c], (wqg_h[:, 1, c, :], wqg_l[:, 1, c, :]), False, c == DC - 1)
                    last.then_inc(lg_mm, 1)
                pe.wait_ge(lq_f, hf * 2 + 2)
                for j in range(4):
                    for k in range(DC):
                        last = mm(PS[:, (6, 7, 4, 5)[j], k * 136:(k + 1) * 136],
                                  hh[:, 0, k * BANK + j * P:k * BANK + (j + 1) * P],
                                  R1[:, ds(hf * 2 + j // 2, 1), k, :].rearrange("p a n -> p (a n)"),
                                  start=True, stop=True)
                    last.then_inc(la_mm, 1)
                normed(3, hf)
                for j in range(4):
                    pe.wait_ge(tl["lo"][3], hf * 2 + j // 2 + 1)
                    for c in range(DC):
                        last = three(PS[:, 2 + j // 2, (j % 2) * D:(j % 2 + 1) * D], tok(j)[c],
                                     (wo1_h[:, c, :], wo1_l[:, c, :]), c == 0, c == DC - 1)
                    last.then_inc(lo_mm, 1)

                normed(2, hf)
                for j in range(4):
                    pe.wait_ge(tl["lo"][2], hf * 2 + j // 2 + 1)
                    for c in range(DC):
                        last = three(PS[:, 4, j * NE:(j + 1) * NE], tok(j)[c], (rt_h[:, c, :], rt_l[:, c, :]),
                                     c == 0, c == DC - 1)
                last.then_inc(rt_mm, 1)
                pe.wait_ge(rt_sub, hf + 1)
                gate_up(1, hf)
                if hf == 0:
                    pe.wait_ge(ht_lo[1], 2)
                    normed(0, 1, FRONT[1])
                for j in range(4):
                    if j == 2 and hf == 0:
                        pe.wait_ge(ht_lo[1], 4)
                        rotate(1)
                    pe.wait_ge(ht_lo[1], hf * 4 + j + 1)
                    for f in range(NE):
                        last = three(PS[:, GB[j], 0:D], (hT_h[:, j, f * P:(f + 1) * P], hT_l[:, j, f * P:(f + 1) * P]),
                                     (ed_h[:, f, :], ed_l[:, f, :]), f == 0, f == NE - 1)
                    last.then_inc(dn_mm[1], 1)
                if hf == 0:
                    transpose_quantised(1)

            return normed, rotate, transpose_quantised, rest

        def tail_act(act, copy):
            def hi_part(n, hf, banks=(0, 1)):
                for t in range(2):
                    act.wait_ge(tl["tr"][n], hf * 2 + t + 1)
                    copy(xnT_h[:, :, t * 2 * P:(t + 1) * 2 * P], PS[:, banks[t], :].rearrange("p (c n) -> p c n", c=DC))\
                        .then_inc(tl["hi"][n], 1)

            def gate_up(n, hf):
                for j in range(4):
                    act.wait_ge(gu_mm[n], hf * 4 + j + 1)
                    if j >= 2:
                        act.wait_ge(gu_h[n], hf * 4 + j - 1)
                    g0 = 4 - 4 * (j % 2)
                    act.activation(sil[:, j % 2, :], PS[:, g0:g0 + 2, :].rearrange("p b n -> p (b n)"), ACT.Silu,
                                   scale=dq[:, 0, j:j + 1] if n == 0 else 1 / WS).then_inc(gu_silu[n], 1)
                for j in range(4):
                    act.wait_ge(ht_tr[n], hf * 4 + j + 1)
                    copy(hT_h[:, j, :], PS[:, GB[j]:GB[j] + 2, :].rearrange("p b n -> p (b n)"))\
                        .then_inc(ht_hi[n], 1)

            def copy_quantised(hf):
                for c in range(DC):
                    act.wait_ge(qt_tr[0], hf * 2 + c + 1)
                    copy(qiT[:, 0, c * BANK:(c + 1) * BANK], ps16(FRONT[hf][c])[:, 0:BANK]).then_inc(qt_ev[0], 1)

            def rest(hf):
                gate_up(0, hf)
                def round_scaled(j):
                    act.wait_ge(q_scale, hf + 1)
                    if j >= 2:
                        act.wait_ge(fw_q[1], hf * 4 + j - 1)
                    act.activation(qf[:, j % 2, :], PS[:, GB[j]:GB[j] + 2, :].rearrange("p b n -> p (b n)"), ACT.Copy,
                                   scale=am[:, 2, j:j + 1], bias=MAGIC).then_inc(q_round, 1)

                round_scaled(0)
                round_scaled(1)
                for j in range(4):
                    if j + 2 < 4:
                        round_scaled(j + 2)
                    act.wait_ge(qt_tr[1], hf * 4 + j + 1)
                    copy(qiT[:, j, :], ps16(GB[j])).then_inc(qt_ev[1], 1)
                hi_part(1, hf)
                for k in range(DC):
                    act.wait_ge(lq_mm, hf * 2 + k + 1)
                    copy(sil[:, 0, k * BANK:(k + 1) * BANK], PS[:, 4 + k, :], 1 / WS).then_inc(lq_copy, 1)
                for k in range(DC):
                    act.wait_ge(lq_min, hf * 2 + k + 1)
                    e = sil[:, 1, k * BANK:(k + 1) * BANK]
                    act.activation(e, e, ACT.Exp).then_inc(lq_exp, 1)
                for j in range(4):
                    act.wait_ge(lg_mm, hf * 4 + both(j))
                    act.activation(sg[:, j, :], PS[:, 2 + j // 2, (j % 2) * D:(j % 2 + 1) * D], ACT.Sigmoid,
                                   scale=1 / WS).then_inc(lg_sig, 1)
                hi_part(3, hf)
                hi_part(2, hf)
                act.wait_ge(rt_sub, hf + 1)
                act.activation(pb[:, :, :], lg[:, :, :], ACT.Exp).then_inc(rt_exp, 1)
                gate_up(1, hf)
                if hf == 0:
                    hi_part(0, 1, FRONT[1])
                    copy_quantised(1)

            return hi_part, copy_quantised, rest

        def tail_pool(pool):
            made = [1]
            for hf in range(2):
                for n in range(3):
                    if n == 1:
                        for j in range(4):
                            pool.wait_ge(gu_h[0], hf * 4 + j + 1)
                            if j >= 2:
                                pool.wait_ge(bf2, hf * 4 + j - 1)
                            a, o = (t.rearrange("p (h n) -> p h n", h=2) for t in (hh[:, j, :], qf[:, j % 2, :]))
                            pool.tensor_tensor(o[:, 0, :], a[:, 0, :], a[:, 1, :], ALU.add)
                            pool.tensor_tensor(o[:, 1, :], a[:, 0, :], a[:, 1, :], ALU.subtract).then_inc(bf1, 1)
                    for t in range(2):
                        at, made[0] = slice(2 * t, 2 * t + 2), made[0] + 1
                        pool.wait_ge(tl["agg"][n], hf * 2 + t + 1)
                        pool.tensor_tensor(rstd[:, at], mv[:, at, 1], eps_ln[:, at], ALU.add).then_inc(ln_var, 1)
                        pool.wait_ge(ln_var, made[0])
                        pool.tensor_tensor(rstd[:, at], rstd[:, at], mhalf[:, at], ALU.pow).then_inc(tl["rstd"][n], 1)

        def tail_dve(dve, link):
            def aggregate(n, pair):
                for j in (2 * pair, 2 * pair + 1):
                    ins = dve.bn_aggr(mv[:, j, :], stat[:, j, :])
                ins.then_inc(tl["agg"][n], 1)

            def first_stats(hf):
                for j in range(4):
                    ins = dve.bn_stats(stat[:, j, :], xs[:, ds(hf * 1024 + j * D, D)])
                link(ins)
                aggregate(0, 0)
                aggregate(0, 1)

            def norm_rows(n, hf):
                for j in range(4):
                    dve.wait_ge(tl["rstd"][n], hf * 2 + j // 2 + 1)
                    dve.tensor_scalar(xn4[:, j, :], xs[:, ds(hf * 1024 + j * D, D)], mv[:, j, 0:1],
                                      rstd[:, j:j + 1], ALU.subtract, ALU.mult).then_inc(tl["norm"][n], 1)

            def lo_part(n, hf, banks=(0, 1)):
                for t in range(2):
                    dve.wait_ge(tl["hi"][n], hf * 2 + t + 1)
                    at = slice(t * 2 * P, (t + 1) * 2 * P)
                    dve.tensor_tensor(xnT_l[:, :, at], PS[:, banks[t], :].rearrange("p (c n) -> p c n", c=DC),
                                      xnT_h[:, :, at], ALU.subtract).then_inc(tl["lo"][n], 1)

            def h_lo(n, hf):
                for j in range(4):
                    dve.wait_ge(ht_hi[n], hf * 4 + j + 1)
                    dve.tensor_tensor(hT_l[:, j, :], PS[:, GB[j]:GB[j] + 2, :].rearrange("p b n -> p (b n)"),
                                      hT_h[:, j, :], ALU.subtract).then_inc(ht_lo[n], 1)

            def quant_scales(weights, made=None):
                link(dve.tensor_scalar(am[:, 0, :], am[:, 0, :], EPS_Q, None, ALU.max))
                link(dve.reciprocal(am[:, 1, :], am[:, 0, :]))
                for k, (w, f) in enumerate(weights):
                    dve.tensor_scalar(dq[:, k, :], am[:, 0, :], wmean[:, w:w + 1], f / 127.0, ALU.mult, ALU.mult)
                ins = dve.tensor_scalar(am[:, 2, :], am[:, 1, :], 127.0, None, ALU.mult)
                if made:
                    ins.then_inc(made, 1)
                else:
                    link(ins)

            def add_to_x(hf, o, j, scale, done_sem):
                at = xs[:, ds(hf * 1024 + j * D, D)]
                dve.scalar_tensor_tensor(at, o, scale, at, ALU.mult, ALU.add).then_inc(done_sem, 1)

            def stats(hf, j, done_sem, n):
                dve.wait_ge(done_sem, hf * 4 + j + 1)
                ins = dve.bn_stats(stat[:, j, :], xs[:, ds(hf * 1024 + j * D, D)])
                if j % 2:
                    link(ins)
                    aggregate(n, j // 2)

            def quantise(hf):
                for j in range(4):
                    dve.wait_ge(fw_mm[0], hf * 4 + both(j))
                    ins = dve.tensor_reduce(am[:, 0, j:j + 1], PS[:, FRONT[hf][2 + j // 2], (j % 2) * D:(j % 2 + 1) * D], AX_X,
                                            ALU.max, apply_absolute_value=True)
                link(ins)
                quant_scales(((0, 1.0), (1, 0.5)))
                for j in range(4):
                    ins = dve.tensor_scalar(qf[:, 0, j * D:(j + 1) * D], PS[:, FRONT[hf][2 + j // 2], (j % 2) * D:(j % 2 + 1) * D],
                                            am[:, 2, j:j + 1], MAGIC, ALU.mult, ALU.add)
                link(ins)
                dve.tensor_scalar(qi[:, :, 0:D], qf[:, 0, :].rearrange("p (j n) -> p j n", j=4), MAGIC, 127.0,
                                  ALU.subtract, ALU.min).then_inc(fw_q[0], 1)

            def rest(hf):
                def butterfly(j):
                    dve.wait_ge(bf1, hf * 4 + j + 1)
                    a, o = (t.rearrange("p (h q n) -> p h q n", h=2, q=2) for t in (qf[:, j % 2, :], hh[:, j, :]))
                    dve.tensor_tensor(o[:, :, 0, :], a[:, :, 0, :], a[:, :, 1, :], ALU.add)
                    dve.tensor_tensor(o[:, :, 1, :], a[:, :, 0, :], a[:, :, 1, :], ALU.subtract).then_inc(bf2, 1)

                for j in range(4):
                    dve.wait_ge(gu_silu[0], hf * 4 + j + 1)
                    g0 = 4 - 4 * (j % 2)
                    dve.scalar_tensor_tensor(hh[:, j, :], PS[:, g0 + 2:g0 + 4, :].rearrange("p b n -> p (b n)"),
                                             dq[:, 1, j:j + 1], sil[:, j % 2, :], ALU.mult, ALU.mult)\
                       .then_inc(gu_h[0], 1)
                    if j:
                        butterfly(j - 1)
                butterfly(3)
                h_lo(0, hf)
                for j in range(4):
                    dve.wait_ge(fw_mm[1], hf * 4 + j + 1)
                    y = PS[:, GB[j]:GB[j] + 2, :].rearrange("p b n -> p (b n)")
                    ins = dve.tensor_reduce(am[:, 0, j:j + 1], y, AX_X, ALU.max, apply_absolute_value=True)
                link(ins)
                quant_scales(((2, 1.0),), q_scale)
                for j in range(4):
                    dve.wait_ge(q_round, hf * 4 + j + 1)
                    dve.tensor_scalar(qi[:, j, :], qf[:, j % 2, :], MAGIC, 127.0, ALU.subtract, ALU.min)\
                       .then_inc(fw_q[1], 1)
                for j in range(4):
                    dve.wait_ge(dn_mm[0], hf * 4 + j + 1)
                    add_to_x(hf, PS[:, GB[j] + 1, 0:D], j, dq[:, 0, j:j + 1], dn_x[0])
                    if j:
                        stats(hf, j - 1, dn_x[0], 1)
                stats(hf, 3, dn_x[0], 1)

                norm_rows(1, hf)
                lo_part(1, hf)
                for k in range(DC):
                    dve.wait_ge(lq_copy, hf * 2 + k + 1)
                    dve.tensor_scalar_min(sil[:, 1, k * BANK:(k + 1) * BANK], sil[:, 0, k * BANK:(k + 1) * BANK], 0.0)\
                       .then_inc(lq_min, 1)
                for k in range(DC):
                    dve.wait_ge(lq_exp, hf * 2 + k + 1)
                    dve.scalar_tensor_tensor(hh[:, 0, k * BANK:(k + 1) * BANK], sil[:, 0, k * BANK:(k + 1) * BANK], 0.0,
                                             sil[:, 1, k * BANK:(k + 1) * BANK], ALU.max, ALU.add).then_inc(lq_f, 1)
                heads = lambda j: PS[:, (6, 7, 4, 5)[j], 0:2 * 136].rearrange("p (k n) -> p k n", k=DC)
                for j in range(4):
                    dve.wait_ge(la_mm, hf * 4 + j + 1)
                    ins = dve.tensor_scalar(z[:, j, :].rearrange("p (k h) -> p k h", k=DC), heads(j)[:, :, P:136],
                                            EPS_Z, None, ALU.add)
                link(ins)
                link(dve.reciprocal(z[:, :, :], z[:, :, :]))
                for j in range(4):
                    for k in range(DC):
                        ins = dve.tensor_tensor(
                            xn4[:, j, k * P:(k + 1) * P].rearrange("p (h e) -> p h e", h=8),
                            heads(j)[:, k, 0:P].rearrange("p (h e) -> p h e", h=8),
                            z[:, j, k * 8:(k + 1) * 8].unsqueeze(2).broadcast_to([P, 8, 16]), ALU.mult)
                link(ins)
                for t in range(2):
                    dve.wait_ge(lg_sig, hf * 4 + 2 * t + 2)
                    at = slice(2 * t, 2 * t + 2)
                    dve.tensor_tensor(xn4[:, at, :], xn4[:, at, :], sg[:, at, :], ALU.mult).then_inc(tl["norm"][3], 1)
                lo_part(3, hf)
                for j in range(4):
                    dve.wait_ge(lo_mm, hf * 4 + both(j))
                    add_to_x(hf, PS[:, 2 + j // 2, (j % 2) * D:(j % 2 + 1) * D], j, 1 / WS, lo_x)
                    if j:
                        stats(hf, j - 1, lo_x, 2)
                stats(hf, 3, lo_x, 2)

                norm_rows(2, hf)
                lo_part(2, hf)
                dve.wait_ge(rt_mm, hf + 1)
                link(dve.tensor_scalar(flat(lg), PS[:, 4, 0:4 * NE], 1 / WS, None, ALU.mult))
                link(dve.reduce_max(r4[:, 0, :], lg[:, :, :], AX_X))
                over = lambda r: r.unsqueeze(2).broadcast_to([P, 4, NE])
                dve.tensor_tensor(lg[:, :, :], lg[:, :, :], over(r4[:, 0, :]), ALU.subtract).then_inc(rt_sub, 1)
                dve.wait_ge(rt_exp, hf + 1)
                link(dve.reduce_sum(r4[:, 1, :], pb[:, :, :], AX_X))
                link(dve.reciprocal(r4[:, 2, :], r4[:, 1, :]))
                link(dve.tensor_tensor(pb[:, :, :], pb[:, :, :], over(r4[:, 2, :]), ALU.mult))
                pe_ = flat(pb).unsqueeze(2).broadcast_to([P, 4 * NE, NE])
                pj_ = pb[:, :, :].unsqueeze(2).broadcast_to([P, 4, NE, NE])
                g4 = lambda t: t[:, :, :].rearrange("p t (e j) -> p t e j", e=NE)
                pe4 = pb[:, :, :].unsqueeze(3).broadcast_to([P, 4, NE, NE])
                dve.tensor_tensor(g4(gt), pj_, pe4, ALU.is_gt)
                link(dve.tensor_tensor(g4(eq), pj_, pe4, ALU.is_equal))
                link(dve.tensor_tensor(flat(eq), flat(eq), flat(lower), ALU.mult))
                link(dve.tensor_tensor(flat(gt), flat(gt), flat(eq), ALU.add))
                link(dve.reduce_sum(flat(rk), flat(gt).rearrange("p (a j) -> p a j", j=NE), AX_X))
                link(dve.scalar_tensor_tensor(flat(rk), flat(rk), 1.5, flat(pb), ALU.is_lt, ALU.mult))
                link(dve.reduce_sum(r4[:, 1, :], rk[:, :, :], AX_X))
                link(dve.reciprocal(r4[:, 2, :], r4[:, 1, :]))
                dve.scalar_tensor_tensor(pb[:, :, :], rk[:, :, :], 1 / WS, over(r4[:, 2, :]), ALU.mult, ALU.mult)\
                   .then_inc(rt_w, 1)
                if hf == 0:
                    first_stats(1)
                    norm_rows(0, 1)
                dve.wait_ge(rt_w, hf + 1)
                for j in range(4):
                    dve.wait_ge(gu_silu[1], hf * 4 + j + 1)
                    g0 = 4 - 4 * (j % 2)
                    up = PS[:, g0 + 2:g0 + 4, :].rearrange("p b n -> p (b n)")
                    for e in range(NE):
                        ins = dve.scalar_tensor_tensor(hh[:, j, e * P:(e + 1) * P], up[:, e * P:(e + 1) * P],
                                                       pb[:, j, e:e + 1], sil[:, j % 2, e * P:(e + 1) * P],
                                                       ALU.mult, ALU.mult)
                    ins.then_inc(gu_h[1], 1)
                h_lo(1, hf)
                if hf == 0:
                    lo_part(0, 1, FRONT[1])
                for j in range(4):
                    if j == 2 and hf == 0:
                        quantise(1)
                    dve.wait_ge(dn_mm[1], hf * 4 + j + 1)
                    add_to_x(hf, PS[:, GB[j], 0:D], j, 1 / WS, dn_x[1])

            return first_stats, norm_rows, lo_part, quantise, rest

        block = ctx.enter_context(nc.Block())

        @block.sync
        def _(sp):
            sp.dma_start(ident[:, :], c_ident).then_inc(in_const, 16)
            sp.dma_start(xs[:, :].rearrange("p (t d) -> p t d", t=TILES),
                         x.rearrange("(t p) d -> p t d", p=P)).then_inc(in_x, 16)
            for i, (parts, n, scale, hi, lo) in enumerate(loads):
                if i >= STAGES:
                    sp.wait_ge(set_lo, i - STAGES + 1)
                for dst, src in parts:
                    sp.dma_start(dst, src).then_inc(in_w[i % STAGES], 16)
                if i == FIRST:
                    for dst, src in ((mask32[:, :, :], c_mask), (cos[:, :, :], c_cos),
                                     (sin[:, :, :], c_sin), (blk[:, :], c_blk),
                                     (nwb[:, 0, :], q_norm.partition_broadcast(P)),
                                     (nwb[:, 1, :], k_norm.partition_broadcast(P)),
                                     (wcol[:, :], k_norm.rearrange("(p a) -> p a", a=1))):
                        sp.dma_start(dst, src).then_inc(in_const, 16)
            sp.dma_start(lanes[:, 1:], w_lanes[:, 0:LANE_N]).then_inc(lane_in, 16)
            with sp.Fori(1, NG) as g:
                sp.wait_ge(lane_sum, g)
                sp.dma_start(lanes[:, 1:], w_lanes[:, ds(g * LANE_N, LANE_N)]).then_inc(lane_in, 16)
            sp.wait_ge(kq_lo, NG * KQ_STEPS)
            for i, (parts, n, scale, hi, lo) in enumerate(tloads):
                if i >= STAGES:
                    sp.wait_ge(tw_lo, i - STAGES + 1)
                for dst, src in parts:
                    sp.dma_start(dst, src).then_inc(tw_in[i % STAGES], 16)
                if i == 1:
                    for dst, src in ((H0[:, :, :], c_h256), (lower[:, :, :], c_lower),
                                     (bgs[:, :], bg.rearrange("(a n) -> a n", a=1))):
                        sp.dma_start(dst, src).then_inc(tw_const, 16)
            outv = out.rearrange("(t p) d -> p t d", p=P)
            for hf in range(2):
                sp.wait_ge(dn_x[1], 4 * hf + 4)
                sp.dma_start(outv[:, 4 * hf:4 * hf + 4, :],
                             xs[:, hf * 1024:hf * 1024 + 1024].rearrange("p (t d) -> p t d", t=4)).then_inc(in_out, 16)
            sp.wait_ge(in_out, 32)

        @block.tensor
        def _(pe):
            mm = pe.matmul

            def three(o, lhs, rhs, start, stop):
                (ah, al), (bh, bl) = lhs, rhs
                mm(o, ah, bh, start=start, stop=False)
                mm(o, ah, bl, start=False, stop=False)
                return mm(o, al, bh, start=False, stop=stop)

            pe.wait_ge(in_const, 16)
            for k in range(4):
                c, half = k // 2, k % 2
                pe.wait_ge(ln_out, 4 * half + 4)
                for j in range(4):
                    t = 4 * half + j
                    last = pe.transpose(PS[:, TB + k % 2 if k < 2 else OB + k % 2, j * P:(j + 1) * P],
                                        xn[:, t * D + c * P:t * D + (c + 1) * P], ident[:, :])
                last.then_inc(ln_tr, 1)

            def l1_proj(b, n, par, nrows, col):
                wait(pe, l1_v, n - 1)
                for c in range(DC):
                    last = three(PS[0:nrows, SB + par, :],
                                 (ctx_h[:, b, c, ds(col, nrows)], ctx_l[:, b, c, ds(col, nrows)]),
                                 (w1_h[:, c, :], w1_l[:, c, :]), c == 0, c == DC - 1)
                last.then_inc(l1_mm, 1)

            def l1_summary(b, n, par, nrows, first, final):
                pe.wait_ge(l1_k, n + 1)
                for c in range(DC):
                    last = mm(PS[:, (TB, OB)[b % 2] + c, 0:129], kf_s[0:nrows, par, c * P:(c + 1) * P],
                              vf_s[0:nrows, par, c, :], start=first, stop=final)
                last.then_inc(l1_sum, 1)

            def l1_last(b, t):
                l1_summary(b, b * CT + t, (b + t) % 2, P, False, t == CT - 1)

            pe.wait_ge(ln_lo, 4)
            for b in range(B):
                n = b * CT
                p0, p1 = b % 2, (b + 1) % 2
                pe.wait_ge(set_lo, FIRST if b == 0 else FIRST + 4 * (b - 1) + 2)
                l1_proj(b, n, p0, CREM, (CT - 1) * P)
                if b:
                    l1_last(b - 1, CT - 2)
                l1_proj(b, n + 1, p1, P, 0)
                if b:
                    l1_last(b - 1, CT - 1)
                l1_proj(b, n + 2, p0, P, P)
                wait(pe, l1_R, b - 1)
                l1_summary(b, n, p0, CREM, True, False)
                with pe.Fori(0, (CT - 3) // 2) as i:
                    l1_proj(b, n + i * 2 + 3, p1, P, i * (2 * P) + 2 * P)
                    l1_summary(b, n + i * 2 + 1, p1, P, False, False)
                    l1_proj(b, n + i * 2 + 4, p0, P, i * (2 * P) + 3 * P)
                    l1_summary(b, n + i * 2 + 2, p0, P, False, False)
            l1_last(B - 1, CT - 2)
            l1_last(B - 1, CT - 1)

            def piece(p, g, par, bank=XB):
                b, kv = g // KVH, g % KVH
                kind = PIECES[p]
                if kind in ("q0", "q1"):
                    lt = int(kind[1])
                    jobs = [(PS[:, bank, :], xT_h, xT_l, (b * L + lt * P), P, wsf_h, wsf_l, 0, 512)]
                elif kind == "self":
                    jobs = [(PS[:, bank, lt * 256:lt * 256 + 256], xT_h, xT_l, (b * L + lt * P), P, wsf_h, wsf_l, 512, 256)
                            for lt in range(LT)]
                elif kind == "rem":
                    jobs = [(PS[0:CREM, bank, 0:256], None, None, (CT - 1) * P, CREM, wc_h, wc_l, 0, 256)]
                else:
                    jobs = [(PS[:, bank, j * 256:j * 256 + 256], None, None, (2 * kind[1] + j) * P, P, wc_h, wc_l, 0, 256)
                            for j in range(2)]
                for o, ah, al, col, n, bh, bl, w0, wn in jobs:
                    for c in range(DC):
                        if ah is None:
                            lhs = (ctx_h[:, b, c, col:col + n], ctx_l[:, b, c, col:col + n])
                        else:
                            lhs = (ah[:, c, ds(col, n)], al[:, c, ds(col, n)])
                        last = three(o, lhs, (bh[:, c, kv, w0:w0 + wn], bl[:, c, kv, w0:w0 + wn]),
                                     c == 0, c == DC - 1)
                last.then_inc(pc_mm, 1)

            def transpose_kq(s, g, par, bank=XB):
                if s in (0, 6):
                    lt = s // 6
                    pe.wait_ge(rope_done, g * len(ROPES) + ROPES.index(f"q{lt}1") + 1)
                    for j in range(REP):
                        last = pe.transpose(PS[:, bank, j * P:(j + 1) * P], qr[:, lt * REP + j, :], ident[:, :])
                elif s == 4:
                    pe.wait_ge(pc_norm, pieces_done(3, g))
                    last = pe.transpose(PS[:, bank, 0:CREM], kr[0:CREM, CT - 1, :], ident[0:CREM, 0:CREM])
                elif s == 5:
                    pe.wait_ge(rope_done, g * len(ROPES) + ROPES.index("k") + 1)
                    for j in range(LT):
                        last = pe.transpose(PS[:, bank, j * P:(j + 1) * P], kr[:, CT + j, :], ident[:, :])
                else:
                    pe.wait_ge(pc_norm, pieces_done(3 + 2 * s, g))
                    for j in range(4):
                        last = pe.transpose(PS[:, bank, j * P:(j + 1) * P], kr[:, 4 * (s - 1) + j, :], ident[:, :])
                last.then_inc(kq_tr, 1)

            def out_proj(i, g):
                kv = g % KVH
                if i < LT:
                    pe.wait_ge(o_done, (g + 1) * UNITS)
                    for h in range(REP):
                        last = pe.transpose(PS[:, XB, h * P:(h + 1) * P], o_s[:, i, h, :], ident[:, :])
                    last.then_inc(ot_tr, 1)
                    return
                for lt in range(LT):
                    for h in range(REP):
                        last = three(PS[:, XB, lt * D:(lt + 1) * D],
                                     (oT_h[:, lt, h * P:(h + 1) * P], oT_l[:, lt, h * P:(h + 1) * P]),
                                     (wo_h[:, ds(kv * REP + h, 1), :].rearrange("p a n -> p (a n)"),
                                      wo_l[:, ds(kv * REP + h, 1), :].rearrange("p a n -> p (a n)")),
                                     h == 0, h == REP - 1)
                last.then_inc(oj_mm, 1)

            def qk(u, c, g, par):
                h, lt = u // LT, u % LT
                wait(pe, exp_done, g * (UNITS * CHUNKS) + (u - 1) * CHUNKS + c + 1)
                if u == 0:
                    pe.wait_ge(kq_lo, kq_done([[0, 1], [2], [3], [4, 5]][c], g))
                if u == 1 and c == 0:
                    pe.wait_ge(kq_lo, kq_done([6], g))
                n = cols(lt, c)
                o = PS[:, SB + c, 0:n]
                qs = lt * REP + h
                if c == CHUNKS - 1:
                    mm(o, identb[:, :], mask[:, lt, 0:n], start=True, stop=False)
                three(o, (qT_h[:, par, qs, :], qT_l[:, par, qs, :]),
                      (kT_h[:, par, c * BANK:c * BANK + n], kT_l[:, par, c * BANK:c * BANK + n]),
                      c < CHUNKS - 1, True).then_inc(qk_done, 1)

            def transpose_p(u, c, g):
                n = g * (UNITS * CHUNKS) + u * CHUNKS + c
                pe.wait_ge(exp_done, n + 1)
                wait(pe, pt_lo, n - 1)
                for j in range(cols(u % LT, c) // P):
                    last = pe.transpose(PS[:, TB + c % 2, j * P:(j + 1) * P],
                                        pr[:, c * BANK + j * P:c * BANK + (j + 1) * P], ident[:, :])
                last.then_inc(pt_tr, 1)

            def pv(u, c, g, par):
                n = g * (UNITS * CHUNKS) + u * CHUNKS + c
                pe.wait_ge(pt_lo, n + 1)
                if c == 0:
                    if u == 0:
                        pe.wait_ge(vs_lo, v_done(NP - 1, g))
                    wait(pe, o_done, g * UNITS + u)
                tiles = cols(u % LT, c) // P
                for j in range(tiles):
                    t = c * 4 + j
                    first, final = c == 0 and j == 0, c == CHUNKS - 1 and j == tiles - 1
                    ph, pl = pT_h[:, c, j * P:(j + 1) * P], pT_l[:, c, j * P:(j + 1) * P]
                    mm(PS[:, OB, 0:DH + 1], ph, v_h[:, par, t, :], start=first, stop=False)
                    mm(PS[:, OB, 0:DH], ph, v_l[:, par, t, :], start=False, stop=False)
                    last = mm(PS[:, OB, 0:DH + 1], pl, v_h[:, par, t, :], start=False, stop=final)
                if c == CHUNKS - 1:
                    last.then_inc(pv_done, 1)

            def mean(i):
                if i == 0:
                    pe.wait_ge(lane_sum, NG)
                    pe.transpose(PS[0:1, XB, 0:3 * LANES], lanes[:, 0:1], ident[0:3 * LANES, 0:3 * LANES])\
                      .then_inc(lane_tr, 1)
                else:
                    mm(PS[:, XB, 0:NTERN], ones[0:1, :], lsum[:, 3 * LANES:], start=True, stop=True).then_inc(lane_b, 1)

            kinds = {"out": out_proj, "piece": piece, "kq": transpose_kq, "mean": mean}
            normed, rotate, transpose_quantised, rest = tail_pe(pe, three)

            def group(g, par, first, last):
                before = [(PREP_JOBS[-1], g)]
                for u in range(UNITS):
                    todo = list(jobs_of(u, first, last))

                    def job():
                        if todo and todo[0][0] == "weight":
                            todo.pop(0)
                        elif todo:
                            wait_bank(pe, *before[0])
                            before[0] = (todo[0], g - 1 if todo[0][0] == "out" else g + 1)
                            run_job(g, par, todo.pop(0), kinds)

                    for c in range(CHUNKS):
                        transpose_p(u, c, g)
                        if u + 1 < UNITS:
                            qk(u + 1, c, g, par)
                        elif not last:
                            qk(0, c, g + 1, 1 - par)
                        if c == 1:
                            job()
                    if last and u == UNITS - 1:
                        normed(0, 0)
                    job()
                    pv(u, 0, g, par)
                    pv(u, 1, g, par)
                    pv(u, 2, g, par)
                    pv(u, 3, g, par)
                    job()

            pe.wait_ge(set_lo, NL)
            pe.wait_ge(made_const, 2)
            pe.wait_ge(l1_R, B)
            for n, (kind, i) in enumerate(PREP_JOBS):
                if n >= len(PREP_BANKS):
                    wait_bank(pe, PREP_JOBS[n - len(PREP_BANKS)], 0)
                kinds[kind](i, 0, 0, prep_bank(n))
            for c in range(CHUNKS):
                qk(0, c, 0, 0)
            groups(pe, group)
            pe.wait_ge(tw_const, 48)
            pe.wait_ge(tw_lo, NTL)
            pe.wait_ge(tw_made, 1)
            for n, (kind, i) in enumerate(OUT_JOBS):
                wait_bank(pe, OUT_JOBS[n - 1] if n else ("mean", 1), NG - 1)
                kinds[kind](i, NG - 1)
                if n == 1:
                    rotate(0)
            transpose_quantised(0)
            pe.wait_ge(x1_done, NG)
            for hf in range(2):
                rest(hf)

        @block.scalar
        def _(act):
            copy = lambda o, i, scale=1.0: act.activation(o, i, ACT.Copy, scale=scale)

            def set_hi_part(i):
                parts, n, scale, hi, lo = loads[i]
                act.wait_ge(in_w[i % STAGES], load_count[i])
                copy(hi, stage[i % STAGES][:, 0:n], scale).then_inc(set_hi, 1)

            for k in range(4):
                c, half = k // 2, k % 2
                if k == 0:
                    set_hi_part(0)
                act.wait_ge(ln_tr, k + 1)
                copy(xT_h[:, c, half * BANK:(half + 1) * BANK],
                     PS[:, TB + k % 2 if k < 2 else OB + k % 2, :]).then_inc(ln_hi, 1)
            for i in range(1, FIRST):
                set_hi_part(i)

            def l1_step(n, par, nrows):
                act.wait_ge(l1_mm, n + 1)
                wait(act, l1_k, n - 1)
                copy(k_s[0:nrows, par, :], PS[0:nrows, SB + par, 0:256], 1 / WS).then_inc(l1_copy, 1)
                act.wait_ge(l1_min, n + 1)
                act.activation(ex_s[0:nrows, par, :], ex_s[0:nrows, par, :], ACT.Exp).then_inc(l1_exp, 1)

            act.wait_ge(made_const, 1)
            l1_walk(act, l1_step, set_hi_part)

            def piece_out(p, g, par, bank=XB):
                kind = PIECES[p]
                q = kind in ("q0", "q1")
                wait(act, pc_norm, pieces_done(p, g) - 2)
                act.wait_ge(pc_mm, pieces_done(p, g))
                rows, w = (CREM if kind == "rem" else P), (DH if q else 2 * DH)
                for j in range(piece_slots(p)):
                    act.activation(sq[0:rows, p % 2, j, :], PS[0:rows, bank, j * w:j * w + DH], ACT.Square,
                                   scale=1 / WS, accum_out=ss[0:rows, p % 2, j:j + 1])
                v = PS[0:rows, bank, 0:piece_slots(p) * w].rearrange("p (t d) -> p t d", d=w)
                copy(piece_rows(p)[0:rows, :, :], v[:, :, 0:DH], 1 / WS).then_inc(pc_copy, 1)
                if not q:
                    t = piece_tile(p)
                    copy(v_h[0:rows, par, t:t + piece_slots(p), 0:DH], v[:, :, DH:], 1 / WS).then_inc(vs_hi, 1)

            def kq_hi_part(s, g, par, bank=XB):
                act.wait_ge(kq_tr, kq_done([s], g))
                o, i, w = kq_view(s, kT_h, qT_h, par, bank)
                act.activation(o, i, ACT.Copy, scale=wcol[:, 0:1] if w else 1.0).then_inc(kq_hi, 1)

            def exp(u, c, g):
                n = g * (UNITS * CHUNKS) + u * CHUNKS + c
                if c == 0:
                    act.wait_ge(nb_done, g * UNITS + u + 1)
                w = cols(u % LT, c)
                act.activation(pr[:, c * BANK:c * BANK + w], PS[:, SB + c, 0:w], ACT.Exp,
                               bias=nb[:, u % 2:u % 2 + 1], scale=SCALE).then_inc(exp_done, 1)

            def p_hi(u, c, g):
                act.wait_ge(pt_tr, g * (UNITS * CHUNKS) + u * CHUNKS + c + 1)
                w = cols(u % LT, c)
                copy(pT_h[:, c, 0:w], PS[:, TB + c % 2, 0:w]).then_inc(pt_hi, 1)

            def out_hi_part(i, g):
                if i < LT:
                    wait(act, oj_mm, g)
                    act.wait_ge(ot_tr, g * 2 + i + 1)
                    copy(oT_h[:, i, :], PS[:, XB, :]).then_inc(ot_hi, 1)

            def weight_hi_part(i):
                parts, n, scale, hi, lo = tloads[i]
                if i < NSPLIT:
                    act.wait_ge(tw_in[i % STAGES], tload_count[i])
                    copy(hi, tst(i, n), scale).then_inc(tw_hi, 1)
                    act.wait_ge(tw_hi, 2 * i + 1)
                    copy(tst(i, n), tst(i, n), scale).then_inc(tw_hi, 1)

            kinds = {"out": out_hi_part, "piece": piece_out, "kq": kq_hi_part,
                     "weight": weight_hi_part, "mean": lambda i: None}

            def group(g, par, first, last):
                for u in range(UNITS):
                    todo = list(jobs_of(u, first, last))

                    def job():
                        if todo:
                            run_job(g, par, todo.pop(0), kinds)

                    p_hi(u, 0, g)
                    exp(u, 2, g)
                    p_hi(u, 1, g)
                    exp(u, 3, g)
                    job()
                    p_hi(u, 2, g)
                    p_hi(u, 3, g)
                    job()
                    if u + 1 < UNITS or not last:
                        nu, ng = ((u + 1, g) if u + 1 < UNITS else (0, g + 1))
                        exp(nu, 0, ng)
                        exp(nu, 1, ng)
                    job()

            act.wait_ge(made_const, 2)
            for n, (kind, i) in enumerate(PREP_JOBS):
                kinds[kind](i, 0, 0, prep_bank(n))
            exp(0, 0, 0)
            exp(0, 1, 0)
            hi_part, copy_quantised, rest = tail_act(act, copy)
            groups(act, group)
            hi_part(0, 0)
            for kind, i in OUT_JOBS:
                kinds[kind](i, NG - 1)
            copy_quantised(0)
            act.wait_ge(x1_done, NG)
            for hf in range(2):
                rest(hf)

        @block.vector
        def _(dve):
            steps = [0]

            def link(ins):
                steps[0] += 1
                ins.then_inc(dve_step, 1)
                dve.wait_ge(dve_step, steps[0])

            dve.memset(ones[:, :], 1.0)
            dve.memset(lanes[:, 0:1], 0.0)
            for t, value in ((mhalf, -0.5), (eps_ln, EPS_LN), (eps_rms, EPS_RMS), (per_dh, 1.0 / DH)):
                dve.memset(t[:, :], value)
            dve.memset(vf_s[:, :, :, :], 1.0).then_inc(made_const, 1)

            dve.wait_ge(in_x, 16)
            for t in range(TILES):
                dve.bn_stats(stat[:, t, :], xs[:, t * D:(t + 1) * D]).then_inc(ln_stat, 1)
            for t in range(TILES):
                dve.wait_ge(ln_stat, t + 1)
                dve.bn_aggr(mv[:, t, :], stat[:, t, :]).then_inc(ln_agg, 1)

            def set_lo_part(i):
                parts, n, scale, hi, lo = loads[i]
                dve.wait_ge(set_hi, i + 1)
                dve.scalar_tensor_tensor(lo, stage[i % STAGES][:, 0:n], scale, hi, ALU.mult, ALU.subtract)\
                   .then_inc(set_lo, 1)

            dve.wait_ge(ln_rstd, 1)
            for t in range(TILES):
                dve.tensor_scalar(xn[:, t * D:(t + 1) * D], xs[:, t * D:(t + 1) * D], mv[:, t, 0:1],
                                  rstd[:, t:t + 1], ALU.subtract, ALU.mult).then_inc(ln_out, 1)
            for k in range(4):
                c, half = k // 2, k % 2
                if k == 0:
                    set_lo_part(0)
                dve.wait_ge(ln_hi, k + 1)
                dve.tensor_tensor(xT_l[:, c, half * BANK:(half + 1) * BANK],
                                  PS[:, TB + k % 2 if k < 2 else OB + k % 2, :],
                                  xT_h[:, c, half * BANK:(half + 1) * BANK], ALU.subtract).then_inc(ln_lo, 1)
            for i in range(1, FIRST):
                set_lo_part(i)

            def to_bf16():
                dve.tensor_copy(identb[:, :], ident[:, :])
                dve.tensor_copy(mask[:, :, :], mask32[:, :, :]).then_inc(tab_made, 1)

            def l1_step(n, par, nrows):
                dve.wait_ge(l1_copy, n + 1)
                dve.tensor_scalar_min(ex_s[0:nrows, par, :], k_s[0:nrows, par, :], 0.0).then_inc(l1_min, 1)
                wait(dve, l1_sum, n - 1)
                dve.tensor_scalar(vf_s[0:nrows, par, :, 0:P],
                                  PS[0:nrows, SB + par, 256:512].rearrange("p (c n) -> p c n", c=DC),
                                  1 / WS, None, ALU.mult).then_inc(l1_v, 1)
                dve.wait_ge(l1_exp, n + 1)
                dve.scalar_tensor_tensor(kf_s[0:nrows, par, :], k_s[0:nrows, par, :], 0.0,
                                         ex_s[0:nrows, par, :], ALU.max, ALU.add).then_inc(l1_k, 1)

            def l1_end(b):
                if b == 0:
                    dve.wait_ge(in_const, 16 * 8)
                if b == B - 1:
                    to_bf16()
                dve.wait_ge(l1_sum, b * CT + CT)
                bank = (TB, OB)[b % 2]
                for c in range(DC):
                    dve.tensor_tensor(R1[:, b, c, 0:P], PS[:, bank + c, 0:P], blk[:, 0:P], ALU.mult)
                    last = dve.tensor_scalar(R1[:, b, c, P:136], blk[:, P:136], PS[:, bank + c, P:P + 1], None, ALU.mult)
                last.then_inc(l1_R, 1)

            l1_walk(dve, l1_step, set_lo_part, l1_end)

            dve.wait_ge(set_lo, NL)
            dve.wait_ge(l1_sum, B * CT)
            dve.wait_ge(tab_made, 9)
            dve.memset(kr[:, CT - 1, :], 0.0)
            dve.memset(ss[:, :, :], 1.0)
            for par in range(2):
                dve.memset(v_h[:, par, CT - 1, 0:DH], 1.0)
                dve.memset(v_h[:, par, :, DH:DH + 1], 1.0)
                dve.memset(v_l[:, par, CT - 1, :], 0.0)
                dve.memset(kT_h[:, par, SC:CT * P], 0.0)
                last = dve.memset(kT_l[:, par, SC:CT * P], 0.0)
            last.then_inc(made_const, 1)

            def piece_lo(p, g, par, bank=XB):
                if p in KV_PIECES:
                    t, n = piece_tile(p), piece_slots(p)
                    rows = CREM if PIECES[p] == "rem" else P
                    dve.wait_ge(vs_hi, v_done(p, g))
                    v = PS[0:rows, bank, 0:n * 2 * DH].rearrange("p (t d) -> p t d", d=2 * DH)[:, :, DH:]
                    dve.scalar_tensor_tensor(v_l[0:rows, par, t:t + n, :], v, 1 / WS, v_h[0:rows, par, t:t + n, 0:DH],
                                             ALU.mult, ALU.subtract).then_inc(vs_lo, 1)

            def kq_lo_part(s, g, par, bank=XB):
                dve.wait_ge(kq_hi, kq_done([s], g))
                hi, i, w = kq_view(s, kT_h, qT_h, par, bank)
                lo, _, _ = kq_view(s, kT_l, qT_l, par, bank)
                if w:
                    dve.scalar_tensor_tensor(lo, i, wcol[:, 0:1], hi, ALU.mult, ALU.subtract).then_inc(kq_lo, 1)
                else:
                    dve.tensor_tensor(lo, i, hi, ALU.subtract).then_inc(kq_lo, 1)

            def chunk_max(u, c, g):
                dve.wait_ge(qk_done, g * (UNITS * CHUNKS) + u * CHUNKS + c + 1)
                dve.reduce_max(mx[:, c:c + 1], PS[:, SB + c, 0:cols(u % LT, c)], AX_X).then_inc(mx_part, 1)

            def row_max(u, g):
                dve.wait_ge(mx_part, g * (UNITS * CHUNKS) + u * CHUNKS + CHUNKS)
                dve.reduce_max(mr[:, :], mx[:, :], AX_X).then_inc(mx_all, 1)
                dve.wait_ge(mx_all, g * UNITS + u + 1)
                dve.tensor_scalar(nb[:, u % 2:u % 2 + 1], mr[:, :], -SCALE, PSCALE_LN, ALU.mult, ALU.add)\
                   .then_inc(nb_done, 1)

            def p_lo(u, c, g):
                dve.wait_ge(pt_hi, g * (UNITS * CHUNKS) + u * CHUNKS + c + 1)
                w = cols(u % LT, c)
                dve.tensor_tensor(pT_l[:, c, 0:w], PS[:, TB + c % 2, 0:w], pT_h[:, c, 0:w], ALU.subtract)\
                   .then_inc(pt_lo, 1)

            def lane_step(g):
                dve.wait_ge(lane_in, g * 16 + 16)
                dve.tensor_reduce(lanes[:, 0:1], lanes[:, :], AX_X, ALU.add, apply_absolute_value=True)\
                   .then_inc(lane_sum, 1)

            def out_norm(u, g):
                h, lt = u // LT, u % LT
                if u == 0:
                    wait(dve, ot_tr, 2 * g)
                dve.wait_ge(pv_done, g * UNITS + u + 1)
                dve.reciprocal(rden[:, :], PS[:, OB, DH:DH + 1]).then_inc(rd_done, 1)
                dve.wait_ge(rd_done, g * UNITS + u + 1)
                dve.tensor_scalar(o_s[:, lt, h, :], PS[:, OB, 0:DH], rden[:, 0:1], None, ALU.mult)\
                   .then_inc(o_done, 1)

            def out_lo_part(i, g):
                if i < LT:
                    dve.wait_ge(ot_hi, g * 2 + i + 1)
                    dve.tensor_tensor(oT_l[:, i, :], PS[:, XB, :], oT_h[:, i, :], ALU.subtract).then_inc(ot_lo, 1)
                    return
                dve.wait_ge(oj_mm, g + 1)
                wait(dve, x1_done, g)
                at = xs[:, ds(g // KVH * BANK, BANK)]
                dve.scalar_tensor_tensor(at, PS[:, XB, :], 1 / WS, at, ALU.mult, ALU.add).then_inc(x1_done, 1)

            def mean(i):
                if i == 0:
                    dve.wait_ge(lane_tr, 1)
                    dve.reduce_sum(lsum[:, 3 * LANES:],
                                   PS[0:1, XB, 0:3 * LANES].rearrange("p (i j) -> p i j", j=LANES), AX_X)\
                       .then_inc(lane_tot, 1)
                    return
                dve.wait_ge(lane_b, 1)
                dve.tensor_scalar(wmean[:, 0:NTERN], PS[:, XB, 0:NTERN], 1.0 / (FF * D), EPS_Q, ALU.mult, ALU.max)\
                   .then_inc(mean_out, 1)
                dve.wait_ge(mean_out, 1)
                dve.tensor_scalar(thr[:, 0:NTERN], wmean[:, 0:NTERN], 0.5, None, ALU.mult)
                link(dve.tensor_scalar(thr[:, 4:4 + NTERN], wmean[:, 0:NTERN], -0.5, None, ALU.mult))

            def weight_lo_part(i):
                parts, n, scale, hi, lo = tloads[i]
                w, t = tst(i, n), (i - NSPLIT) // 2
                if t < 0:
                    return
                dve.wait_ge(tw_lo, i)
                dve.wait_ge(tw_in[i % STAGES], tload_count[i])
                link(dve.tensor_scalar(tern[:, :], w, thr[:, 4 + t:5 + t], None, ALU.is_lt))
                dve.scalar_tensor_tensor(hi, w, thr[:, t:t + 1], tern[:, :], ALU.is_gt, ALU.subtract)\
                   .then_inc(tw_lo, 1)
                dve.wait_ge(tw_lo, i + 1)

            kinds = {"out": out_lo_part, "piece": piece_lo, "kq": kq_lo_part,
                     "weight": weight_lo_part, "mean": mean}
            first_stats, norm_rows, lo_part, quantise, rest = tail_dve(dve, link)

            def group(g, par, first, last):
                for u in range(UNITS):
                    todo = list(jobs_of(u, first, last))

                    def job():
                        if todo:
                            run_job(g, par, todo.pop(0), kinds)

                    nu, ng = ((u + 1, g) if u + 1 < UNITS else (0, g + 1))
                    for c in range(CHUNKS):
                        p_lo(u, c, g)
                        if u + 1 < UNITS or not last:
                            chunk_max(nu, c, ng)
                        if c == 1:
                            job()
                    if u + 1 < UNITS or not last:
                        row_max(nu, ng)
                    if u == LANE_AT:
                        lane_step(g)
                    job()
                    if last and u == UNITS - 1:
                        lo_part(0, 0)
                    out_norm(u, g)
                    job()
                    if last and u == UNITS - 4:
                        dve.wait_ge(tw_const, 48)
                        dve.tensor_copy(ident16[:, :], ident[:, :])
                        dve.tensor_scalar(bgs[:, :], bgs[:, :], WS, None, ALU.mult).then_inc(tw_made, 1)
                    if last and u == UNITS - 3:
                        first_stats(0)
                    if last and u == UNITS - 2:
                        norm_rows(0, 0)

            def norm(p):
                n, v = piece_slots(p), piece_rows(p)
                dve.wait_ge(rs_made, p + 1)
                dve.tensor_tensor(v, v, rs[:, 0:n].unsqueeze(2).broadcast_to([P, n, DH]), ALU.mult).then_inc(pc_norm, 1)

            def rope(r):
                v, cs, sn = rope_operands(r)
                dve.wait_ge(pc_norm, {"k": 2, "q0": 1, "q1": 3}[r[:2]])
                wait(dve, rope_done, ROPES.index(r))
                dve.tensor_tensor(rot[:, 0, :, :], v, cs, ALU.mult)
                dve.tensor_tensor(rot[:, 1, :, 0:64], v[:, :, 64:DH], sn[:, :, 0:64], ALU.mult)
                link(dve.tensor_tensor(rot[:, 1, :, 64:DH], v[:, :, 0:64], sn[:, :, 64:DH], ALU.mult))
                dve.tensor_tensor(v, rot[:, 0, :, :], rot[:, 1, :, :], ALU.add).then_inc(rope_done, 1)

            todo = list(POOL_ORDER)
            for n, (kind, i) in enumerate(PREP_JOBS):
                kinds[kind](i, 0, 0, prep_bank(n))
                while kind == "piece" and todo and (isinstance(todo[0], str) or todo[0] < i):
                    e = todo.pop(0)
                    rope(e) if isinstance(e, str) else norm(e)
                if kind == "piece" and i == NP - 1:
                    norm(todo.pop(0))
            for c in range(CHUNKS):
                chunk_max(0, c, 0)
            row_max(0, 0)
            groups(dve, group)
            for kind, i in OUT_JOBS:
                if i == 2:
                    quantise(0)
                kinds[kind](i, NG - 1)
            for hf in range(2):
                rest(hf)

        @block.gpsimd
        def _(pool):
            pool.wait_ge(ln_agg, TILES)
            pool.wait_ge(made_const, 1)
            pool.tensor_tensor(rstd[:, :], mv[:, :, 1], eps_ln[:, :], ALU.add).then_inc(ln_var, 1)
            pool.wait_ge(ln_var, 1)
            pool.tensor_tensor(rstd[:, :], rstd[:, :], mhalf[:, 0:TILES], ALU.pow).then_inc(ln_rstd, 1)

            pool.wait_ge(in_const, 16 * 8)
            for k in range(2):
                for lt in range(LT):
                    pool.tensor_tensor(tab[:, 2 * k, lt, :], cos[:, lt, :], nwb[:, k, :], ALU.mult)
                    for a, o in ((0, 64), (64, 0)):
                        pool.tensor_tensor(tab[:, 2 * k + 1, lt, a:a + 64], sin[:, lt, a:a + 64],
                                           nwb[:, k, o:o + 64], ALU.mult).then_inc(tab_made, 1)

            PER_PIECE, PER_ROPE = 3, 3
            PER_G = NP * PER_PIECE + len(ROPES) * PER_ROPE

            def prepare(g, first=False):
                done = [0 if first else (g - 1) * PER_G + NP * (PER_PIECE - 1)]

                def step(ins):
                    done[0] = done[0] + 1
                    ins.then_inc(pool_step, 1)
                    pool.wait_ge(pool_step, done[0])

                for p in POOL_ORDER:
                    if first and isinstance(p, str):
                        continue
                    if not isinstance(p, str):
                        n = piece_slots(p)
                        v = piece_rows(p)
                        pool.wait_ge(pc_copy, pieces_done(p, g))
                        wait(pool, pc_norm, g * NP + p)
                        step(pool.tensor_tensor(rs[:, 0:n], ss[:, p % 2, 0:n], per_dh[:, 0:n], ALU.mult))
                        step(pool.tensor_tensor(rs[:, 0:n], rs[:, 0:n], eps_rms[:, 0:n], ALU.add))
                        last = pool.tensor_tensor(rs[:, 0:n], rs[:, 0:n], mhalf[:, 0:n], ALU.pow)
                        if first:
                            last.then_inc(rs_made, 1)
                            continue
                        step(last)
                        pool.tensor_tensor(v, v, rs[:, 0:n].unsqueeze(2).broadcast_to([P, n, DH]), ALU.mult)\
                            .then_inc(pc_norm, 1)
                    else:
                        r = ROPES.index(p)
                        pool.wait_ge(pc_norm, g * NP + {"k": 2, "q0": 1, "q1": 3}[p[:2]])
                        wait(pool, rope_done, g * len(ROPES) + r)
                        v, cs, sn = rope_operands(p)
                        step(pool.tensor_tensor(rot[:, 0, :, :], v, cs, ALU.mult))
                        pool.tensor_tensor(rot[:, 1, :, 0:64], v[:, :, 64:DH], sn[:, :, 0:64], ALU.mult)\
                            .then_inc(pool_step, 1)
                        done[0] = done[0] + 1
                        step(pool.tensor_tensor(rot[:, 1, :, 64:DH], v[:, :, 0:64], sn[:, :, 64:DH], ALU.mult))
                        pool.tensor_tensor(v, rot[:, 0, :, :], rot[:, 1, :, :], ALU.add).then_inc(rope_done, 1)

            pool.wait_ge(made_const, 2)
            prepare(0, True)
            with pool.Fori(1, NG) as g:
                prepare(g)
            for i, (parts, n, scale, hi, lo) in enumerate(tloads[:NSPLIT]):
                pool.wait_ge(tw_hi, 2 * i + 2)
                pool.tensor_tensor(lo, tst(i, n), hi, ALU.subtract).then_inc(tw_lo, 1)
            tail_pool(pool)


def _hadamard(n):
    i = np.arange(n)
    bits = i[:, None] & i[None, :]
    parity = np.zeros((n, n), np.int64)
    for k in range(n.bit_length()):
        parity ^= (bits >> k) & 1
    return (1.0 - 2.0 * parity) / np.sqrt(n)


def _constants():
    ident = np.eye(P, dtype=np.float32)
    mask = np.zeros((P, LT, width(1)), np.float32)
    for lt in range(LT):
        mask[:, lt, SC - LAST:CT * P - LAST] = -1e30
        first = (CT + lt) * P - LAST
        mask[:, lt, first:first + P] = np.where(np.arange(P)[None, :] > np.arange(P)[:, None], -1e30, 0)
    inv = np.float32(1.0) / np.float32(10000.0) ** (np.arange(0, DH, 2, dtype=np.float32) / np.float32(DH))
    angle = np.outer(np.arange(L, dtype=np.float32), inv).astype(np.float32)
    cos = np.concatenate([np.cos(angle)] * 2, -1).astype(np.float32)
    sin = np.concatenate([-np.sin(angle), np.sin(angle)], -1).astype(np.float32)
    tiles = lambda a, n: np.ascontiguousarray(a.reshape(n, P, -1).transpose(1, 0, 2))
    blk = np.zeros((P, 136), np.float32)
    blk[:, 0:P] = np.arange(P)[:, None] // 16 == np.arange(P)[None, :] // 16
    blk[:, P:] = np.arange(P)[:, None] // 16 == np.arange(8)[None, :]
    lower = np.broadcast_to(np.tile((np.arange(NE)[None, :] < np.arange(NE)[:, None]).astype(np.float32), (4, 1)),
                            (P, 4 * NE, NE))
    return dict(c_ident=ident, c_mask=mask,
                c_cos=tiles(cos, LT), c_sin=tiles(sin, LT), c_h256=tiles(_hadamard(D), DC).astype(np.float16),
                c_blk=blk,
                c_lower=np.ascontiguousarray(lower))


def kernel(**inputs):
    import numpy as _np
    import concourse.bacc as _bacc
    from concourse import mybir as _mybir
    from concourse.bass_utils import run_bass_kernel_spmd as _run

    a = {n: _np.asarray(v) for n, v in inputs.items()}
    gu = a["L1_ffn_expert_gate_up"]
    laid = dict(
        x=a["x"].reshape(B * L, D), ctxT=a["ctx_2048"].transpose(0, 2, 1),
        wq=a["L0_xattn_wq"], wk=a["L0_xattn_wk"], wv=a["L0_xattn_wv"], wo=a["L0_xattn_wo"],
        wk_ctx=a["L0_xattn_wk_ctx"], wv_ctx=a["L0_xattn_wv_ctx"],
        q_norm=a["L0_xattn_q_norm_w"], k_norm=a["L0_xattn_k_norm_w"],
        w_gateT=a["L0_ffn_w_gate"].T, w_upT=a["L0_ffn_w_up"].T, w_downT=a["L0_ffn_w_down"].T,
        WqT=a["L1_xattn_Wq"].T, WgT=a["L1_xattn_Wg"].T, bg=a["L1_xattn_bg"], WkvT=a["L1_xattn_Wkv"].T,
        WoT=a["L1_xattn_Wo"].T, routerT=a["L1_ffn_router_gate"].T,
        w_lanes=_np.concatenate([a[n].reshape(-1, LANES).T for n in
                        ("L0_ffn_w_gate", "L0_ffn_w_up", "L0_ffn_w_down")]),
        e_gate=gu[:, :, 0::2].transpose(1, 0, 2).reshape(D, NE * FI),
        e_up=gu[:, :, 1::2].transpose(1, 0, 2).reshape(D, NE * FI), e_down=a["L1_ffn_expert_down"], **_constants())
    nc = _bacc.Bacc("TRN2", target_bir_lowering=False, num_devices=1)
    arrays, args = {}, {}
    for name, v in laid.items():
        v = _np.ascontiguousarray(v)
        arrays[f"in_{name}"] = v
        args[name] = nc.dram_tensor(f"in_{name}", v.shape, _mybir.dt.from_np(v.dtype), kind="ExternalInput").ap()
    out = nc.dram_tensor("out_x", (B * L, D), _mybir.dt.float32, kind="ExternalOutput").ap()
    build(nc, *args.values(), out)
    r = _run(nc, [arrays], core_ids=[0])
    return r.results[0]["out_x"].reshape(B, L, D)
```
